# Optimizing a Trainium2 kernel written in Bass

```python
import numpy as np
import jax
import jax.numpy as jnp

def _softmax(x, axis=-1):
    return jax.nn.softmax(x, axis=axis)

def _gelu(x):
    return jax.nn.gelu(x, approximate=True)

def _silu(x):
    return jax.nn.silu(x)

def _sigmoid(x):
    return jax.nn.sigmoid(x)

def _layernorm(x, axis=-1, eps=1e-05):
    m = jnp.mean(x, axis=axis, keepdims=True)
    v = jnp.var(x, axis=axis, keepdims=True)
    return (x - m) / jnp.sqrt(v + eps)

def _scatter_add(tgt, idx, src, axis=0):
    return tgt.at[idx].add(src)

def _segment_sum(src, seg, n):
    return jax.ops.segment_sum(src, seg, n)
kernel_name = 'mk_gnn_ffn_d4_gnn_r32_df38ae'

def setup_inputs(seed: int=0):
    np.random.seed(seed)
    _w = jnp.asarray

    def _rec_inputs():
        import jax
        import jax.numpy as jnp
        _gk = jax.random.key(seed)
        x = -0.0002117 + 1 * jax.random.normal(jax.random.fold_in(_gk, 1), (3125, 256), jnp.float32)
        _s = jax.random.randint(jax.random.fold_in(_gk, 2), (25000,), 0, 3125, jnp.int32)
        _d = jax.random.randint(jax.random.fold_in(_gk, 3), (25000,), 0, 3125, jnp.int32)
        _loop = jnp.arange(3125, dtype=jnp.int32)
        src = jnp.concatenate([_s, _d, _loop])
        dst = jnp.concatenate([_d, _s, _loop])
        _o = jnp.argsort(dst, stable=True)
        src = src[_o]
        dst = dst[_o]
        edge_weight = jax.random.uniform(jax.random.fold_in(_gk, 14), (53125,), jnp.float32, 0.0, 0.999999)
        return (x, src, dst, edge_weight)
    x, src, dst, edge_weight = _rec_inputs()

    def _L0_gnn_setup():
        import jax, jax.numpy as jnp
        import numpy as np
        N_NODES = 3125
        N_EDGES = 50000
        D_IN = 256
        D_OUT = 256
        key = jax.random.key(seed)
        k1, k2, k3, k4, k5 = jax.random.split(key, 5)
        feat = jax.random.normal(k1, (N_NODES, D_IN), dtype=jnp.float32)
        lim = float(np.sqrt(6.0 / (D_IN + D_OUT)))
        W_neigh = jax.random.uniform(k2, (D_OUT, D_IN), minval=-lim, maxval=lim, dtype=jnp.float32)
        W_self = jax.random.uniform(k3, (D_OUT, D_IN), minval=-lim, maxval=lim, dtype=jnp.float32)
        b_self = jnp.zeros((D_OUT,), dtype=jnp.float32)
        src = jax.random.randint(k4, (N_EDGES,), 0, N_NODES, dtype=jnp.int32)
        dst = jax.random.randint(k5, (N_EDGES,), 0, N_NODES, dtype=jnp.int32)
        return {'feat': feat, 'W_neigh': W_neigh, 'W_self': W_self, 'b_self': b_self, 'src': src, 'dst': dst}
    _L0_gnn_all = _L0_gnn_setup()
    _L0_gnn_in = {k: v for k, v in _L0_gnn_all.items() if k in ('W_neigh', 'W_self', 'b_self')}
    del _L0_gnn_all

    def _L0_ffn_setup():
        import math
        import jax, jax.numpy as jnp
        import numpy as np
        CAPACITY_FACTOR = 1.25
        key = jax.random.key(seed)
        ks = jax.random.split(key, 5)
        B, L, D, F, E = (8, 256, 256, 1024, 8)
        h = jax.random.normal(ks[0], (B, L, D), dtype=jnp.float32)
        gate_w = jax.random.normal(ks[1], (D, E), dtype=jnp.float32) * 0.02
        gate_b = jnp.zeros((E,), dtype=jnp.float32)
        w1 = jax.random.normal(ks[2], (E, D, F), dtype=jnp.float32) * (1.0 / math.sqrt(D))
        b1 = jnp.zeros((E, F), dtype=jnp.float32)
        w2 = jax.random.normal(ks[3], (E, F, D), dtype=jnp.float32) * (1.0 / math.sqrt(F))
        b2 = jnp.zeros((E, D), dtype=jnp.float32)
        return {'h': h, 'gate_w': gate_w, 'gate_b': gate_b, 'w1': w1, 'b1': b1, 'w2': w2, 'b2': b2}
    _L0_ffn_all = _L0_ffn_setup()
    _L0_ffn_in = {k: v for k, v in _L0_ffn_all.items() if k in ('gate_w', 'gate_b', 'w1', 'b1', 'w2', 'b2')}
    del _L0_ffn_all

    def _L1_gnn_setup():
        import jax, jax.numpy as jnp
        import numpy as np
        N, E = (50000, 25000)
        IN_DIM = 256
        OUT_DIM = 256
        H = 8
        D = OUT_DIM // H
        SCALE = D ** (-0.5)
        LN_EPS = 1e-05

        def _layernorm(x, g, b):
            mu = jnp.mean(x, axis=-1, keepdims=True)
            var = jnp.mean((x - mu) ** 2, axis=-1, keepdims=True)
            return (x - mu) * jax.lax.rsqrt(var + LN_EPS) * g + b
        key = jax.random.key(seed)
        ks = jax.random.split(key, 12)
        s = 1.0 / np.sqrt(IN_DIM)
        inp = {'x': jax.random.normal(ks[0], (N, IN_DIM), jnp.float32), 'edge_index': jax.random.randint(ks[1], (2, E), 0, N, jnp.int64), 'batch': jnp.zeros((N,), jnp.int64), 'Wq': jax.random.uniform(ks[2], (IN_DIM, OUT_DIM), jnp.float32, -s, s), 'Wk': jax.random.uniform(ks[3], (IN_DIM, OUT_DIM), jnp.float32, -s, s), 'Wv': jax.random.uniform(ks[4], (IN_DIM, OUT_DIM), jnp.float32, -s, s), 'Wo_w': jax.random.uniform(ks[5], (OUT_DIM, OUT_DIM), jnp.float32, -s, s), 'Wo_b': jnp.zeros((OUT_DIM,), jnp.float32), 'ln1_g': jnp.ones((OUT_DIM,), jnp.float32), 'ln1_b': jnp.zeros((OUT_DIM,), jnp.float32), 'ln2_g': jnp.ones((OUT_DIM,), jnp.float32), 'ln2_b': jnp.zeros((OUT_DIM,), jnp.float32), 'ffn_w1': jax.random.uniform(ks[6], (OUT_DIM, 2 * OUT_DIM), jnp.float32, -s, s), 'ffn_b1': jnp.zeros((2 * OUT_DIM,), jnp.float32), 'ffn_w2': jax.random.uniform(ks[7], (2 * OUT_DIM, OUT_DIM), jnp.float32, -s, s), 'ffn_b2': jnp.zeros((OUT_DIM,), jnp.float32)}
        return inp
    _L1_gnn_all = _L1_gnn_setup()
    _L1_gnn_in = {k: v for k, v in _L1_gnn_all.items() if k in ('Wq', 'Wk', 'Wv', 'Wo_w', 'Wo_b', 'ln1_g', 'ln1_b', 'ln2_g', 'ln2_b', 'ffn_w1', 'ffn_b1', 'ffn_w2', 'ffn_b2')}
    del _L1_gnn_all

    def _L1_ffn_setup():
        import jax, jax.numpy as jnp
        import numpy as np
        B, S, D, H, E, K = (8, 256, 256, 1024, 8, 2)
        key = jax.random.key(seed)
        ks = jax.random.split(key, 7)
        s_in = 1.0 / np.sqrt(D)
        s_hid = 1.0 / np.sqrt(H)
        return {'x': jax.random.normal(ks[0], (B, S, D), dtype=jnp.float32), 'Wg': jax.random.uniform(ks[1], (E, D), jnp.float32, -s_in, s_in), 'bg': jax.random.uniform(ks[2], (E,), jnp.float32, -s_in, s_in), 'W1': jax.random.uniform(ks[3], (E, H, D), jnp.float32, -s_in, s_in), 'b1': jax.random.uniform(ks[4], (E, H), jnp.float32, -s_in, s_in), 'W2': jax.random.uniform(ks[5], (E, D, H), jnp.float32, -s_hid, s_hid), 'b2': jax.random.uniform(ks[6], (E, D), jnp.float32, -s_hid, s_hid)}
    _L1_ffn_all = _L1_ffn_setup()
    _L1_ffn_in = {k: v for k, v in _L1_ffn_all.items() if k in ('Wg', 'bg', 'W1', 'b1', 'W2', 'b2')}
    del _L1_ffn_all

    def _L2_gnn_setup():
        import jax, jax.numpy as jnp
        import numpy as np
        N_NODES = 3125
        N_EDGES = 50000
        D = 256
        key = jax.random.key(seed)
        ks = jax.random.split(key, 8)
        h6_all = jax.random.normal(ks[0], (N_NODES, D), dtype=jnp.float32)
        edge_index = jax.random.randint(ks[1], (2, N_EDGES), 0, N_NODES, dtype=jnp.int64)
        edge_weight = jax.random.uniform(ks[2], (N_EDGES,), dtype=jnp.float32)
        s = 1.0 / np.sqrt(D)
        W = jax.random.normal(ks[3], (D, D), dtype=jnp.float32) * s
        b = jnp.zeros((D,), dtype=jnp.float32)
        W1 = jax.random.normal(ks[4], (D, D), dtype=jnp.float32) * s
        b1 = jnp.zeros((D,), dtype=jnp.float32)
        W2 = jax.random.normal(ks[5], (D, D), dtype=jnp.float32) * s
        b2 = jnp.zeros((D,), dtype=jnp.float32)
        return {'h6_all': h6_all, 'edge_index': edge_index, 'edge_weight': edge_weight, 'W': W, 'b': b, 'W1': W1, 'b1': b1, 'W2': W2, 'b2': b2}
    _L2_gnn_all = _L2_gnn_setup()
    _L2_gnn_in = {k: v for k, v in _L2_gnn_all.items() if k in ('W', 'b', 'W1', 'b1', 'W2', 'b2')}
    del _L2_gnn_all

    def _L2_ffn_setup():
        import math
        import jax, jax.numpy as jnp
        import numpy as np
        CAPACITY_FACTOR = 1.25
        TOP_K = 2
        LN_EPS = 1e-05

        def _layer_norm(x, gamma, beta):
            mu = jnp.mean(x, axis=-1, keepdims=True)
            var = jnp.var(x, axis=-1, keepdims=True)
            return (x - mu) * jax.lax.rsqrt(var + LN_EPS) * gamma + beta
        key = jax.random.key(seed)
        ks = jax.random.split(key, 4)
        B, S, D, F, E = (8, 128, 256, 512, 8)
        x = jax.random.normal(ks[0], (B, S, D), dtype=jnp.float32)
        Wr = jax.random.normal(ks[1], (D, E), dtype=jnp.float32) / np.sqrt(D)
        br = jnp.zeros((E,), jnp.float32)
        W1 = jax.random.normal(ks[2], (E, D, F), dtype=jnp.float32) / np.sqrt(D)
        b1 = jnp.zeros((E, F), jnp.float32)
        W2 = jax.random.normal(ks[3], (E, F, D), dtype=jnp.float32) / np.sqrt(F)
        b2 = jnp.zeros((E, D), jnp.float32)
        gamma = jnp.ones((D,), jnp.float32)
        beta = jnp.zeros((D,), jnp.float32)
        return {'x': x, 'Wr': Wr, 'br': br, 'W1': W1, 'b1': b1, 'W2': W2, 'b2': b2, 'gamma': gamma, 'beta': beta}
    _L2_ffn_all = _L2_ffn_setup()
    _L2_ffn_in = {k: v for k, v in _L2_ffn_all.items() if k in ('Wr', 'br', 'W1', 'b1', 'W2', 'b2', 'gamma', 'beta')}
    del _L2_ffn_all

    def _L3_gnn_setup():
        import jax, jax.numpy as jnp
        import numpy as np
        N_NODES = 3125
        BN_EPS = 1e-05

        def gcn_conv(x, src, dst, W, b, n):
            h = x @ W
            loop = jnp.arange(n, dtype=src.dtype)
            s = jnp.concatenate([src, loop])
            d = jnp.concatenate([dst, loop])
            deg = jax.ops.segment_sum(jnp.ones(s.shape, h.dtype), d, num_segments=n)
            dinv = jnp.where(deg > 0, jax.lax.rsqrt(jnp.maximum(deg, 1.0)), 0.0)
            norm = dinv[s] * dinv[d]
            msg = h[s] * norm[:, None]
            out = jax.ops.segment_sum(msg, d, num_segments=n)
            return out + b

        def batch_norm(x, gamma, beta):
            mean = jnp.mean(x, axis=0)
            var = jnp.mean(jnp.square(x - mean), axis=0)
            return (x - mean) * jax.lax.rsqrt(var + BN_EPS) * gamma + beta
        key = jax.random.key(seed)
        ks = jax.random.split(key, 10)
        d0, d1, d2 = (256, 128, 64)
        d_cat = d0 + d1 + d2
        inp = {'node_features': jax.random.normal(ks[0], (N_NODES, d0), jnp.float32), 'edge_idx': jax.random.randint(ks[1], (2, 50000), 0, N_NODES, jnp.int64), 'W1': jax.random.normal(ks[2], (d0, d1), jnp.float32) * (1.0 / np.sqrt(d0)), 'b1': jnp.zeros((d1,), jnp.float32), 'g1': jnp.ones((d1,), jnp.float32), 'be1': jnp.zeros((d1,), jnp.float32), 'W2': jax.random.normal(ks[3], (d1, d2), jnp.float32) * (1.0 / np.sqrt(d1)), 'b2': jnp.zeros((d2,), jnp.float32), 'g2': jnp.ones((d2,), jnp.float32), 'be2': jnp.zeros((d2,), jnp.float32), 'Wfc': jax.random.normal(ks[4], (d_cat, d0), jnp.float32) * (1.0 / np.sqrt(d_cat)), 'bfc': jnp.zeros((d0,), jnp.float32)}
        return inp
    _L3_gnn_all = _L3_gnn_setup()
    _L3_gnn_in = {k: v for k, v in _L3_gnn_all.items() if k in ('W1', 'b1', 'g1', 'be1', 'W2', 'b2', 'g2', 'be2', 'Wfc', 'bfc')}
    del _L3_gnn_all

    def _L3_ffn_setup():
        import jax, jax.numpy as jnp
        import numpy as np
        B, N, D = (16, 128, 256)
        NUM_EXPERTS, TOP_K, HEADS = (4, 2, 4)
        N_EDGES = 32768
        LN_EPS = 1e-05

        def _layernorm(x, g, b):
            mu = x.mean(-1, keepdims=True)
            var = ((x - mu) ** 2).mean(-1, keepdims=True)
            return (x - mu) * jax.lax.rsqrt(var + LN_EPS) * g + b

        def _forward(x, edge_index, W_gat, att_src, att_dst, b_gat, ln_gamma, ln_beta, W1, b1, W2, b2):
            Bc, Nc, Dc = x.shape
            M = Bc * Nc
            x_flat = x.reshape(M, Dc)
            h = (x_flat @ W_gat).reshape(M, HEADS, NUM_EXPERTS)
            loops = jnp.arange(M, dtype=edge_index.dtype)
            src = jnp.concatenate([edge_index[0], loops])
            dst = jnp.concatenate([edge_index[1], loops])
            a_src = (h * att_src).sum(-1)
            a_dst = (h * att_dst).sum(-1)
            e = jax.nn.leaky_relu(a_src[src] + a_dst[dst], negative_slope=0.2)
            e_max = jax.ops.segment_max(e, dst, num_segments=M)
            ee = jnp.exp(e - e_max[dst])
            denom = jax.ops.segment_sum(ee, dst, num_segments=M)
            alpha = ee / (denom[dst] + 1e-16)
            msg = h[src] * alpha[:, :, None]
            agg = jax.ops.segment_sum(msg, dst, num_segments=M).reshape(M, HEADS * NUM_EXPERTS) + b_gat
            scores = _layernorm(agg, ln_gamma, ln_beta).reshape(M, HEADS, NUM_EXPERTS).mean(1)
            scores = scores.reshape(Bc, Nc, NUM_EXPERTS)
            topk_s, topk_i = jax.lax.top_k(scores, TOP_K)
            w = jax.nn.softmax(topk_s, axis=-1)
            out = jnp.zeros_like(x)
            for ei in range(NUM_EXPERTS):
                g = jnp.where(topk_i == ei, w, 0.0).sum(-1)
                hh = jax.nn.gelu(x @ W1[ei] + b1[ei], approximate=False)
                out = out + g[..., None] * (hh @ W2[ei] + b2[ei])
            return out
        key = jax.random.key(seed)
        ks = jax.random.split(key, 8)
        s = 0.05
        return {'x': jax.random.normal(ks[0], (B, N, D), jnp.float32), 'W_gat': jax.random.normal(ks[1], (D, HEADS * NUM_EXPERTS), jnp.float32) * s, 'att_src': jax.random.normal(ks[2], (HEADS, NUM_EXPERTS), jnp.float32) * s, 'att_dst': jax.random.normal(ks[3], (HEADS, NUM_EXPERTS), jnp.float32) * s, 'b_gat': jnp.zeros((HEADS * NUM_EXPERTS,), jnp.float32), 'ln_gamma': jnp.ones((HEADS * NUM_EXPERTS,), jnp.float32), 'ln_beta': jnp.zeros((HEADS * NUM_EXPERTS,), jnp.float32), 'W1': jax.random.normal(ks[4], (NUM_EXPERTS, D, 2 * D), jnp.float32) * s, 'b1': jnp.zeros((NUM_EXPERTS, 2 * D), jnp.float32), 'W2': jax.random.normal(ks[5], (NUM_EXPERTS, 2 * D, D), jnp.float32) * s, 'b2': jnp.zeros((NUM_EXPERTS, D), jnp.float32), 'edge_index': jax.random.randint(ks[6], (2, N_EDGES), 0, B * N, jnp.int32)}
    _L3_ffn_all = _L3_ffn_setup()
    _L3_ffn_in = {k: v for k, v in _L3_ffn_all.items() if k in ('W_gat', 'att_src', 'att_dst', 'b_gat', 'ln_gamma', 'ln_beta', 'W1', 'b1', 'W2', 'b2', 'edge_index')}
    del _L3_ffn_all
    return {'x': x, 'src': src, 'dst': dst, 'edge_weight': edge_weight, 'L0_gnn_W_neigh': _L0_gnn_in['W_neigh'], 'L0_gnn_W_self': _L0_gnn_in['W_self'], 'L0_gnn_b_self': _L0_gnn_in['b_self'], 'L0_ffn_gate_w': _L0_ffn_in['gate_w'], 'L0_ffn_gate_b': _L0_ffn_in['gate_b'], 'L0_ffn_w1': _L0_ffn_in['w1'], 'L0_ffn_b1': _L0_ffn_in['b1'], 'L0_ffn_w2': _L0_ffn_in['w2'], 'L0_ffn_b2': _L0_ffn_in['b2'], 'L1_gnn_Wq': _L1_gnn_in['Wq'], 'L1_gnn_Wk': _L1_gnn_in['Wk'], 'L1_gnn_Wv': _L1_gnn_in['Wv'], 'L1_gnn_Wo_w': _L1_gnn_in['Wo_w'], 'L1_gnn_Wo_b': _L1_gnn_in['Wo_b'], 'L1_gnn_ln1_g': _L1_gnn_in['ln1_g'], 'L1_gnn_ln1_b': _L1_gnn_in['ln1_b'], 'L1_gnn_ln2_g': _L1_gnn_in['ln2_g'], 'L1_gnn_ln2_b': _L1_gnn_in['ln2_b'], 'L1_gnn_ffn_w1': _L1_gnn_in['ffn_w1'], 'L1_gnn_ffn_b1': _L1_gnn_in['ffn_b1'], 'L1_gnn_ffn_w2': _L1_gnn_in['ffn_w2'], 'L1_gnn_ffn_b2': _L1_gnn_in['ffn_b2'], 'L1_ffn_Wg': _L1_ffn_in['Wg'], 'L1_ffn_bg': _L1_ffn_in['bg'], 'L1_ffn_W1': _L1_ffn_in['W1'], 'L1_ffn_b1': _L1_ffn_in['b1'], 'L1_ffn_W2': _L1_ffn_in['W2'], 'L1_ffn_b2': _L1_ffn_in['b2'], 'L2_gnn_W': _L2_gnn_in['W'], 'L2_gnn_b': _L2_gnn_in['b'], 'L2_gnn_W1': _L2_gnn_in['W1'], 'L2_gnn_b1': _L2_gnn_in['b1'], 'L2_gnn_W2': _L2_gnn_in['W2'], 'L2_gnn_b2': _L2_gnn_in['b2'], 'L2_ffn_Wr': _L2_ffn_in['Wr'], 'L2_ffn_br': _L2_ffn_in['br'], 'L2_ffn_W1': _L2_ffn_in['W1'], 'L2_ffn_b1': _L2_ffn_in['b1'], 'L2_ffn_W2': _L2_ffn_in['W2'], 'L2_ffn_b2': _L2_ffn_in['b2'], 'L2_ffn_gamma': _L2_ffn_in['gamma'], 'L2_ffn_beta': _L2_ffn_in['beta'], 'L3_gnn_W1': _L3_gnn_in['W1'], 'L3_gnn_b1': _L3_gnn_in['b1'], 'L3_gnn_g1': _L3_gnn_in['g1'], 'L3_gnn_be1': _L3_gnn_in['be1'], 'L3_gnn_W2': _L3_gnn_in['W2'], 'L3_gnn_b2': _L3_gnn_in['b2'], 'L3_gnn_g2': _L3_gnn_in['g2'], 'L3_gnn_be2': _L3_gnn_in['be2'], 'L3_gnn_Wfc': _L3_gnn_in['Wfc'], 'L3_gnn_bfc': _L3_gnn_in['bfc'], 'L3_ffn_W_gat': _L3_ffn_in['W_gat'], 'L3_ffn_att_src': _L3_ffn_in['att_src'], 'L3_ffn_att_dst': _L3_ffn_in['att_dst'], 'L3_ffn_b_gat': _L3_ffn_in['b_gat'], 'L3_ffn_ln_gamma': _L3_ffn_in['ln_gamma'], 'L3_ffn_ln_beta': _L3_ffn_in['ln_beta'], 'L3_ffn_W1': _L3_ffn_in['W1'], 'L3_ffn_b1': _L3_ffn_in['b1'], 'L3_ffn_W2': _L3_ffn_in['W2'], 'L3_ffn_b2': _L3_ffn_in['b2'], 'L3_ffn_edge_index': _L3_ffn_in['edge_index']}

def reference(x, src, dst, edge_weight, L0_gnn_W_neigh, L0_gnn_W_self, L0_gnn_b_self, L0_ffn_gate_w, L0_ffn_gate_b, L0_ffn_w1, L0_ffn_b1, L0_ffn_w2, L0_ffn_b2, L1_gnn_Wq, L1_gnn_Wk, L1_gnn_Wv, L1_gnn_Wo_w, L1_gnn_Wo_b, L1_gnn_ln1_g, L1_gnn_ln1_b, L1_gnn_ln2_g, L1_gnn_ln2_b, L1_gnn_ffn_w1, L1_gnn_ffn_b1, L1_gnn_ffn_w2, L1_gnn_ffn_b2, L1_ffn_Wg, L1_ffn_bg, L1_ffn_W1, L1_ffn_b1, L1_ffn_W2, L1_ffn_b2, L2_gnn_W, L2_gnn_b, L2_gnn_W1, L2_gnn_b1, L2_gnn_W2, L2_gnn_b2, L2_ffn_Wr, L2_ffn_br, L2_ffn_W1, L2_ffn_b1, L2_ffn_W2, L2_ffn_b2, L2_ffn_gamma, L2_ffn_beta, L3_gnn_W1, L3_gnn_b1, L3_gnn_g1, L3_gnn_be1, L3_gnn_W2, L3_gnn_b2, L3_gnn_g2, L3_gnn_be2, L3_gnn_Wfc, L3_gnn_bfc, L3_ffn_W_gat, L3_ffn_att_src, L3_ffn_att_dst, L3_ffn_b_gat, L3_ffn_ln_gamma, L3_ffn_ln_beta, L3_ffn_W1, L3_ffn_b1, L3_ffn_W2, L3_ffn_b2, L3_ffn_edge_index):
    import jax
    import jax.numpy as jnp

    def _L0_gnn_ref(feat, W_neigh, W_self, b_self, src, dst):
        import jax, jax.numpy as jnp
        import numpy as np
        N_NODES = 3125
        N_EDGES = 50000
        D_IN = 256
        D_OUT = 256
        msgs = feat[src]
        neigh_sum = jax.ops.segment_sum(msgs, dst, num_segments=N_NODES)
        deg = jax.ops.segment_sum(jnp.ones((src.shape[0],), dtype=feat.dtype), dst, num_segments=N_NODES)
        h_neigh = neigh_sum / jnp.maximum(deg, 1.0)[:, None]
        h_neigh = h_neigh @ W_neigh.T
        h_self = feat @ W_self.T + b_self
        return h_self + h_neigh

    def _L0_ffn_ref(h, gate_w, gate_b, w1, b1, w2, b2):
        import math
        import jax, jax.numpy as jnp
        import numpy as np
        CAPACITY_FACTOR = 1.25
        B, L, D = h.shape
        E = gate_w.shape[1]
        T = B * L
        C = max(1, math.ceil(CAPACITY_FACTOR * T / E))
        x = h.reshape(T, D)
        logits = x @ gate_w + gate_b
        probs = jax.nn.softmax(logits, axis=-1)
        idx = jnp.argmax(probs, axis=-1)
        prb = jnp.take_along_axis(probs, idx[:, None], axis=1)[:, 0]
        one_hot = jax.nn.one_hot(idx, E, dtype=jnp.float32)
        pos = (jnp.cumsum(one_hot, axis=0) * one_hot).sum(-1).astype(jnp.int32) - 1
        kept = pos < C
        pos_safe = jnp.where(kept, pos, C)
        buf = jnp.zeros((E, C, D), dtype=h.dtype).at[idx, pos_safe].set(x, mode='drop')
        hmid = jax.nn.relu(jnp.einsum('ecd,edf->ecf', buf, w1) + b1[:, None, :])
        ybuf = jnp.einsum('ecf,efd->ecd', hmid, w2) + b2[:, None, :]
        pos_g = jnp.minimum(pos, C - 1)
        y_tok = ybuf[idx, pos_g] * (prb * kept)[:, None]
        y = y_tok.reshape(B, L, D)
        y = jnp.nan_to_num(y, nan=0.0, posinf=10000.0, neginf=-10000.0)
        return y

    def _L1_gnn_ref(x, edge_index, batch, Wq, Wk, Wv, Wo_w, Wo_b, ln1_g, ln1_b, ln2_g, ln2_b, ffn_w1, ffn_b1, ffn_w2, ffn_b2):
        import jax, jax.numpy as jnp
        import numpy as np
        N, E = (50000, 25000)
        IN_DIM = 256
        OUT_DIM = 256
        H = 8
        D = OUT_DIM // H
        SCALE = D ** (-0.5)
        LN_EPS = 1e-05

        def _layernorm(x, g, b):
            mu = jnp.mean(x, axis=-1, keepdims=True)
            var = jnp.mean((x - mu) ** 2, axis=-1, keepdims=True)
            return (x - mu) * jax.lax.rsqrt(var + LN_EPS) * g + b
        n = x.shape[0]
        residual = x
        Q = (x @ Wq).reshape(n, H, D)
        K = (x @ Wk).reshape(n, H, D)
        V = (x @ Wv).reshape(n, H, D)
        src, dst = (edge_index[0], edge_index[1])
        scores = jnp.einsum('ehd,ehd->eh', Q[dst], K[src]) * SCALE
        attn_max = jnp.zeros((n, H), scores.dtype).at[dst].max(scores)
        w = jnp.exp(scores - attn_max[dst])
        attn_sum = jnp.zeros((n, H), w.dtype).at[dst].add(w)
        w = w / (attn_sum[dst] + 1e-08)
        msg = V[src] * w[:, :, None]
        out = jnp.zeros((n, H, D), msg.dtype).at[dst].add(msg)
        out = out.reshape(n, OUT_DIM) @ Wo_w + Wo_b
        out = _layernorm(residual + out, ln1_g, ln1_b)
        ffn = jax.nn.gelu(out @ ffn_w1 + ffn_b1, approximate=False) @ ffn_w2 + ffn_b2
        out = _layernorm(out + ffn, ln2_g, ln2_b)
        return out

    def _L1_ffn_ref(x, Wg, bg, W1, b1, W2, b2):
        import jax, jax.numpy as jnp
        import numpy as np
        B, S, D, H, E, K = (8, 256, 256, 1024, 8, 2)
        gate_scores = jnp.einsum('bsd,ed->bse', x, Wg) + bg
        topk_scores, topk_idx = jax.lax.top_k(gate_scores, K)
        topk_probs = jax.nn.softmax(topk_scores, axis=-1)
        combine = jnp.sum(topk_probs[..., None] * jax.nn.one_hot(topk_idx, E, dtype=x.dtype), axis=-2)
        out = jnp.zeros_like(x)
        for e in range(E):
            h = jax.nn.relu(jnp.einsum('bsd,hd->bsh', x, W1[e]) + b1[e])
            y = jnp.einsum('bsh,dh->bsd', h, W2[e]) + b2[e]
            out = out + combine[..., e:e + 1] * y
        return out

    def _L2_gnn_ref(h6_all, edge_index, edge_weight, W, b, W1, b1, W2, b2):
        import jax, jax.numpy as jnp
        import numpy as np
        N_NODES = 3125
        N_EDGES = 50000
        D = 256
        'GCNConv(256->256, weighted, self-loops, symmetric norm) + 2-layer MLP head.'
        N = h6_all.shape[0]
        row, col = (edge_index[0], edge_index[1])
        sl = jnp.arange(N, dtype=edge_index.dtype)
        row_sl = jnp.concatenate([row, sl])
        col_sl = jnp.concatenate([col, sl])
        ew_sl = jnp.concatenate([edge_weight, jnp.ones((N,), dtype=edge_weight.dtype)])
        deg = jax.ops.segment_sum(ew_sl, row_sl, num_segments=N)
        dinv = jnp.where(deg > 0, jax.lax.rsqrt(deg), 0.0)
        norm = dinv[row_sl] * ew_sl * dinv[col_sl]
        xw = h6_all @ W
        msgs = xw[col_sl] * norm[:, None]
        h7 = jax.ops.segment_sum(msgs, row_sl, num_segments=N) + b
        h = jax.nn.relu(h7 @ W1 + b1)
        out = h @ W2 + b2
        return out

    def _L2_ffn_ref(x, Wr, br, W1, b1, W2, b2, gamma, beta):
        import math
        import jax, jax.numpy as jnp
        import numpy as np
        CAPACITY_FACTOR = 1.25
        TOP_K = 2
        LN_EPS = 1e-05

        def _layer_norm(x, gamma, beta):
            mu = jnp.mean(x, axis=-1, keepdims=True)
            var = jnp.var(x, axis=-1, keepdims=True)
            return (x - mu) * jax.lax.rsqrt(var + LN_EPS) * gamma + beta
        B, S, D = x.shape
        E = Wr.shape[1]
        N = B * S
        K = TOP_K
        logits = jnp.mean(x, axis=1) @ Wr + br
        routing_weights = jax.nn.softmax(logits, axis=-1)
        capacity = float(math.ceil(N * CAPACITY_FACTOR / E))
        expected_loads = routing_weights.sum(axis=0) * (N / B)
        scale = jnp.where(expected_loads > capacity, capacity / expected_loads, 1.0)
        routing_weights = jax.nn.softmax(routing_weights * scale, axis=-1)
        rw_tok = jnp.broadcast_to(routing_weights[:, None, :], (B, S, E)).reshape(N, E)
        top_w, top_i = jax.lax.top_k(rw_tok, K)
        top_w = jax.nn.softmax(top_w, axis=-1)
        xf = x.reshape(N, D)
        h = jax.nn.gelu(jnp.einsum('nd,edf->enf', xf, W1) + b1[:, None, :], approximate=False)
        y = jnp.einsum('enf,efd->end', h, W2) + b2[:, None, :]
        w_dense = jnp.zeros((N, E), x.dtype).at[jnp.arange(N)[:, None], top_i].add(top_w)
        out = jnp.einsum('ne,end->nd', w_dense, y).reshape(B, S, D)
        out = _layer_norm(out + x, gamma, beta)
        return out

    def _L3_gnn_ref(node_features, edge_idx, W1, b1, g1, be1, W2, b2, g2, be2, Wfc, bfc):
        import jax, jax.numpy as jnp
        import numpy as np
        N_NODES = 3125
        BN_EPS = 1e-05

        def gcn_conv(x, src, dst, W, b, n):
            h = x @ W
            loop = jnp.arange(n, dtype=src.dtype)
            s = jnp.concatenate([src, loop])
            d = jnp.concatenate([dst, loop])
            deg = jax.ops.segment_sum(jnp.ones(s.shape, h.dtype), d, num_segments=n)
            dinv = jnp.where(deg > 0, jax.lax.rsqrt(jnp.maximum(deg, 1.0)), 0.0)
            norm = dinv[s] * dinv[d]
            msg = h[s] * norm[:, None]
            out = jax.ops.segment_sum(msg, d, num_segments=n)
            return out + b

        def batch_norm(x, gamma, beta):
            mean = jnp.mean(x, axis=0)
            var = jnp.mean(jnp.square(x - mean), axis=0)
            return (x - mean) * jax.lax.rsqrt(var + BN_EPS) * gamma + beta
        n = node_features.shape[0]
        src, dst = (edge_idx[0], edge_idx[1])
        feats = [node_features]
        x = node_features
        x = gcn_conv(x, src, dst, W1, b1, n)
        x = jax.nn.relu(batch_norm(x, g1, be1))
        feats.append(x)
        x = gcn_conv(x, src, dst, W2, b2, n)
        x = jax.nn.relu(batch_norm(x, g2, be2))
        feats.append(x)
        cat = jnp.concatenate(feats, axis=1)
        return jax.nn.relu(cat @ Wfc + bfc)

    def _L3_ffn_ref(x, W_gat, att_src, att_dst, b_gat, ln_gamma, ln_beta, W1, b1, W2, b2, edge_index):
        import jax, jax.numpy as jnp
        import numpy as np
        B, N, D = (16, 128, 256)
        NUM_EXPERTS, TOP_K, HEADS = (4, 2, 4)
        N_EDGES = 32768
        LN_EPS = 1e-05

        def _layernorm(x, g, b):
            mu = x.mean(-1, keepdims=True)
            var = ((x - mu) ** 2).mean(-1, keepdims=True)
            return (x - mu) * jax.lax.rsqrt(var + LN_EPS) * g + b

        def _forward(x, edge_index, W_gat, att_src, att_dst, b_gat, ln_gamma, ln_beta, W1, b1, W2, b2):
            Bc, Nc, Dc = x.shape
            M = Bc * Nc
            x_flat = x.reshape(M, Dc)
            h = (x_flat @ W_gat).reshape(M, HEADS, NUM_EXPERTS)
            loops = jnp.arange(M, dtype=edge_index.dtype)
            src = jnp.concatenate([edge_index[0], loops])
            dst = jnp.concatenate([edge_index[1], loops])
            a_src = (h * att_src).sum(-1)
            a_dst = (h * att_dst).sum(-1)
            e = jax.nn.leaky_relu(a_src[src] + a_dst[dst], negative_slope=0.2)
            e_max = jax.ops.segment_max(e, dst, num_segments=M)
            ee = jnp.exp(e - e_max[dst])
            denom = jax.ops.segment_sum(ee, dst, num_segments=M)
            alpha = ee / (denom[dst] + 1e-16)
            msg = h[src] * alpha[:, :, None]
            agg = jax.ops.segment_sum(msg, dst, num_segments=M).reshape(M, HEADS * NUM_EXPERTS) + b_gat
            scores = _layernorm(agg, ln_gamma, ln_beta).reshape(M, HEADS, NUM_EXPERTS).mean(1)
            scores = scores.reshape(Bc, Nc, NUM_EXPERTS)
            topk_s, topk_i = jax.lax.top_k(scores, TOP_K)
            w = jax.nn.softmax(topk_s, axis=-1)
            out = jnp.zeros_like(x)
            for ei in range(NUM_EXPERTS):
                g = jnp.where(topk_i == ei, w, 0.0).sum(-1)
                hh = jax.nn.gelu(x @ W1[ei] + b1[ei], approximate=False)
                out = out + g[..., None] * (hh @ W2[ei] + b2[ei])
            return out
        return _forward(x, edge_index, W_gat, att_src, att_dst, b_gat, ln_gamma, ln_beta, W1, b1, W2, b2)
    edge_index = jnp.stack([src, dst])
    batch0 = jnp.zeros((3125,), jnp.int32)
    x = x + _L0_gnn_ref(_layernorm(x, axis=-1), L0_gnn_W_neigh, L0_gnn_W_self, L0_gnn_b_self, src, dst)
    x = x + _L0_ffn_ref(_layernorm(x, axis=-1)[None], L0_ffn_gate_w, L0_ffn_gate_b, L0_ffn_w1, L0_ffn_b1, L0_ffn_w2, L0_ffn_b2)[0]
    x = x + _L1_gnn_ref(_layernorm(x, axis=-1), edge_index, batch0, L1_gnn_Wq, L1_gnn_Wk, L1_gnn_Wv, L1_gnn_Wo_w, L1_gnn_Wo_b, L1_gnn_ln1_g, L1_gnn_ln1_b, L1_gnn_ln2_g, L1_gnn_ln2_b, L1_gnn_ffn_w1, L1_gnn_ffn_b1, L1_gnn_ffn_w2, L1_gnn_ffn_b2)
    x = x + _L1_ffn_ref(_layernorm(x, axis=-1)[None], L1_ffn_Wg, L1_ffn_bg, L1_ffn_W1, L1_ffn_b1, L1_ffn_W2, L1_ffn_b2)[0]
    x = x + _L2_gnn_ref(_layernorm(x, axis=-1), edge_index, edge_weight, L2_gnn_W, L2_gnn_b, L2_gnn_W1, L2_gnn_b1, L2_gnn_W2, L2_gnn_b2)
    x = x + _L2_ffn_ref(_layernorm(x, axis=-1)[None], L2_ffn_Wr, L2_ffn_br, L2_ffn_W1, L2_ffn_b1, L2_ffn_W2, L2_ffn_b2, L2_ffn_gamma, L2_ffn_beta)[0]
    x = x + _L3_gnn_ref(_layernorm(x, axis=-1), edge_index, L3_gnn_W1, L3_gnn_b1, L3_gnn_g1, L3_gnn_be1, L3_gnn_W2, L3_gnn_b2, L3_gnn_g2, L3_gnn_be2, L3_gnn_Wfc, L3_gnn_bfc)
    x = x + _L3_ffn_ref(_layernorm(x, axis=-1)[None], L3_ffn_W_gat, L3_ffn_att_src, L3_ffn_att_dst, L3_ffn_b_gat, L3_ffn_ln_gamma, L3_ffn_ln_beta, L3_ffn_W1, L3_ffn_b1, L3_ffn_W2, L3_ffn_b2, L3_ffn_edge_index)[0]
    return x

_drawn_inputs = setup_inputs


def setup_inputs(seed=0):
    import zlib

    import numpy as np

    out = dict(_drawn_inputs(seed))
    spreads = {'L0_gnn_b_self': (0.0, 0.1),
     'L0_ffn_gate_b': (0.0, 0.1),
     'L0_ffn_b1': (0.0, 0.578),
     'L0_ffn_b2': (0.0, 0.457),
     'L1_gnn_Wo_b': (0.0, 0.1),
     'L1_gnn_ln1_g': (1.0, 0.2),
     'L1_gnn_ln1_b': (0.0, 0.1),
     'L1_gnn_ln2_g': (1.0, 0.2),
     'L1_gnn_ln2_b': (0.0, 0.1),
     'L1_gnn_ffn_b1': (0.0, 0.285),
     'L1_gnn_ffn_b2': (0.0, 0.1),
     'L2_gnn_b': (0.0, 0.1),
     'L2_gnn_b1': (0.0, 0.1),
     'L2_gnn_b2': (0.0, 0.1),
     'L2_ffn_br': (0.0, 0.8),
     'L2_ffn_b1': (0.0, 0.424),
     'L2_ffn_b2': (0.0, 0.28),
     'L2_ffn_gamma': (1.0, 0.2),
     'L2_ffn_beta': (0.0, 0.1),
     'L3_gnn_b1': (0.0, 0.8),
     'L3_gnn_g1': (1.0, 0.6),
     'L3_gnn_be1': (0.0, 0.541),
     'L3_gnn_b2': (0.0, 0.8),
     'L3_gnn_g2': (1.0, 0.6),
     'L3_gnn_be2': (0.0, 0.8),
     'L3_gnn_bfc': (0.0, 0.306),
     'L3_ffn_b_gat': (0.0, 0.1),
     'L3_ffn_ln_gamma': (1.0, 0.2),
     'L3_ffn_ln_beta': (0.0, 0.304),
     'L3_ffn_b1': (0.0, 0.53),
     'L3_ffn_b2': (0.0, 0.381)}
    factors = {'L1_gnn_Wq': 3.33,
     'L1_gnn_Wk': 3.111,
     'L1_ffn_bg': 3.551,
     'L1_ffn_b1': 8.0,
     'L1_ffn_b2': 7.176,
     'L3_ffn_att_src': 3.573,
     'L3_ffn_att_dst': 5.924}
    for name, (base, spread) in spreads.items():
        noise = np.random.default_rng([zlib.crc32(name.encode()), seed]).standard_normal(out[name].shape)
        drawn = base * np.exp(spread * noise) if base else spread * noise
        out[name] = jnp.asarray(drawn.astype(out[name].dtype))
    for name, factor in factors.items():
        out[name] = (out[name] * factor).astype(out[name].dtype)
    return out
```

```python
from contextlib import ExitStack

import concourse.bass as bass
from concourse import mybir

F32 = mybir.dt.float32
BF16 = mybir.dt.bfloat16
I32 = mybir.dt.int32
ALU = mybir.AluOpType
ACT = mybir.ActivationFunctionType
AX = mybir.AxisListType

N = 3125
P = 125
T = N // P
D = 256
DC = D // 128
EC = 128
RING = 5
FIELDS = 4
EPS = 1e-5
GROUP = RING * P
PIECES = ((0, 375), (375, 250))


def chunk_bound(edges):
    most = (edges + T * (EC - 1)) // EC
    return -(-most // 8) * 8


class Stage:

    count = 0

    def __init__(self, nc, name):
        Stage.count += 1
        self.nc, self.name, self.ctx, self.sems = nc, f"{name}{Stage.count}", ExitStack(), []

    def __enter__(self):
        self.ctx.__enter__()
        return self

    def __exit__(self, *e):
        if self.sems and e[0] is None:
            self.nc.clear_and_free_semaphores(self.sems)
            self.nc.all_engine_barrier()
        return self.ctx.__exit__(*e)

    def sb(self, name, shape, dt=F32):
        return self.ctx.enter_context(self.nc.sbuf_tensor(f"{self.name}_{name}", shape, dt))

    def ps(self, name, shape, dt=F32):
        return self.ctx.enter_context(self.nc.psum_tensor(f"{self.name}_{name}", shape, dt))

    def sem(self, name):
        self.sems.append(self.nc.alloc_semaphore(f"{self.name}_{name}"))
        return self.sems[-1]

    def block(self):
        return self.nc.Block()


class Steps:

    def __init__(self, eng, sem):
        self.eng, self.sem, self.n, self.at = eng, sem, 0, None

    def __call__(self, ins):
        ins.then_inc(self.sem, 1)
        self.n += 1
        self.eng.wait_ge(self.sem, self.n if self.at is None else self.at + self.n)

    def loop(self, i, per):
        self.base, self.at, self.n = (self.n, self.n + i * per, 0)

    def leave(self, count, per):
        assert self.n == per, (self.n, per)
        self.n, self.at = self.base + count * per, None


def bcast(ap, shape):
    return ap.broadcast_to(shape)


def tile_of(t, width):
    return bass.ds(t * width, width)



def constants(nc, c, I):
    with Stage(nc, "const") as s:
        zero = s.sem("zero")
        made = s.sem("made")
        with s.block() as block:
            @block.gpsimd
            def _(pool):
                nc.gpsimd.memset(c["ident"][:], 0.0).then_inc(zero, 1)
                nc.gpsimd.iota(c["iota"][:], pattern=[[1, 128]], base=0, channel_multiplier=0,
                               allow_small_or_imprecise_dtypes=True).then_inc(made, 1)
                nc.gpsimd.memset(c["ones"][:], 1.0).then_inc(made, 1)
                pool.wait_ge(zero, 1)
                nc.gpsimd.affine_select(out=c["ident"][:], in_=c["ident"][:], compare_op=ALU.not_equal,
                                        fill=1.0, base=0, pattern=[[-1, 128]],
                                        channel_multiplier=1).then_inc(made, 1)



def transfer(nc, name, pairs):
    with Stage(nc, name) as s:
        by_sync, by_act = s.sem("by_sync"), s.sem("by_act")
        with s.block() as block:
            @block.sync
            def _(sp):
                for dst, src in pairs[0::2]:
                    sp.dma_start(dst, src).then_inc(by_sync, 16)
                sp.wait_ge(by_sync, 16 * len(pairs[0::2]))

            @block.scalar
            def _(act):
                for dst, src in pairs[1::2]:
                    act.dma_start(dst, src).then_inc(by_act, 16)
                if len(pairs) > 1:
                    act.wait_ge(by_act, 16 * len(pairs[1::2]))


def by_tile(dram, width):
    return dram.rearrange("(t p) f -> p t f", p=P)


def as_tiles(sb, width):
    return sb[:].rearrange("p (t f) -> p t f", f=width)



def bucket(nc, c, name, key_d, other_d, weight_d, parts, cols, loops, chunks, sorted_d, rec, blk):
    iters, groups, per = loops
    assert iters * groups * per == cols
    with Stage(nc, name) as s:
        key_i = s.sb("key_i", [parts, cols], I32)
        other_i = s.sb("other_i", [parts, cols], I32)
        key = s.sb("key", [parts, cols])
        thr = s.sb("thr", [128, T + 1])
        member = s.sb("member", [parts, T * cols], BF16)
        before = s.sb("before", [parts, T * cols])
        above = s.sb("above", [parts, cols])
        zeros = s.sb("zeros", [parts, cols])
        carry = s.sb("carry", [parts, 1])
        ones_b = s.sb("ones_b", [parts, parts], BF16)
        tri = s.sb("tri", [parts, parts], BF16)
        first = s.sb("first", [parts, T])
        ends = s.sb("ends", [parts, T])
        count_f = s.sb("count_f", [parts, T])
        count_i = s.sb("count_i", [parts, T], I32)
        cstart = s.sb("cstart", [parts, T])
        cend = s.sb("cend", [parts, T])
        adj = s.sb("adj", [parts, T])
        pos = s.sb("pos", [parts, cols])
        sub = s.sb("sub", [parts, cols])
        q1 = s.sb("q1", [parts, cols])
        q2 = s.sb("q2", [parts, cols])
        pos_i = s.sb("pos_i", [parts, cols], I32)
        row_i = s.sb("row_i", [parts, cols], I32)
        slot_i = s.sb("slot_i", [parts, cols], I32)
        records = s.sb("records", [parts, cols * FIELDS])
        blk_f = s.sb("blk_f", [1, chunks])
        citer = s.sb("citer", [1, chunks])
        rec_s = [s.sb(f"rec_s{g}", [parts, per * FIELDS]) for g in range(groups)]
        dst_s = [s.sb(f"dst_s{g}", [parts, per], I32) for g in range(groups)]
        ps = [s.ps(f"ps{h}", [parts, 512]) for h in range(2)]
        loaded = s.sem("loaded")
        steps = s.sem("steps")
        made = s.sem("made")
        blank = s.sem("blank")
        blanked = s.sem("blanked")
        masks = s.sem("masks")
        totals = s.sem("totals")
        summed = s.sem("summed")
        ranks = s.sem("ranks")
        ranked = s.sem("ranked")
        staged = [s.sem(f"staged{g}") for g in range(groups)]
        sent = [s.sem(f"sent{g}") for g in range(groups)]
        back = s.sem("back")
        go = s.sem("go")
        rec4 = records[:].rearrange("p (c f) -> p c f", f=FIELDS)

        with s.block() as block:
            @block.sync
            def _(sp):
                sp.dma_start(key_i[:], key_d).then_inc(loaded, 16)
                sp.dma_start(other_i[:], other_d).then_inc(loaded, 16)
                if weight_d is not None:
                    sp.dma_start(sub[:], weight_d).then_inc(loaded, 16)
                sp.wait_ge(blank, 2)
                sp.dma_start(sorted_d.rearrange("(p c) f -> p (c f)", p=EC), rec[:]).then_inc(blanked, 16)
                for g in range(groups):
                    sp.wait_ge(sent[g], 16 * per * iters)
                sp.dma_start(rec[:], sorted_d.rearrange("(p c) f -> p (c f)", p=EC)).then_inc(back, 16)
                sp.wait_ge(back, 16)

            @block.gpsimd
            def _(pool):
                nc.gpsimd.iota(thr[:], pattern=[[P, T + 1]], base=0, channel_multiplier=0,
                               allow_small_or_imprecise_dtypes=True).then_inc(made, 1)
                nc.gpsimd.iota(citer[:], pattern=[[1, chunks]], base=0, channel_multiplier=0,
                               allow_small_or_imprecise_dtypes=True).then_inc(made, 1)
                nc.gpsimd.memset(tri[:], -1.0).then_inc(made, 1)
                nc.gpsimd.memset(ones_b[:], 1.0).then_inc(made, 1)
                pool.wait_ge(made, 4)
                nc.gpsimd.affine_select(out=tri[:], in_=tri[:], compare_op=ALU.is_ge, fill=0.0, base=0,
                                        pattern=[[-1, parts]], channel_multiplier=1).then_inc(made, 1)
                pool.wait_ge(blanked, 16)
                with pool.Fori(0, iters) as i:
                    for g in range(groups):
                        pool.wait_ge(staged[g], 2 * i + 2)
                        pool.sem_inc(go, 1)
                        for k in range(per):
                            pool.indirect_dma_start(
                                sorted_d, bass.IndirectOffsetOnAxis(ap=dst_s[g][:, k:k + 1], axis=0),
                                rec_s[g][:, k * FIELDS:(k + 1) * FIELDS], None).then_inc(sent[g], 16)

            @block.tensor
            def _(pe):
                pe.wait_ge(made, 5)
                pe.wait_ge(masks, T)
                with pe.Fori(0, T) as b:
                    pe.wait_ge(summed, b)
                    nc.tensor.matmul(ps[0][:, 0:cols], ones_b[:], member[:, tile_of(b, cols)],
                                     start=True, stop=True).then_inc(totals, 1)
                with pe.Fori(0, T) as b:
                    pe.wait_ge(ranked, b)
                    nc.tensor.matmul(ps[1][:, 0:cols], tri[:], member[:, tile_of(b, cols)],
                                     start=True, stop=True).then_inc(ranks, 1)

            @block.vector
            def _(dve):
                step = Steps(dve, steps)
                nc.vector.memset(rec[:], 0.0).then_inc(blank, 1)
                dve.wait_ge(blank, 1)
                nc.vector.memset(rec[:].rearrange("p (c f) -> p c f", f=FIELDS)[:, :, 1], -1.0).then_inc(blank, 1)
                dve.wait_ge(loaded, 32 if weight_d is None else 48)
                dve.wait_ge(made, 5)
                step(nc.vector.tensor_copy(key[:], key_i[:]))
                step(nc.vector.memset(records[:], 1.0))
                step(nc.vector.tensor_copy(rec4[:, :, 0], other_i[:]))
                if weight_d is not None:
                    step(nc.vector.tensor_copy(rec4[:, :, 2], sub[:]))
                step(nc.vector.memset(zeros[:], 0.0))
                step(nc.vector.memset(carry[:], 0.0))
                step(nc.vector.memset(pos[:], 0.0))
                step(nc.vector.tensor_copy(sub[:], key[:]))
                with dve.Fori(0, T) as b:
                    step.loop(b, 1)
                    dve.wait_ge(masks, b)
                    step(nc.vector.tensor_scalar(above[:], key[:], thr[0:parts, bass.ds(b, 1)], None, ALU.is_ge))
                    nc.vector.scalar_tensor_tensor(member[:, tile_of(b, cols)], key[:],
                                                   thr[0:parts, bass.ds(b + 1, 1)], above[:],
                                                   ALU.is_lt, ALU.mult).then_inc(masks, 1)
                step.leave(T, 1)
                with dve.Fori(0, T) as b:
                    step.loop(b, 1)
                    dve.wait_ge(totals, b + 1)
                    step(nc.vector.tensor_tensor_scan(before[:, tile_of(b, cols)], zeros[:], ps[0][:, 0:cols],
                                                      carry[:], ALU.add, ALU.add))
                    nc.vector.tensor_copy(carry[:], before[:, bass.ds(b * cols + cols - 1, 1)]).then_inc(summed, 1)
                    dve.wait_ge(summed, b + 1)
                step.leave(T, 1)
                last = before[:].rearrange("p (b c) -> p b c", c=cols)[:, :, cols - 1]
                step(nc.vector.tensor_copy(ends[:], last))
                step(nc.vector.memset(first[:], 0.0))
                step(nc.vector.tensor_copy(first[:, 1:T], ends[:, 0:T - 1]))
                step(nc.vector.tensor_tensor(count_f[:], ends[:], first[:], ALU.subtract))
                step(nc.vector.tensor_scalar(count_f[:], count_f[:], float(EC - 1), None, ALU.add))
                step(nc.vector.tensor_copy(count_i[:], count_f[:]))
                step(nc.vector.tensor_scalar(count_i[:], count_i[:], 7, None, ALU.arith_shift_right))
                step(nc.vector.tensor_copy(count_f[:], count_i[:]))
                step(nc.vector.tensor_tensor_scan(cend[:], zeros[:, 0:T], count_f[:], 0.0, ALU.add, ALU.add))
                step(nc.vector.tensor_tensor(cstart[:], cend[:], count_f[:], ALU.subtract))
                step(nc.vector.scalar_tensor_tensor(adj[:], cstart[:], float(EC), first[:], ALU.mult, ALU.subtract))
                step(nc.vector.memset(blk_f[:], -1.0))
                for b in range(T):
                    step(nc.vector.scalar_tensor_tensor(blk_f[:], citer[:], cstart[0:1, b:b + 1], blk_f[:],
                                                        ALU.is_ge, ALU.add))
                step(nc.vector.tensor_copy(blk[:], blk_f[:]))
                with dve.Fori(0, T) as b:
                    step.loop(b, 3)
                    dve.wait_ge(ranks, b + 1)
                    nc.vector.scalar_tensor_tensor(q1[:], ps[1][:, 0:cols], adj[:, bass.ds(b, 1)],
                                                   before[:, tile_of(b, cols)], ALU.add, ALU.add).then_inc(ranked, 1)
                    dve.wait_ge(ranked, b + 1)
                    step(nc.vector.tensor_tensor(q2[:], q1[:], member[:, tile_of(b, cols)], ALU.mult))
                    step(nc.vector.tensor_tensor(pos[:], pos[:], q2[:], ALU.add))
                    step(nc.vector.scalar_tensor_tensor(q2[:], member[:, tile_of(b, cols)],
                                                        thr[0:parts, bass.ds(b, 1)], sub[:], ALU.mult, ALU.subtract))
                    nc.vector.tensor_scalar(sub[:], q2[:], -1.0, None, ALU.mult).then_inc(masks, 1)
                    dve.wait_ge(masks, T + 1 + b)
                step.leave(T, 3)
                step(nc.vector.tensor_copy(rec4[:, :, 1], sub[:]))
                step(nc.vector.tensor_copy(pos_i[:], pos[:]))
                step(nc.vector.tensor_scalar(row_i[:], pos_i[:], EC - 1, None, ALU.bitwise_and))
                step(nc.vector.tensor_scalar(slot_i[:], pos_i[:], 7, None, ALU.arith_shift_right))
                step(nc.vector.tensor_copy(q1[:], row_i[:]))
                step(nc.vector.tensor_copy(q2[:], slot_i[:]))
                step(nc.vector.scalar_tensor_tensor(pos[:], q1[:], float(chunks), q2[:], ALU.mult, ALU.add))
                step(nc.vector.tensor_copy(pos_i[:], pos[:]))
                with dve.Fori(0, iters) as i:
                    for g in range(groups):
                        dve.wait_ge(sent[g], 16 * per * i)
                        at = (i * groups + g) * per
                        nc.vector.tensor_copy(rec_s[g][:], records[:, bass.ds(at * FIELDS, per * FIELDS)]).then_inc(staged[g], 1)
                        nc.vector.tensor_copy(dst_s[g][:], pos_i[:, bass.ds(at, per)]).then_inc(staged[g], 1)



U = 8
HALF = 4


def ahead(i, u, by, last):
    v = u + by
    if v < U:
        return i, v
    return None if last else (i + 1, v - U)


def edge_loop(eng, chunks, body, before=None):
    if before is not None:
        before()
    with eng.Fori(0, chunks // U - 1) as i:
        body(i, False)
    body(chunks // U - 1, True)


def stage_records(nc, act, chunks, rec, rec_s, idx_s, staged, landed, onehots):
    def body(i, last):
        for h in range(2):
            if landed is not None:
                for u in range(HALF):
                    act.wait_ge(landed[HALF * h + u], 16 * i)
            act.wait_ge(onehots, U * i + HALF * (h + 1))
            src = rec[:, bass.ds((i * U + h * HALF) * FIELDS, HALF * FIELDS)]
            if idx_s is not None:
                nc.scalar.copy(idx_s[h][:], src.rearrange("p (u f) -> p u f", f=FIELDS)[:, :, 0]).then_inc(staged[h], 1)
            nc.scalar.copy(rec_s[h][:], src).then_inc(staged[h], 1)
    edge_loop(act, chunks, body)


def gather_rows(nc, pool, chunks, table, idx_s, slots, staged, used, landed, go):
    def body(i, last):
        for u in range(U):
            if u % HALF == 0:
                pool.wait_ge(staged[u // HALF], 2 * i + 2)
            pool.wait_ge(used, U * i + u + 1)
            pool.sem_inc(go, 1)
            pool.indirect_dma_start(slots[u], None, table,
                                    bass.IndirectOffsetOnAxis(ap=idx_s[u // HALF][:, u % HALF:u % HALF + 1], axis=0)
                                    ).then_inc(landed[u], 16)
    edge_loop(pool, chunks, body)


def one_hot(nc, c, dve, out, rec_s, u):
    r = rec_s[u // HALF]
    k = (u % HALF) * FIELDS
    return nc.vector.tensor_scalar(out[:, 0:P], c["iota"][:, 0:P], r[:, k + 1:k + 2], r[:, k + 2:k + 3],
                                   ALU.is_equal, ALU.mult)


def segment_sum(nc, c, name, table, width, rec, blk, chunks, acc, count):
    wide = width + (1 if count else 0)
    with Stage(nc, name) as s:
        rec_s = [s.sb(f"rec_s{h}", [EC, HALF * FIELDS]) for h in range(2)]
        idx_s = [s.sb(f"idx_s{h}", [EC, HALF], I32) for h in range(2)] if table is not None else None
        rows = [s.sb(f"rows{u}", [EC, wide]) for u in range(U)] if table is not None else None
        oh = [s.sb(f"oh{u}", [EC, 128]) for u in range(HALF)]
        ps = [s.ps(f"ps{u}", [P, 512]) for u in range(HALF)]
        staged = [s.sem(f"staged{h}") for h in range(2)]
        landed = [s.sem(f"landed{u}") for u in range(U)] if table is not None else None
        onehots = s.sem("onehots")
        used = s.sem("used")
        added = s.sem("added")
        zeroed, go, counted = s.sem("zeroed"), s.sem("go"), s.sem("counted")
        per_half = 2 if table is not None else 1
        with s.block() as block:
            @block.scalar
            def _(act):
                stage_records(nc, act, chunks, rec, rec_s, idx_s, staged, landed, onehots)

            if table is not None:
                @block.gpsimd
                def _(pool):
                    gather_rows(nc, pool, chunks, table, idx_s, [r[:, 0:width] for r in rows], staged, used, landed, go)

            @block.vector
            def _(dve):
                dve.sem_inc(onehots, U)
                dve.sem_inc(added, HALF)
                if count and table is not None:
                    for u in range(U):
                        nc.vector.memset(rows[u][:, width:wide], 1.0).then_inc(counted, 1)
                nc.vector.memset(acc[:], 0.0).then_inc(zeroed, 1)
                dve.wait_ge(zeroed, 1)

                def make(i, u):
                    if u % HALF == 0:
                        dve.wait_ge(staged[u // HALF], per_half * (i + 1))
                    dve.wait_ge(used, U * i + u + 1 + HALF)
                    one_hot(nc, c, dve, oh[u % HALF], rec_s, u).then_inc(onehots, 1)

                def body(i, last):
                    for u in range(U):
                        nxt = ahead(i, u, HALF - 1, last)
                        if nxt:
                            make(*nxt)
                        b = dve.value_load(blk[0:1, bass.ds(i * U + u, 1)], min_val=0, max_val=T - 1)
                        dve.wait_ge(used, U + U * i + u + 1)
                        dve.wait_ge(added, HALF + U * i + u)
                        to = acc[:, bass.ds(b * wide, wide)]
                        nc.vector.tensor_tensor(to, to, ps[u % HALF][:, 0:wide], ALU.add).then_inc(added, 1)

                edge_loop(dve, chunks, body, lambda: [make(0, u) for u in range(HALF - 1)])

            @block.tensor
            def _(pe):
                pe.sem_inc(used, U)
                if count and table is not None:
                    pe.wait_ge(counted, U)

                def body(i, last):
                    for u in range(U):
                        if table is not None:
                            pe.wait_ge(landed[u], 16 * i + 16)
                        pe.wait_ge(onehots, U + U * i + u + 1)
                        pe.wait_ge(added, U * i + u + 1)
                        rhs = rows[u][:] if table is not None else c["ones"][:, 0:1]
                        nc.tensor.matmul(ps[u % HALF][:, 0:wide], oh[u % HALF][:, 0:P], rhs,
                                         start=True, stop=True).then_inc(used, 1)
                edge_loop(pe, chunks, body)


def edge_scores(nc, c, name, k_table, q, rec, blk, chunks, heads, scale, scores):
    with Stage(nc, name) as s:
        rec_s = [s.sb(f"rec_s{h}", [EC, HALF * FIELDS]) for h in range(2)]
        idx_s = [s.sb(f"idx_s{h}", [EC, HALF], I32) for h in range(2)]
        rows = [s.sb(f"rows{u}", [EC, D]) for u in range(U)]
        oh = [s.sb(f"oh{u}", [EC, 128]) for u in range(HALF)]
        oht = [s.sb(f"oht{u}", [P, EC]) for u in range(HALF)]
        prod = [s.sb(f"prod{u}", [EC, D]) for u in range(2)]
        ps_t = [s.ps(f"ps_t{u}", [P, 512]) for u in range(2)]
        ps_q = [s.ps(f"ps_q{u}", [EC, 512]) for u in range(4)]
        staged = [s.sem(f"staged{h}") for h in range(2)]
        landed = [s.sem(f"landed{u}") for u in range(U)]
        onehots = s.sem("onehots")
        turned = s.sem("turned")
        kept = s.sem("kept")
        spread = s.sem("spread")
        multiplied = s.sem("multiplied")
        reduced, go = s.sem("reduced"), s.sem("go")
        with s.block() as block:
            @block.scalar
            def _(act):
                act.sem_inc(kept, HALF)

                def stage(i, h):
                    for u in range(HALF):
                        act.wait_ge(landed[HALF * h + u], 16 * i)
                    act.wait_ge(onehots, U * i + HALF * (h + 1))
                    src = rec[:, bass.ds((i * U + h * HALF) * FIELDS, HALF * FIELDS)]
                    nc.scalar.copy(idx_s[h][:], src.rearrange("p (u f) -> p u f", f=FIELDS)[:, :, 0]).then_inc(staged[h], 1)
                    nc.scalar.copy(rec_s[h][:], src).then_inc(staged[h], 1)

                def body(i, last):
                    for u in range(U):
                        act.wait_ge(turned, HALF + U * i + u + 1)
                        act.wait_ge(spread, U * i + u + 1)
                        nc.scalar.copy(oht[u % HALF][:], ps_t[u % 2][:, 0:EC]).then_inc(kept, 1)
                        if u % HALF == HALF - 1 and not last:
                            stage(i + 1, u // HALF)
                edge_loop(act, chunks, body, lambda: [stage(0, h) for h in range(2)])

            @block.gpsimd
            def _(pool):
                gather_rows(nc, pool, chunks, k_table, idx_s, [r[:] for r in rows], staged, multiplied, landed, go)

            @block.vector
            def _(dve):
                dve.sem_inc(onehots, U)
                dve.sem_inc(multiplied, U)
                dve.sem_inc(reduced, 2)

                def make(i, u):
                    if u % HALF == 0:
                        dve.wait_ge(staged[u // HALF], 2 * (i + 1))
                    dve.wait_ge(turned, U * i + u + 1)
                    one_hot(nc, c, dve, oh[u % HALF], rec_s, u).then_inc(onehots, 1)

                def body(i, last):
                    for u in range(U):
                        nxt = ahead(i, u, HALF - 1, last)
                        if nxt:
                            make(*nxt)
                        dve.wait_ge(spread, HALF + U * i + u + 1)
                        dve.wait_ge(landed[u], 16 * i + 16)
                        dve.wait_ge(reduced, U * i + u + 1)
                        nc.vector.scalar_tensor_tensor(prod[u % 2][:], ps_q[u % 4][:, 0:D], float(scale), rows[u][:],
                                                       ALU.mult, ALU.mult).then_inc(multiplied, 1)
                        dve.wait_ge(multiplied, U + U * i + u + 1)
                        nc.vector.tensor_reduce(scores[:, bass.ds((i * U + u) * heads, heads)],
                                                prod[u % 2][:].rearrange("p (h d) -> p h d", h=heads),
                                                AX.X, ALU.add).then_inc(reduced, 1)
                edge_loop(dve, chunks, body, lambda: [make(0, u) for u in range(HALF - 1)])

            @block.tensor
            def _(pe):
                pe.sem_inc(turned, HALF)
                pe.sem_inc(spread, HALF)

                def turn(i, u):
                    pe.wait_ge(onehots, U + U * i + u + 1)
                    pe.wait_ge(kept, U * i + u + 3)
                    nc.tensor.transpose(ps_t[u % 2][:, 0:EC], oh[u % HALF][:, 0:P], c["ident"][:]).then_inc(turned, 1)

                def body(i, last):
                    for u in range(U):
                        nxt = ahead(i, u, 2, last)
                        if nxt:
                            turn(*nxt)
                        b = pe.value_load(blk[0:1, bass.ds(i * U + u, 1)], min_val=0, max_val=T - 1)
                        pe.wait_ge(kept, HALF + U * i + u + 1)
                        pe.wait_ge(multiplied, U * i + u + 1 + HALF)
                        nc.tensor.matmul(ps_q[u % 4][:, 0:D], oht[u % HALF][:], q[:, bass.ds(b * D, D)],
                                         start=True, stop=True).then_inc(spread, 1)
                edge_loop(pe, chunks, body, lambda: [turn(0, u) for u in range(2)])


BIG = 1e30


def segment_max(nc, c, name, values, stride, heads, rec, blk, chunks, best, masked):
    wide = heads * EC
    banks = wide // 512
    with Stage(nc, name) as s:
        rec_s = [s.sb(f"rec_s{h}", [EC, HALF * FIELDS]) for h in range(2)]
        oh = [s.sb(f"oh{u}", [EC, 128]) for u in range(HALF)]
        away = [s.sb(f"away{u}", [EC, 128], BF16) for u in range(HALF)]
        ident_b = s.sb("ident_b", [EC, 512], BF16)
        diag = [s.sb(f"diag{u}", [EC, wide]) for u in range(2)]
        top = [s.sb(f"top{u}", [P, heads]) for u in range(2)]
        ps = [s.ps(f"ps{u}", [P, 512 * banks]) for u in range(2)]
        staged = [s.sem(f"staged{h}") for h in range(2)]
        onehots = s.sem("onehots")
        aways = s.sem("aways")
        diags = s.sem("diags")
        spread = s.sem("spread")
        reduced = s.sem("reduced")
        merged = s.sem("merged")
        idents = s.sem("idents")
        with s.block() as block:
            @block.scalar
            def _(act):
                def stage(i, h):
                    act.wait_ge(onehots, U * i + HALF * (h + 1))
                    nc.scalar.copy(rec_s[h][:], rec[:, bass.ds((i * U + h * HALF) * FIELDS, HALF * FIELDS)]
                                   ).then_inc(staged[h], 1)

                def body(i, last):
                    for u in range(U):
                        act.wait_ge(spread, U * i + u + 3)
                        for h in range(heads):
                            ins = nc.scalar.activation(diag[u % 2][:, h * EC:(h + 1) * EC], c["ident"][:], ACT.Copy,
                                                       scale=values[:, bass.ds((i * U + u) * stride + h, 1)])
                        ins.then_inc(diags, 1)
                        if u % HALF == HALF - 1 and not last:
                            stage(i + 1, u // HALF)
                edge_loop(act, chunks, body, lambda: [stage(0, h) for h in range(2)])

            @block.vector
            def _(dve):
                dve.sem_inc(onehots, U)
                dve.sem_inc(reduced, 2)
                dve.sem_inc(merged, 2)
                if masked:
                    for k in range(4):
                        nc.vector.tensor_copy(ident_b[:, k * EC:(k + 1) * EC], c["ident"][:]).then_inc(idents, 1)

                def make(i, u):
                    if u % HALF == 0:
                        dve.wait_ge(staged[u // HALF], i + 1)
                    dve.wait_ge(spread, U * i + u + 1)
                    one_hot(nc, c, dve, oh[u % HALF], rec_s, u).then_inc(onehots, 1)
                    if masked:
                        dve.wait_ge(onehots, U + U * i + u + 1)
                        nc.vector.tensor_scalar(away[u % HALF][:, 0:P], oh[u % HALF][:, 0:P], 1.0, BIG,
                                                ALU.subtract, ALU.mult).then_inc(aways, 1)

                def body(i, last):
                    for u in range(U):
                        nxt = ahead(i, u, HALF - 1, last)
                        if nxt:
                            make(*nxt)
                        b = dve.value_load(blk[0:1, bass.ds(i * U + u, 1)], min_val=0, max_val=T - 1)
                        dve.wait_ge(spread, HALF + U * i + u + 1)
                        dve.wait_ge(merged, U * i + u + 1)
                        nc.vector.tensor_reduce(top[u % 2][:], ps[u % 2][:, 0:wide].rearrange("p (h e) -> p h e", e=EC),
                                                AX.X, ALU.max).then_inc(reduced, 1)
                        dve.wait_ge(reduced, 2 + U * i + u + 1)
                        dve.wait_ge(merged, U * i + u + 2)
                        to = best[:, bass.ds(b * heads, heads)]
                        nc.vector.tensor_tensor(to, to, top[u % 2][:], ALU.max).then_inc(merged, 1)
                edge_loop(dve, chunks, body, lambda: [make(0, u) for u in range(HALF - 1)])

            @block.tensor
            def _(pe):
                pe.sem_inc(spread, HALF)
                if masked:
                    pe.wait_ge(idents, 4)

                def body(i, last):
                    for u in range(U):
                        pe.wait_ge(onehots, U + U * i + u + 1)
                        pe.wait_ge(diags, U * i + u + 1)
                        pe.wait_ge(reduced, U * i + u + 1)
                        if masked:
                            pe.wait_ge(aways, U * i + u + 1)
                        for k in range(banks):
                            out = ps[u % 2][:, 512 * k:512 * (k + 1)]
                            if masked:
                                nc.tensor.matmul(out, away[u % HALF][:, 0:P], ident_b[:], start=True, stop=False)
                            ins = nc.tensor.matmul(out, oh[u % HALF][:, 0:P], diag[u % 2][:, 512 * k:512 * (k + 1)],
                                                   start=not masked, stop=True)
                        ins.then_inc(spread, 1)
                edge_loop(pe, chunks, body)


def softmax_sum(nc, c, name, heads, hd, rec, blk, chunks, acc, per_node, pn, table, scores, stored, leaky):
    vw = heads * hd
    wide = vw + heads
    with Stage(nc, name) as s:
        rec_s = [s.sb(f"rec_s{h}", [EC, HALF * FIELDS]) for h in range(2)]
        idx_s = [s.sb(f"idx_s{h}", [EC, HALF], I32) for h in range(2)]
        rows = [s.sb(f"rows{u}", [EC, vw]) for u in range(U)] if table is not None else None
        oh = [s.sb(f"oh{u}", [EC, 128]) for u in range(U)]
        oht = [s.sb(f"oht{u}", [P, EC]) for u in range(HALF)]
        arg = [s.sb(f"arg{u}", [EC, heads]) for u in range(HALF)]
        arg2 = [s.sb(f"arg2{u}", [EC, heads]) for u in range(HALF)]
        msg = [s.sb(f"msg{u}", [EC, wide]) for u in range(HALF)]
        ps_t = [s.ps(f"ps_t{u}", [P, 512]) for u in range(2)]
        ps_n = [s.ps(f"ps_n{u}", [EC, 512]) for u in range(2)]
        ps_a = [s.ps(f"ps_a{u}", [P, 512]) for u in range(4)]
        staged = [s.sem(f"staged{h}") for h in range(2)]
        landed = [s.sem(f"landed{u}") for u in range(U)]
        onehots = s.sem("onehots")
        turned = s.sem("turned")
        kept = s.sem("kept")
        spread = s.sem("spread")
        args = s.sem("args")
        inner = s.sem("inner")
        exps = s.sem("exps")
        msgs = s.sem("msgs")
        summed = s.sem("summed")
        added = s.sem("added")
        zeroed, go = s.sem("zeroed"), s.sem("go")
        per_half = 2 if table is not None else 1
        with s.block() as block:
            @block.scalar
            def _(act):
                act.sem_inc(kept, HALF)
                act.sem_inc(exps, HALF)

                def stage(i, h):
                    act.wait_ge(onehots, U * i + HALF * (h + 1))
                    src = rec[:, bass.ds((i * U + h * HALF) * FIELDS, HALF * FIELDS)]
                    if table is not None:
                        for u in range(HALF):
                            act.wait_ge(landed[HALF * h + u], 16 * i)
                        nc.scalar.copy(idx_s[h][:], src.rearrange("p (u f) -> p u f", f=FIELDS)[:, :, 0]).then_inc(staged[h], 1)
                    nc.scalar.copy(rec_s[h][:], src).then_inc(staged[h], 1)

                def keep(i, u):
                    act.wait_ge(turned, HALF + U * i + u + 1)
                    act.wait_ge(spread, U * i + u + 1)
                    nc.scalar.copy(oht[u % HALF][:], ps_t[u % 2][:, 0:EC]).then_inc(kept, 1)

                def body(i, last):
                    for u in range(U):
                        nxt = ahead(i, u, 2, last)
                        if nxt:
                            keep(*nxt)
                        act.wait_ge(args, HALF + U * i + u + 1)
                        act.wait_ge(summed, U * i + u + 5)
                        nc.scalar.activation(msg[u % HALF][:, vw:wide], arg[u % HALF][:], ACT.Exp).then_inc(exps, 1)
                        if u % HALF == HALF - 1 and not last:
                            stage(i + 1, u // HALF)
                edge_loop(act, chunks, body, lambda: ([stage(0, h) for h in range(2)], [keep(0, u) for u in range(2)]))

            if table is not None:
                @block.gpsimd
                def _(pool):
                    gather_rows(nc, pool, chunks, table, idx_s, [r[:] for r in rows], staged, msgs, landed, go)

            @block.vector
            def _(dve):
                dve.sem_inc(onehots, U)
                dve.sem_inc(args, HALF)
                dve.sem_inc(msgs, U)
                dve.sem_inc(added, HALF)
                nc.vector.memset(acc[:], 0.0).then_inc(zeroed, 1)
                dve.wait_ge(zeroed, 1)

                def make(i, u):
                    if u % HALF == 0:
                        dve.wait_ge(staged[u // HALF], per_half * (i + 1))
                    dve.wait_ge(summed, U * i + u + 1)
                    one_hot(nc, c, dve, oh[u], rec_s, u).then_inc(onehots, 1)

                def argue(i, u):
                    n = U * i + u
                    dve.wait_ge(spread, HALF + n + 1)
                    dve.wait_ge(exps, n + 1)
                    if not leaky:
                        nc.vector.tensor_tensor(arg[u % HALF][:], scores[:, bass.ds(n * heads, heads)],
                                                ps_n[u % 2][:, pn - heads:pn], ALU.subtract).then_inc(args, 1)
                        return
                    a = arg2[u % HALF]
                    w = arg[u % HALF]
                    nc.vector.tensor_tensor(a[:], stored[:, bass.ds(n * wide + vw, heads)], ps_n[u % 2][:, 0:heads],
                                            ALU.add).then_inc(inner, 1)
                    dve.wait_ge(inner, 3 * n + 1)
                    nc.vector.scalar_tensor_tensor(w[:], a[:], 0.2, a[:], ALU.mult, ALU.max).then_inc(inner, 1)
                    dve.wait_ge(inner, 3 * n + 2)
                    nc.vector.tensor_tensor(a[:], w[:], ps_n[u % 2][:, heads:2 * heads], ALU.subtract).then_inc(inner, 1)
                    dve.wait_ge(inner, 3 * n + 3)
                    nc.vector.tensor_scalar(w[:], a[:], 0.0, None, ALU.min).then_inc(args, 1)

                def body(i, last):
                    for u in range(U):
                        n = U * i + u
                        nxt = ahead(i, u, 3, last)
                        if nxt:
                            make(*nxt)
                        nxt = ahead(i, u, 1, last)
                        if nxt:
                            argue(*nxt)
                        dve.wait_ge(exps, HALF + n + 1)
                        if table is not None:
                            dve.wait_ge(landed[u], 16 * i + 16)
                            vals = rows[u][:]
                        else:
                            vals = stored[:, bass.ds(n * wide, vw)]
                        w = msg[u % HALF][:, vw:wide].unsqueeze(2).broadcast_to([EC, heads, hd])
                        nc.vector.tensor_tensor(msg[u % HALF][:, 0:vw].rearrange("p (h d) -> p h d", h=heads),
                                                vals.rearrange("p (h d) -> p h d", h=heads), w, ALU.mult).then_inc(msgs, 1)
                        if u > 0:
                            add(i, u - 1)
                    add(i, U - 1)

                def add(i, u):
                    n = U * i + u
                    b = dve.value_load(blk[0:1, bass.ds(n, 1)], min_val=0, max_val=T - 1)
                    dve.wait_ge(summed, U + n + 1)
                    dve.wait_ge(added, HALF + n)
                    to = acc[:, bass.ds(b * wide, wide)]
                    nc.vector.tensor_tensor(to, to, ps_a[u % 4][:, 0:wide], ALU.add).then_inc(added, 1)

                edge_loop(dve, chunks, body, lambda: ([make(0, u) for u in range(3)], argue(0, 0)))

            @block.tensor
            def _(pe):
                pe.sem_inc(turned, HALF)
                pe.sem_inc(spread, HALF)
                pe.sem_inc(summed, U)

                def turn(i, u):
                    pe.wait_ge(onehots, U + U * i + u + 1)
                    pe.wait_ge(kept, U * i + u + 3)
                    nc.tensor.transpose(ps_t[u % 2][:, 0:EC], oh[u][:, 0:P], c["ident"][:]).then_inc(turned, 1)

                def node_rows(i, u):
                    n = U * i + u
                    b = pe.value_load(blk[0:1, bass.ds(n, 1)], min_val=0, max_val=T - 1)
                    pe.wait_ge(kept, HALF + n + 1)
                    pe.wait_ge(args, n + 3)
                    nc.tensor.matmul(ps_n[u % 2][:, 0:pn], oht[u % HALF][:], per_node[:, bass.ds(b * pn, pn)],
                                     start=True, stop=True).then_inc(spread, 1)

                def body(i, last):
                    for u in range(U):
                        n = U * i + u
                        nxt = ahead(i, u, 2, last)
                        if nxt:
                            turn(*nxt)
                        nxt = ahead(i, u, 1, last)
                        if nxt:
                            node_rows(*nxt)
                        pe.wait_ge(msgs, U + n + 1)
                        pe.wait_ge(added, n + 1)
                        nc.tensor.matmul(ps_a[u % 4][:, 0:wide], oh[u][:, 0:P], msg[u % HALF][:],
                                         start=True, stop=True).then_inc(summed, 1)
                edge_loop(pe, chunks, body, lambda: ([turn(0, u) for u in range(2)], node_rows(0, 0)))


def gather_all(nc, c, name, table, width, rec, chunks, stored):
    with Stage(nc, name) as s:
        idx_s = [s.sb(f"idx_s{h}", [EC, HALF], I32) for h in range(2)]
        rows = [s.sb(f"rows{u}", [EC, width]) for u in range(U)]
        staged = [s.sem(f"staged{h}") for h in range(2)]
        landed = [s.sem(f"landed{u}") for u in range(U)]
        used, go = s.sem("used"), s.sem("go")
        with s.block() as block:
            @block.scalar
            def _(act):
                def body(i, last):
                    for h in range(2):
                        for u in range(HALF):
                            act.wait_ge(landed[HALF * h + u], 16 * i)
                        src = rec[:, bass.ds((i * U + h * HALF) * FIELDS, HALF * FIELDS)]
                        nc.scalar.copy(idx_s[h][:], src.rearrange("p (u f) -> p u f", f=FIELDS)[:, :, 0]).then_inc(staged[h], 2)
                edge_loop(act, chunks, body)

            @block.gpsimd
            def _(pool):
                gather_rows(nc, pool, chunks, table, idx_s, [r[:] for r in rows], staged, used, landed, go)

            @block.vector
            def _(dve):
                dve.sem_inc(used, U)

                def body(i, last):
                    for u in range(U):
                        dve.wait_ge(landed[u], 16 * i + 16)
                        nc.vector.tensor_copy(stored[:, bass.ds((i * U + u) * width, width)], rows[u][:]).then_inc(used, 1)
                edge_loop(dve, chunks, body)



def tiles_loop(eng, body):
    with eng.Fori(0, T // RING) as i:
        for u in range(RING):
            body(i * RING + u, u)


def layernorm(nc, name, src, dst, gamma=None, beta=None):
    with Stage(nc, name) as s:
        stats = s.sb("stats", [P, T * 6])
        mv = s.sb("mv", [P, T * 2])
        var = s.sb("var", [P, T])
        std = s.sb("std", [P, T])
        rstd = s.sb("rstd", [P, T])
        gb = s.sb("gb", [P, 2 * D]) if gamma is not None else None
        loaded, steps, eps_added, rooted = s.sem("loaded"), s.sem("steps"), s.sem("eps_added"), s.sem("rooted")
        with s.block() as block:
            if gamma is not None:
                @block.sync
                def _(sp):
                    sp.dma_start(gb[:, 0:D], gamma.partition_broadcast(P)).then_inc(loaded, 16)
                    sp.dma_start(gb[:, D:2 * D], beta.partition_broadcast(P)).then_inc(loaded, 16)

            @block.scalar
            def _(act):
                act.wait_ge(eps_added, 1)
                nc.scalar.activation(std[:], var[:], ACT.Sqrt).then_inc(rooted, 1)

            @block.vector
            def _(dve):
                step = Steps(dve, steps)
                tiles_loop(dve, lambda t, u: nc.vector.bn_stats(stats[:, tile_of(t, 6)], src[:, tile_of(t, D)]
                                                                ).then_inc(steps, 1))
                step.n = T
                dve.wait_ge(steps, T)
                for t in range(T):
                    nc.vector.bn_aggr(mv[:, 2 * t:2 * t + 2], stats[:, 6 * t:6 * t + 6]).then_inc(steps, 1)
                step.n = 2 * T
                dve.wait_ge(steps, 2 * T)
                mv2 = mv[:].rearrange("p (t k) -> p t k", k=2)
                nc.vector.tensor_scalar(var[:], mv2[:, :, 1], EPS, None, ALU.add).then_inc(eps_added, 1)
                dve.wait_ge(rooted, 1)
                step(nc.vector.reciprocal(rstd[:], std[:]))
                tiles_loop(dve, lambda t, u: nc.vector.tensor_scalar(
                    dst[:, tile_of(t, D)], src[:, tile_of(t, D)], mv[:, bass.ds(2 * t, 1)], rstd[:, bass.ds(t, 1)],
                    ALU.subtract, ALU.mult).then_inc(steps, 1))
                step.n += T
                dve.wait_ge(steps, step.n)
                if gamma is not None:
                    dve.wait_ge(loaded, 32)
                    full = as_tiles(dst, D)
                    step(nc.vector.tensor_tensor(full, full, gb[:, 0:D].unsqueeze(1).broadcast_to([P, T, D]), ALU.mult))
                    step(nc.vector.tensor_tensor(full, full, gb[:, D:2 * D].unsqueeze(1).broadcast_to([P, T, D]), ALU.add))


def turn_tiles(nc, c, name, src, width, dst, stride=None, scale=None):
    stride = stride or width
    cw = min(width, 128)
    nch = width // cw
    with Stage(nc, name) as s:
        tile = [s.sb(f"tile{u}", [P, width]) for u in range(RING)]
        ps = [s.ps(f"ps{u}", [cw, nch * P]) for u in range(RING)]
        copied = s.sem("copied")
        turned = s.sem("turned")
        stored = s.sem("stored")
        go = s.sem("go")
        with s.block() as block:
            @block.scalar
            def _(act):
                def body(t, u):
                    act.wait_ge(turned, t + 1)
                    nc.scalar.copy(tile[u][:], src[:, bass.ds(t * stride, width)]).then_inc(copied, 1)
                tiles_loop(act, body)

            @block.tensor
            def _(pe):
                pe.sem_inc(turned, RING)

                def body(t, u):
                    pe.wait_ge(copied, t + 1)
                    pe.wait_ge(stored, t + 1)
                    pe.sem_inc(go, 1)
                    for k in range(nch):
                        ins = nc.tensor.transpose(ps[u][:, k * P:(k + 1) * P], tile[u][:, k * cw:(k + 1) * cw],
                                                  c["ident"][0:P, 0:P])
                    ins.then_inc(turned, 1)
                tiles_loop(pe, body)

            @block.vector
            def _(dve):
                dve.sem_inc(stored, RING)

                def body(t, u):
                    dve.wait_ge(turned, RING + t + 1)
                    for k in range(nch):
                        ins = nc.vector.tensor_copy(dst[0:cw, bass.ds(t * P + k * N, P)], ps[u][:, k * P:(k + 1) * P])
                    ins.then_inc(stored, 1)
                tiles_loop(dve, body)


def project(nc, c, name, sources, wide, mode, dst, bias=None, scale=None, stride=None):
    stride = stride or wide
    with Stage(nc, name) as s:
        w = [s.sb(f"w{k}", [kp, wide]) for k, (_, kp, _, _) in enumerate(sources)]
        lhs = [s.sb(f"lhs{u}", [128, len(sources) * P]) for u in range(RING)]
        brow = s.sb("brow", [1, wide]) if bias is not None else None
        ps = [s.ps(f"ps{u}", [P, 512]) for u in range(RING)]
        loaded = s.sem("loaded")
        copied = s.sem("copied")
        multiplied = s.sem("multiplied")
        stored = s.sem("stored")
        with s.block() as block:
            @block.sync
            def _(sp):
                for k, (_, _, _, wd) in enumerate(sources):
                    sp.dma_start(w[k][:], wd).then_inc(loaded, 16)
                if bias is not None:
                    sp.dma_start(brow[:], bias).then_inc(loaded, 16)

            @block.scalar
            def _(act):
                def body(t, u):
                    act.wait_ge(multiplied, t + 1)
                    for k, (src, kp, ch, _) in enumerate(sources):
                        nc.scalar.copy(lhs[u][0:kp, k * P:(k + 1) * P], src[0:kp, bass.ds(t * P + ch * N, P)]).then_inc(copied, 1)
                tiles_loop(act, body)

            @block.tensor
            def _(pe):
                pe.sem_inc(multiplied, RING)
                pe.wait_ge(loaded, 16 * (len(sources) + (bias is not None)))

                def body(t, u):
                    pe.wait_ge(copied, (t + 1) * len(sources))
                    pe.wait_ge(stored, t + 1)
                    if bias is not None:
                        nc.tensor.matmul(ps[u][:, 0:wide], c["ones"][0:1, 0:P], brow[:], start=True, stop=False)
                    for k, (_, kp, _, _) in enumerate(sources):
                        ins = nc.tensor.matmul(ps[u][:, 0:wide], lhs[u][0:kp, k * P:(k + 1) * P], w[k][:],
                                               start=(k == 0 and bias is None), stop=(k == len(sources) - 1))
                    ins.then_inc(multiplied, 1)
                tiles_loop(pe, body)

            @block.vector
            def _(dve):
                dve.sem_inc(stored, RING)

                def body(t, u):
                    dve.wait_ge(multiplied, RING + t + 1)
                    out = ps[u][:, 0:wide]
                    to = dst[:, bass.ds(t * stride, wide)]
                    if mode == "copy":
                        ins = nc.vector.tensor_copy(to, out)
                    elif mode == "scale":
                        ins = nc.vector.tensor_scalar(to, out, scale[:, bass.ds(t, 1)], None, ALU.mult)
                    elif mode == "add":
                        ins = nc.vector.tensor_tensor(to, to, out, ALU.add)
                    elif mode == "relu_add":
                        ins = nc.vector.scalar_tensor_tensor(to, out, 0.0, to, ALU.max, ALU.add)
                    ins.then_inc(stored, 1)
                tiles_loop(dve, body)



def network(nc, c, name, xt, experts, hidden, act_fn, w1_d, b1_d, w2_d, b2_d, gate, acc):
    fc = hidden // 128
    jh = fc // 2
    twin = min(experts, 2)
    steps_per = T // RING
    PRIME = 4 * steps_per
    with Stage(nc, name) as s:
        w1 = [s.sb(f"w1_{e}", [128, DC * hidden]) for e in range(twin)]
        w2 = [s.sb(f"w2_{e}", [128, fc * D]) for e in range(twin)]
        b1 = s.sb("b1", [128, experts * fc])
        b2 = s.sb("b2", [experts, D])
        gt = s.sb("gt", [experts, RING * P]) if gate is not None else None
        gs = [s.sb(f"gs{u}", [P, experts]) for u in range(RING)] if gate is not None else None
        h = [s.sb(f"h{q}", [128, jh * GROUP]) for q in range(2)]
        ps_h = [s.ps(f"ps_h{r}", [128, 1024]) for r in range(2)]
        ps_y = s.ps("ps_y", [P, 3 * 512])
        w_in = [s.sem(f"w_in{e}") for e in range(twin)]
        small = s.sem("small")
        hidden_ready = s.sem("hidden_ready")
        activated = s.sem("activated")
        multiplied = s.sem("multiplied")
        summed = s.sem("summed")
        go, g_copied, g_turned, g_kept, biased, bias_kept = (s.sem(n) for n in (
            "go", "g_copied", "g_turned", "g_kept", "biased", "bias_kept"))

        def ycols(k):
            return ps_y[:, (k // 2) * 512 + (k % 2) * D:(k // 2) * 512 + (k % 2) * D + D]

        with s.block() as block:
            @block.sync
            def _(sp):
                sp.dma_start(b1[:], b1_d).then_inc(small, 16)
                sp.dma_start(b2[:], b2_d).then_inc(small, 16)
                with sp.Fori(0, experts // twin) as eo:
                    for e in range(twin):
                        ex = eo * twin + e
                        sp.wait_ge(multiplied, 2 * steps_per * (ex + 1))
                        sp.dma_start(w1[e][:], w1_d[bass.ds(ex, 1), :, :].rearrange("e p f -> (e p) f")).then_inc(w_in[e], 16)
                        sp.dma_start(w2[e][:], w2_d[bass.ds(ex, 1), :, :].rearrange("e p f -> (e p) f")).then_inc(w_in[e], 16)

            @block.scalar
            def _(act):
                act.sem_inc(activated, 2)
                act.wait_ge(small, 32)
                if gate is not None:
                    def copy_gate(t, u):
                        act.wait_ge(g_turned, t + 1)
                        nc.scalar.copy(gs[u][:], gate[0:P, bass.ds(t * experts, experts)]).then_inc(g_copied, 1)
                    tiles_loop(act, copy_gate)
                with act.Fori(0, experts // twin) as eo:
                    for e in range(twin):
                        ex = eo * twin + e
                        with act.Fori(0, steps_per) as g:
                            st = ex * steps_per + g
                            for q in range(2):
                                act.wait_ge(multiplied, PRIME + 2 * st + q - 1)
                                for j in range(jh):
                                    act.wait_ge(hidden_ready, 2 * jh * st + q * jh + j + 1)
                                    for m, (m0, mn) in enumerate(PIECES):
                                        ins = nc.scalar.activation(
                                            h[q][:, j * GROUP + m0:j * GROUP + m0 + mn],
                                            ps_h[j % 2][:, 512 * m:512 * m + mn], act_fn,
                                            bias=b1[:, bass.ds(ex * fc + q * jh + j, 1)])
                                    ins.then_inc(activated, 1)

            @block.tensor
            def _(pe):
                pe.sem_inc(multiplied, PRIME)
                pe.wait_ge(small, 32)
                if gate is not None:
                    pe.sem_inc(g_turned, RING)

                    def bias_part(t, u):
                        pe.wait_ge(g_copied, t + 1)
                        pe.wait_ge(bias_kept, t)
                        nc.tensor.transpose(ps_h[0][0:experts, 0:P], gs[u][:], c["ident"][0:P, 0:P]).then_inc(g_turned, 1)
                        pe.wait_ge(g_kept, t + 1)
                        nc.tensor.matmul(ps_h[1][0:P, 0:D], gt[:, u * P:(u + 1) * P], b2[:], start=True, stop=True).then_inc(biased, 1)
                    tiles_loop(pe, bias_part)
                    pe.wait_ge(bias_kept, T)
                with pe.Fori(0, experts // twin) as eo:
                    for e in range(twin):
                        ex = eo * twin + e
                        pe.wait_ge(w_in[e], 32 * (eo + 1))
                        pe.sem_inc(go, 1)
                        with pe.Fori(0, steps_per) as g:
                            st = ex * steps_per + g
                            for q in range(2):
                                for j in range(jh):
                                    pe.wait_ge(activated, 2 * jh * st + q * jh + j + 1)
                                    f0 = (q * jh + j) * 128
                                    for m, (m0, mn) in enumerate(PIECES):
                                        for k in range(DC):
                                            ins = nc.tensor.matmul(
                                                ps_h[j % 2][:, 512 * m:512 * m + mn],
                                                w1[e][:, k * hidden + f0:k * hidden + f0 + 128],
                                                xt[:, bass.ds(g * GROUP + (k * N + m0), mn)],
                                                start=(k == 0), stop=(k == DC - 1))
                                    ins.then_inc(hidden_ready, 1)
                            for q in range(2):
                                pe.wait_ge(activated, 2 + 2 * jh * st + (q + 1) * jh)
                                if q == 0:
                                    pe.wait_ge(summed, st + 1)
                                for k in range(RING):
                                    for j in range(jh):
                                        ins = nc.tensor.matmul(
                                            ycols(k), h[q][:, j * GROUP + k * P:j * GROUP + (k + 1) * P],
                                            w2[e][:, (q * jh + j) * D:(q * jh + j + 1) * D],
                                            start=(q == 0 and j == 0 and k % 2 == 0), stop=(q == 1 and j == jh - 1),
                                            skip_group_check=True)
                                ins.then_inc(multiplied, 1)

            @block.vector
            def _(dve):
                dve.sem_inc(summed, 1)
                dve.wait_ge(small, 32)
                if gate is not None:
                    def keep_bias(t, u):
                        dve.wait_ge(g_turned, RING + t + 1)
                        nc.vector.tensor_copy(gt[:, u * P:(u + 1) * P], ps_h[0][0:experts, 0:P]).then_inc(g_kept, 1)
                        dve.wait_ge(biased, t + 1)
                        nc.vector.tensor_copy(acc[:, tile_of(t, D)], ps_h[1][0:P, 0:D]).then_inc(bias_kept, 1)
                    tiles_loop(dve, keep_bias)
                    dve.wait_ge(bias_kept, T)
                with dve.Fori(0, experts) as ex:
                    with dve.Fori(0, steps_per) as g:
                        st = ex * steps_per + g
                        dve.wait_ge(multiplied, PRIME + 2 * st + 2)
                        dve.wait_ge(summed, st + 1)
                        for k in range(RING):
                            to = acc[:, bass.ds(g * (RING * D) + k * D, D)]
                            if gate is None:
                                ins = nc.vector.tensor_copy(to, ycols(k))
                            else:
                                ins = nc.vector.scalar_tensor_tensor(
                                    to, ycols(k), gate[0:P, bass.ds(g * (RING * experts) + k * experts + ex, 1)], to,
                                    ALU.mult, ALU.add)
                        ins.then_inc(summed, 1)



def first_of(nc, step, eq, out, seen, experts):
    step(nc.vector.memset(seen[:], 0.0))
    for e in range(experts):
        step(nc.vector.tensor_tensor(out[:, :, e], eq[:, :, e], seen[:], ALU.is_gt))
        step(nc.vector.tensor_tensor(seen[:], seen[:], eq[:, :, e], ALU.max))


def top_two(nc, c, name, scores, n, experts, gate, replicate=None):
    with Stage(nc, name) as s:
        eq = s.sb("eq", [P, n * experts])
        one = s.sb("one", [P, n * experts])
        two = s.sb("two", [P, n * experts])
        rest = s.sb("rest", [P, n * experts])
        seen, m1, m2, gap, ex, den, w1, w2 = (s.sb(k, [P, n]) for k in ("seen", "m1", "m2", "gap", "ex", "den", "w1", "w2"))
        steps, exps = s.sem("steps"), s.sem("exps")
        gap_ready = s.sem("gap_ready")

        def view(x):
            return x[:, 0:n * experts].rearrange("p (t e) -> p t e", e=experts)

        def wide(x):
            return x[:].unsqueeze(2).broadcast_to([P, n, experts])

        with s.block() as block:
            @block.scalar
            def _(act):
                act.wait_ge(gap_ready, 1)
                nc.scalar.activation(ex[:], gap[:], ACT.Exp).then_inc(exps, 1)

            @block.vector
            def _(dve):
                step = Steps(dve, steps)
                V = nc.vector
                sc = view(scores)
                step(V.tensor_reduce(m1[:], sc, AX.X, ALU.max))
                step(V.tensor_tensor(view(eq), sc, wide(m1), ALU.is_equal))
                first_of(nc, step, view(eq), view(one), seen, experts)
                step(V.scalar_tensor_tensor(rest[:], one[:], -3e38, scores[:, 0:n * experts], ALU.mult, ALU.add))
                step(V.tensor_reduce(m2[:], view(rest), AX.X, ALU.max))
                step(V.tensor_tensor(view(eq), view(rest), wide(m2), ALU.is_equal))
                first_of(nc, step, view(eq), view(two), seen, experts)
                V.tensor_tensor(gap[:], m2[:], m1[:], ALU.subtract).then_inc(gap_ready, 1)
                dve.wait_ge(exps, 1)
                step(V.tensor_scalar(den[:], ex[:], 1.0, None, ALU.add))
                step(V.reciprocal(w1[:], den[:]))
                step(V.tensor_tensor(w2[:], ex[:], w1[:], ALU.mult))
                step(V.tensor_tensor(view(one), view(one), wide(w1), ALU.mult))
                step(V.tensor_tensor(view(two), view(two), wide(w2), ALU.mult))
                if replicate is None:
                    step(V.tensor_tensor(gate[:], one[:], two[:], ALU.add))
                else:
                    step(V.tensor_tensor(one[:], one[:], two[:], ALU.add))
                    step(V.tensor_copy(gate[:].rearrange("p (t e) -> p t e", e=experts),
                                       one[:].unsqueeze(1).broadcast_to([P, replicate, experts])))


def top_one(nc, c, name, logits, experts, capacity, gate):
    with Stage(nc, name) as s:
        n = T
        big = [P, n * experts]
        shift, ex, probs, eq, one, inside, totals, before, pos, kept = (s.sb(k, big) for k in (
            "shift", "ex", "probs", "eq", "one", "inside", "totals", "before", "pos", "kept"))
        mx, tot, inv, pm, seen, zeros = (s.sb(k, [P, n]) for k in ("mx", "tot", "inv", "pm", "seen", "zeros"))
        upto = s.sb("upto", [P, P])
        ps = [s.ps(f"ps{k}", [P, 512]) for k in range(2)]
        steps, exps, shifted, counted, hot, made = (s.sem(k) for k in ("steps", "exps", "shifted", "counted", "hot", "made"))

        def view(x):
            return x[:].rearrange("p (t e) -> p t e", e=experts)

        def wide(x):
            return x[:].unsqueeze(2).broadcast_to([P, n, experts])

        with s.block() as block:
            @block.gpsimd
            def _(pool):
                nc.gpsimd.memset(upto[:], 1.0).then_inc(made, 1)
                pool.wait_ge(made, 1)
                nc.gpsimd.affine_select(out=upto[:], in_=upto[:], compare_op=ALU.is_ge, fill=0.0, base=0,
                                        pattern=[[1, P]], channel_multiplier=-1).then_inc(made, 1)

            @block.scalar
            def _(act):
                act.wait_ge(shifted, 1)
                nc.scalar.activation(ex[:], shift[:], ACT.Exp).then_inc(exps, 1)

            @block.tensor
            def _(pe):
                pe.wait_ge(made, 2)
                pe.wait_ge(hot, 1)
                nc.tensor.matmul(ps[0][:, 0:n * experts], upto[:], one[:], start=True, stop=True).then_inc(counted, 1)
                nc.tensor.matmul(ps[1][:, 0:n * experts], c["ones"][0:P, 0:P], one[:], start=True, stop=True).then_inc(counted, 1)

            @block.vector
            def _(dve):
                step = Steps(dve, steps)
                V = nc.vector
                step(V.tensor_reduce(mx[:], view(logits), AX.X, ALU.max))
                V.tensor_tensor(view(shift), view(logits), wide(mx), ALU.subtract).then_inc(shifted, 1)
                dve.wait_ge(exps, 1)
                step(V.tensor_reduce(tot[:], view(ex), AX.X, ALU.add))
                step(V.reciprocal(inv[:], tot[:]))
                step(V.tensor_tensor(view(probs), view(ex), wide(inv), ALU.mult))
                step(V.tensor_reduce(pm[:], view(probs), AX.X, ALU.max))
                step(V.tensor_tensor(view(eq), view(probs), wide(pm), ALU.is_equal))
                first_of(nc, step, view(eq), view(one), seen, experts)
                step(V.memset(zeros[:], 0.0))
                dve.sem_inc(hot, 1)
                dve.wait_ge(counted, 2)
                step(V.tensor_copy(inside[:], ps[0][:, 0:n * experts]))
                step(V.tensor_copy(totals[:], ps[1][:, 0:n * experts]))
                for e in range(experts):
                    step(V.tensor_tensor_scan(view(before)[:, :, e], zeros[:], view(totals)[:, :, e], 0.0, ALU.add, ALU.add))
                step(V.tensor_tensor(pos[:], before[:], totals[:], ALU.subtract))
                step(V.tensor_tensor(pos[:], pos[:], inside[:], ALU.add))
                step(V.scalar_tensor_tensor(kept[:], pos[:], float(capacity), one[:], ALU.is_le, ALU.mult))
                step(V.tensor_tensor(view(gate), view(kept), wide(pm), ALU.mult))


def finite(nc, name, y):
    top = 3.4028234663852886e38
    w = RING * D
    with Stage(nc, name) as s:
        mask, low, nan = (s.sb(k, [P, w], I32) for k in ("mask", "low", "nan"))
        fill = s.sb("fill", [P, 3])
        steps = s.sem("steps")

        def filled(k):
            return fill[:, k:k + 1].broadcast_to([P, w])

        with s.block() as block:
            @block.vector
            def _(dve):
                step = Steps(dve, steps)
                V = nc.vector
                for k, v in enumerate((1e4, -1e4, 0.0)):
                    step(V.memset(fill[:, k:k + 1], v))
                for g in range(T // RING):
                    yt = y[:, g * w:(g + 1) * w]
                    step(V.tensor_scalar(mask[:], yt, top, None, ALU.is_gt))
                    step(V.tensor_scalar(low[:], yt, -top, None, ALU.is_lt))
                    step(V.tensor_tensor(nan[:], yt, yt, ALU.not_equal))
                    step(V.copy_predicated(yt, mask[:], filled(0)))
                    step(V.copy_predicated(yt, low[:], filled(1)))
                    step(V.copy_predicated(yt, nan[:], filled(2)))


def global_scores(nc, c, name, yt_feat, wr_d, br_d, experts, capacity, scores):
    with Stage(nc, name) as s:
        wr = s.sb("wr", [128, DC * experts])
        br = s.sb("br", [P, experts])
        tot = s.sb("tot", [128, DC])
        mean = s.sb("mean", [128, DC * P])
        lg, ex, rw, load, scale, low, a2, ex2 = (s.sb(k, [P, experts]) for k in ("lg", "ex", "rw", "load", "scale", "low", "a2", "ex2"))
        mx, sm, inv = (s.sb(k, [P, 1]) for k in ("mx", "sm", "inv"))
        ps = s.ps("ps", [P, 512])
        loaded, steps, averaged, routed, asked, exps = (s.sem(k) for k in ("loaded", "steps", "averaged", "routed", "asked", "exps"))
        with s.block() as block:
            @block.sync
            def _(sp):
                sp.dma_start(wr[:], wr_d).then_inc(loaded, 16)
                sp.dma_start(br[:], br_d.partition_broadcast(P)).then_inc(loaded, 16)

            @block.scalar
            def _(act):
                act.wait_ge(asked, 1)
                nc.scalar.activation(ex[:], lg[:], ACT.Exp).then_inc(exps, 1)
                act.wait_ge(asked, 2)
                nc.scalar.activation(ex2[:], a2[:], ACT.Exp).then_inc(exps, 1)

            @block.tensor
            def _(pe):
                pe.wait_ge(loaded, 32)
                pe.wait_ge(averaged, 1)
                for k in range(DC):
                    ins = nc.tensor.matmul(ps[:, 0:experts], mean[:, k * P:(k + 1) * P], wr[:, k * experts:(k + 1) * experts],
                                           start=(k == 0), stop=(k == DC - 1))
                ins.then_inc(routed, 1)

            @block.vector
            def _(dve):
                step = Steps(dve, steps)
                V = nc.vector
                step(V.tensor_reduce(tot[:], yt_feat[:].rearrange("p (k n) -> p k n", k=DC), AX.X, ALU.add))
                V.tensor_scalar(mean[:].rearrange("p (k m) -> p k m", k=DC),
                                tot[:].unsqueeze(2).broadcast_to([128, DC, P]), 1.0 / N, None, ALU.mult).then_inc(averaged, 1)
                dve.wait_ge(loaded, 32)
                dve.wait_ge(routed, 1)
                step(V.tensor_tensor(lg[:], ps[:, 0:experts], br[:], ALU.add))
                step(V.tensor_reduce(mx[:], lg[:], AX.X, ALU.max))
                step(V.tensor_scalar(lg[:], lg[:], mx[:, 0:1], None, ALU.subtract))
                dve.sem_inc(asked, 1)
                dve.wait_ge(exps, 1)
                step(V.tensor_reduce(sm[:], ex[:], AX.X, ALU.add))
                step(V.reciprocal(inv[:], sm[:]))
                step(V.tensor_scalar(rw[:], ex[:], inv[:, 0:1], None, ALU.mult))
                step(V.tensor_scalar(load[:], rw[:], float(N), float(capacity), ALU.mult, ALU.max))
                step(V.reciprocal(scale[:], load[:]))
                step(V.tensor_scalar(scale[:], scale[:], float(capacity), None, ALU.mult))
                step(V.tensor_scalar(low[:], load[:], float(capacity), None, ALU.is_le))
                step(V.tensor_tensor(scale[:], scale[:], low[:], ALU.max))
                step(V.tensor_tensor(a2[:], rw[:], scale[:], ALU.mult))
                step(V.tensor_reduce(mx[:], a2[:], AX.X, ALU.max))
                step(V.tensor_scalar(a2[:], a2[:], mx[:, 0:1], None, ALU.subtract))
                dve.sem_inc(asked, 1)
                dve.wait_ge(exps, 2)
                step(V.tensor_reduce(sm[:], ex2[:], AX.X, ALU.add))
                step(V.reciprocal(inv[:], sm[:]))
                step(V.tensor_scalar(scores[:], ex2[:], inv[:, 0:1], None, ALU.mult))



def vector_steps(nc, name, fn):
    with Stage(nc, name) as s:
        steps = s.sem("steps")
        with s.block() as block:
            @block.vector
            def _(dve):
                fn(Steps(dve, steps), nc.vector)


def root(nc, name, x, out):
    with Stage(nc, name) as s:
        r = s.sb("r", list(x.shape))
        rooted, inverted = s.sem("rooted"), s.sem("inverted")
        with s.block() as block:
            @block.scalar
            def _(act):
                nc.scalar.activation(r[:], x[:], ACT.Sqrt).then_inc(rooted, 1)

            @block.vector
            def _(dve):
                dve.wait_ge(rooted, 1)
                nc.vector.reciprocal(out[:], r[:]).then_inc(inverted, 1)


def batch_norm_relu(nc, name, xt, ch, bias_d, gamma_d, beta_d):
    with Stage(nc, name) as s:
        col = s.sb("col", [ch, 3])
        stats = s.sb("stats", [ch, T * 6])
        mv = s.sb("mv", [ch, 2])
        var, std, rstd = (s.sb(k, [ch, 1]) for k in ("var", "std", "rstd"))
        loaded, steps, ready, rooted, normed, done = (s.sem(k) for k in ("loaded", "steps", "ready", "rooted", "normed", "done"))
        with s.block() as block:
            @block.sync
            def _(sp):
                for k, v in enumerate((bias_d, gamma_d, beta_d)):
                    sp.dma_start(col[:, k:k + 1], v).then_inc(loaded, 16)

            @block.scalar
            def _(act):
                act.wait_ge(ready, 1)
                nc.scalar.activation(std[:], var[:], ACT.Sqrt).then_inc(rooted, 1)
                act.wait_ge(normed, 1)
                nc.scalar.activation(xt[:], xt[:], ACT.Relu, bias=col[:, 2:3], scale=col[:, 1:2]).then_inc(done, 1)

            @block.vector
            def _(dve):
                step = Steps(dve, steps)
                dve.wait_ge(loaded, 48)
                step(nc.vector.tensor_scalar(xt[:], xt[:], col[:, 0:1], None, ALU.add))
                tiles_loop(dve, lambda t, u: nc.vector.bn_stats(stats[:, tile_of(t, 6)], xt[:, tile_of(t, P)]).then_inc(steps, 1))
                step.n += T
                dve.wait_ge(steps, step.n)
                step(nc.vector.bn_aggr(mv[:], stats[:]))
                nc.vector.tensor_scalar(var[:], mv[:, 1:2], EPS, None, ALU.add).then_inc(ready, 1)
                dve.wait_ge(rooted, 1)
                step(nc.vector.reciprocal(rstd[:], std[:]))
                nc.vector.tensor_scalar(xt[:], xt[:], mv[:, 0:1], rstd[:, 0:1], ALU.subtract, ALU.mult).then_inc(normed, 1)
                dve.wait_ge(normed, 1)



def model(nc, I, out, probes=None):
    E0 = 53125
    E3 = 32768
    CH0, CH3 = chunk_bound(E0), chunk_bound(E3)
    heads, hd = 8, 32
    gh, ge = 4, 4
    capacity = -(-N * 5 // (4 * 8))

    def dram(name, shape):
        return nc.dram_tensor(name, shape, F32, kind="Internal").ap()

    with Stage(nc, "model") as m:
        x = m.sb("x", [P, T * D])
        c = {"ident": m.sb("ident", [128, 128]), "iota": m.sb("iota", [128, 128]), "ones": m.sb("ones", [128, 128])}
        count = m.sb("count", [P, T])
        inv2 = m.sb("inv2", [P, T])
        inv3 = m.sb("inv3", [P, T])

        def chunks_of(w):
            wide = w.shape[1] // DC
            return [w[:, k * wide:(k + 1) * wide] for k in range(DC)]

        def from_features(t, w):
            return [(t, 128, k, wk) for k, wk in enumerate(chunks_of(w))]

        def probe(k):
            if probes is not None and k in probes:
                transfer(nc, "probe", [(by_tile(probes[k], D), as_tiles(x, D))])

        constants(nc, c, I)
        transfer(nc, "load_x", [(as_tiles(x, D), by_tile(I["x"], D))])

        with Stage(nc, "graph") as g:
            rec_d, blk_d = g.sb("rec_d", [128, CH0 * FIELDS]), g.sb("blk_d", [1, CH0], I32)
            rec_s, blk_s = g.sb("rec_s", [128, CH0 * FIELDS]), g.sb("blk_s", [1, CH0], I32)
            bucket(nc, c, "by_dst", I["dst"], I["src"], None, 125, 425, (5, 5, 17), CH0,
                   dram("sorted_dst", [CH0 * EC, FIELDS]), rec_d, blk_d)
            bucket(nc, c, "by_src", I["src"], I["dst"], I["edge_weight"], 125, 425, (5, 5, 17), CH0,
                   dram("sorted_src", [CH0 * EC, FIELDS]), rec_s, blk_s)

            y_d = dram("y", [N, D])
            with Stage(nc, "l0g") as s:
                yf = s.sb("yf", [128, DC * N])
                mf = s.sb("mf", [128, DC * N])
                with Stage(nc, "l0y") as s2:
                    y = s2.sb("y", [P, T * D])
                    layernorm(nc, "ln0", x, y)
                    transfer(nc, "store_y0", [(by_tile(y_d, D), as_tiles(y, D))])
                    turn_tiles(nc, c, "turn0", y, D, yf)
                with Stage(nc, "l0a") as s2:
                    acc = s2.sb("acc", [P, T * (D + 1)])
                    inv = s2.sb("inv", [P, T])
                    segment_sum(nc, c, "sum0", y_d, D, rec_d, blk_d, CH0, acc, True)
                    a3 = as_tiles(acc, D + 1)

                    def mean(step, V):
                        step(V.tensor_copy(count[:], a3[:, :, D]))
                        step(V.tensor_scalar(inv[:], count[:], 1.0, None, ALU.max))
                        step(V.reciprocal(inv[:], inv[:]))
                        step(V.tensor_tensor(a3[:, :, 0:D], a3[:, :, 0:D], inv[:].unsqueeze(2).broadcast_to([P, T, D]), ALU.mult))
                        step(V.tensor_scalar(inv3[:], count[:], 1.0, 1.0, ALU.add, ALU.max))
                    vector_steps(nc, "mean0", mean)
                    root(nc, "root3", inv3, inv3)
                    turn_tiles(nc, c, "turn0b", acc, D, mf, stride=D + 1)
                project(nc, c, "out0", from_features(mf, I["L0_gnn_W_neigh"]) + from_features(yf, I["L0_gnn_W_self"]),
                        D, "add", x, bias=I["L0_gnn_b_self"])
            probe(1)

            with Stage(nc, "l0f") as s:
                yf = s.sb("yf", [128, DC * N])
                with Stage(nc, "l0fy") as s2:
                    y = s2.sb("y", [P, T * D])
                    layernorm(nc, "ln0f", x, y)
                    turn_tiles(nc, c, "turn0f", y, D, yf)
                logits, gate = s.sb("logits", [P, T * 8]), s.sb("gate", [P, T * 8])
                acc = s.sb("acc", [P, T * D])
                project(nc, c, "route0", from_features(yf, I["L0_ffn_gate_w"]), 8, "copy", logits, bias=I["L0_ffn_gate_b"])
                top_one(nc, c, "gate0", logits, 8, capacity, gate)
                network(nc, c, "net0", yf, 8, 1024, ACT.Relu, I["L0_ffn_w1"], I["L0_ffn_b1"], I["L0_ffn_w2"], I["L0_ffn_b2"], gate, acc)
                finite(nc, "finite0", acc)
                vector_steps(nc, "res0", lambda step, V: step(V.tensor_tensor(x[:], x[:], acc[:], ALU.add)))
            probe(2)

            k_d, v_d = dram("k", [N, D]), dram("v", [N, D])
            with Stage(nc, "l1g") as s:
                y = s.sb("y", [P, T * D])
                attended = s.sb("attended", [P, T * (D + heads)])
                layernorm(nc, "ln1", x, y)
                with Stage(nc, "l1e") as s1:
                    scores = s1.sb("scores", [EC, CH0 * heads])
                    best = s1.sb("best", [P, T * heads])
                    with Stage(nc, "l1q") as s2:
                        q = s2.sb("q", [P, T * D])
                        with Stage(nc, "l1kv") as s3:
                            yf = s3.sb("yf", [128, DC * N])
                            turn_tiles(nc, c, "turn1", y, D, yf)
                            for wname, table in (("L1_gnn_Wk", k_d), ("L1_gnn_Wv", v_d)):
                                project(nc, c, "kv", from_features(yf, I[wname]), D, "copy", q)
                                transfer(nc, "store_kv", [(by_tile(table, D), as_tiles(q, D))])
                            project(nc, c, "q", from_features(yf, I["L1_gnn_Wq"]), D, "copy", q)
                        edge_scores(nc, c, "scores", k_d, q, rec_d, blk_d, CH0, heads, hd ** -0.5, scores)
                    vector_steps(nc, "max0", lambda step, V: step(V.memset(best[:], 0.0)))
                    segment_max(nc, c, "max1", scores, heads, heads, rec_d, blk_d, CH0, best, False)
                    softmax_sum(nc, c, "att1", heads, hd, rec_d, blk_d, CH0, attended, best, heads, v_d, scores, None, False)
                af = s.sb("af", [128, DC * N])
                inv = s.sb("inv", [P, T * heads])

                def normalise(step, V):
                    a = as_tiles(attended, D + heads)
                    i3 = inv[:].rearrange("p (t h) -> p t h", h=heads)
                    step(V.tensor_scalar(i3, a[:, :, D:D + heads], 1e-8, None, ALU.add))
                    step(V.reciprocal(inv[:], inv[:]))
                    for h in range(heads):
                        v = a[:, :, h * hd:(h + 1) * hd]
                        step(V.tensor_tensor(v, v, i3[:, :, h:h + 1].broadcast_to([P, T, hd]), ALU.mult))
                vector_steps(nc, "norm1", normalise)
                turn_tiles(nc, c, "turn1a", attended, D, af, stride=D + heads)
                project(nc, c, "out1", from_features(af, I["L1_gnn_Wo_w"]), D, "add", y, bias=I["L1_gnn_Wo_b"])
                layernorm(nc, "ln1a", y, y, I["L1_gnn_ln1_g"], I["L1_gnn_ln1_b"])
                turn_tiles(nc, c, "turn1h", y, D, af)
                acc = attended[:, 0:T * D]
                network(nc, c, "net1", af, 1, 512, ACT.Gelu, I["L1_gnn_ffn_w1"], I["L1_gnn_ffn_b1"], I["L1_gnn_ffn_w2"],
                        I["L1_gnn_ffn_b2"], c["ones"], acc)
                vector_steps(nc, "res1", lambda step, V: step(V.tensor_tensor(y[:], y[:], acc, ALU.add)))
                layernorm(nc, "ln1b", y, y, I["L1_gnn_ln2_g"], I["L1_gnn_ln2_b"])
                vector_steps(nc, "res1b", lambda step, V: step(V.tensor_tensor(x[:], x[:], y[:], ALU.add)))
            probe(3)

            with Stage(nc, "l1f") as s:
                yf = s.sb("yf", [128, DC * N])
                with Stage(nc, "l1fy") as s2:
                    y = s2.sb("y", [P, T * D])
                    layernorm(nc, "ln1f", x, y)
                    turn_tiles(nc, c, "turn1f", y, D, yf)
                logits, gate = s.sb("logits", [P, T * 8]), s.sb("gate", [P, T * 8])
                acc = s.sb("acc", [P, T * D])
                project(nc, c, "route1", from_features(yf, I["L1_ffn_Wg"]), 8, "copy", logits, bias=I["L1_ffn_bg"])
                top_two(nc, c, "gate1", logits, T, 8, gate)
                network(nc, c, "net1f", yf, 8, 1024, ACT.Relu, I["L1_ffn_W1"], I["L1_ffn_b1"], I["L1_ffn_W2"], I["L1_ffn_b2"], gate, acc)
                vector_steps(nc, "res1f", lambda step, V: step(V.tensor_tensor(x[:], x[:], acc[:], ALU.add)))
            probe(4)

            z_d = dram("z", [N, D])
            with Stage(nc, "l2g") as s:
                yf = s.sb("yf", [128, DC * N])
                acc = s.sb("acc", [P, T * D])
                with Stage(nc, "l2d") as s2:
                    deg = s2.sb("deg", [P, T])
                    guard = s2.sb("guard", [P, T])
                    segment_sum(nc, c, "deg2", None, 0, rec_s, blk_s, CH0, deg, True)

                    def guarded(step, V):
                        step(V.tensor_scalar(deg[:], deg[:], 1.0, None, ALU.add))
                        step(V.tensor_scalar(guard[:], deg[:], 0.0, None, ALU.is_gt))
                        step(V.tensor_scalar(deg[:], deg[:], 1e-38, None, ALU.max))
                    vector_steps(nc, "guard2", guarded)
                    root(nc, "root2", deg, inv2)
                    vector_steps(nc, "guard2b", lambda step, V: step(V.tensor_tensor(inv2[:], inv2[:], guard[:], ALU.mult)))
                with Stage(nc, "l2y") as s2:
                    y = s2.sb("y", [P, T * D])
                    layernorm(nc, "ln2", x, y)
                    turn_tiles(nc, c, "turn2", y, D, yf)
                with Stage(nc, "l2z") as s2:
                    z = s2.sb("z", [P, T * D])
                    project(nc, c, "z2", from_features(yf, I["L2_gnn_W"]), D, "scale", z, scale=inv2)
                    transfer(nc, "store_z2", [(by_tile(z_d, D), as_tiles(z, D))])
                    segment_sum(nc, c, "sum2", z_d, D, rec_s, blk_s, CH0, acc, False)

                    def finish(step, V):
                        step(V.tensor_tensor(acc[:], acc[:], z[:], ALU.add))
                        step(V.tensor_tensor(as_tiles(acc, D), as_tiles(acc, D), inv2[:].unsqueeze(2).broadcast_to([P, T, D]), ALU.mult))
                    vector_steps(nc, "self2", finish)
                turn_tiles(nc, c, "turn2b", acc, D, yf)
                column_add(nc, "b2", yf, I["L2_gnn_b"])
                vector_steps(nc, "zero2", lambda step, V: step(V.memset(acc[:], 0.0)))
                project(nc, c, "head2", from_features(yf, I["L2_gnn_W1"]), D, "relu_add", acc, bias=I["L2_gnn_b1"])
                turn_tiles(nc, c, "turn2c", acc, D, yf)
                project(nc, c, "head2b", from_features(yf, I["L2_gnn_W2"]), D, "add", x, bias=I["L2_gnn_b2"])
            probe(5)

            with Stage(nc, "l2f") as s:
                yf = s.sb("yf", [128, DC * N])
                y = s.sb("y", [P, T * D])
                acc = s.sb("acc", [P, T * D])
                scores, gate = s.sb("scores", [P, 8]), s.sb("gate", [P, T * 8])
                layernorm(nc, "ln2f", x, y)
                turn_tiles(nc, c, "turn2f", y, D, yf)
                global_scores(nc, c, "route2", yf, I["L2_ffn_Wr"], I["L2_ffn_br"], 8, capacity, scores)
                top_two(nc, c, "gate2", scores, 1, 8, gate, replicate=T)
                network(nc, c, "net2", yf, 8, 512, ACT.Gelu, I["L2_ffn_W1"], I["L2_ffn_b1"], I["L2_ffn_W2"], I["L2_ffn_b2"], gate, acc)
                vector_steps(nc, "res2", lambda step, V: step(V.tensor_tensor(y[:], y[:], acc[:], ALU.add)))
                layernorm(nc, "ln2b", y, y, I["L2_ffn_gamma"], I["L2_ffn_beta"])
                vector_steps(nc, "res2b", lambda step, V: step(V.tensor_tensor(x[:], x[:], y[:], ALU.add)))
            probe(6)

            z1_d, z2_d = dram("z1", [N, 128]), dram("z2t", [N, 64])
            with Stage(nc, "l3g") as s:
                yf = s.sb("yf", [128, DC * N])
                x1f, x2f = s.sb("x1f", [128, N]), s.sb("x2f", [64, N])
                with Stage(nc, "l3y") as s2:
                    y = s2.sb("y", [P, T * D])
                    layernorm(nc, "ln3", x, y)
                    turn_tiles(nc, c, "turn3", y, D, yf)
                for k, (wide, srcs, table, xf) in enumerate((
                        (128, from_features(yf, I["L3_gnn_W1"]), z1_d, x1f),
                        (64, [(x1f, 128, 0, I["L3_gnn_W2"])], z2_d, x2f))):
                    with Stage(nc, "l3z") as s2:
                        z, acc = s2.sb("z", [P, T * wide]), s2.sb("acc", [P, T * wide])
                        project(nc, c, "z3", srcs, wide, "scale", z, scale=inv3)
                        transfer(nc, "store_z3", [(by_tile(table, wide), as_tiles(z, wide))])
                        segment_sum(nc, c, "sum3", table, wide, rec_d, blk_d, CH0, acc, False)

                        def finish(step, V):
                            step(V.tensor_tensor(acc[:], acc[:], z[:], ALU.add))
                            step(V.tensor_tensor(as_tiles(acc, wide), as_tiles(acc, wide),
                                                 inv3[:].unsqueeze(2).broadcast_to([P, T, wide]), ALU.mult))
                        vector_steps(nc, "self3", finish)
                        turn_tiles(nc, c, "turn3b", acc, wide, xf)
                    batch_norm_relu(nc, "bn3", xf, wide, I[f"L3_gnn_b{k + 1}"], I[f"L3_gnn_g{k + 1}"], I[f"L3_gnn_be{k + 1}"])
                wfc = I["L3_gnn_Wfc"]
                project(nc, c, "out3", [(yf, 128, 0, wfc[0:128, :]), (yf, 128, 1, wfc[128:256, :]),
                                        (x1f, 128, 0, wfc[256:384, :]), (x2f, 64, 0, wfc[384:448, :])],
                        D, "relu_add", x, bias=I["L3_gnn_bfc"])
            probe(7)

        with Stage(nc, "l3f") as s:
            yf = s.sb("yf", [128, DC * N])
            with Stage(nc, "l3fy") as s2:
                y = s2.sb("y", [P, T * D])
                layernorm(nc, "ln3f", x, y)
                turn_tiles(nc, c, "turn3f", y, D, yf)
            gate = s.sb("gate", [P, T * ge])
            with Stage(nc, "gat") as s2:
                attention_gate(nc, c, I, s2, dram, yf, CH3, gh, ge, gate)
            acc = s.sb("acc", [P, T * D])
            network(nc, c, "net3", yf, ge, 512, ACT.Gelu, I["L3_ffn_W1"], I["L3_ffn_b1"], I["L3_ffn_W2"], I["L3_ffn_b2"], gate, acc)
            vector_steps(nc, "res3", lambda step, V: step(V.tensor_tensor(x[:], x[:], acc[:], ALU.add)))
        transfer(nc, "store_out", [(by_tile(out, D), as_tiles(x, D))])


def column_add(nc, name, xf, bias_d):
    with Stage(nc, name) as s:
        col = s.sb("col", [128, DC])
        loaded, steps = s.sem("loaded"), s.sem("steps")
        with s.block() as block:
            @block.sync
            def _(sp):
                sp.dma_start(col[:], bias_d).then_inc(loaded, 16)

            @block.vector
            def _(dve):
                step = Steps(dve, steps)
                dve.wait_ge(loaded, 16)
                for k in range(DC):
                    v = xf[:, k * N:(k + 1) * N]
                    step(nc.vector.tensor_scalar(v, v, col[:, k:k + 1], None, ALU.add))


def attention_gate(nc, c, I, s, dram, yf, chunks, gh, ge, gate):
    w = gh * ge
    rec, blk = s.sb("rec", [128, chunks * FIELDS]), s.sb("blk", [1, chunks], I32)
    bucket(nc, c, "by_dst3", I["edge3_dst"], I["edge3_src"], None, 128, 256, (4, 4, 16), chunks,
           dram("sorted3", [chunks * EC, FIELDS]), rec, blk)
    row = w + gh
    hs = s.sb("hs", [P, T * row])
    best = s.sb("best", [P, T * gh])
    node = s.sb("node", [P, T * 2 * gh])
    att = s.sb("att", [P, 3 * w])
    tmp = s.sb("tmp", [P, T * w])
    e_self, p_self = s.sb("e_self", [P, T * gh]), s.sb("p_self", [P, T * gh])
    acc = s.sb("acc", [P, T * row])
    stored = s.sb("stored", [EC, chunks * row])
    table = dram("gat", [N, row])
    h3, n3, a3 = as_tiles(hs, row), as_tiles(node, 2 * gh), as_tiles(acc, row)

    def heads_of(v):
        return v.rearrange("p t (h e) -> p t h e", h=gh)

    project(nc, c, "h_gat", from_chunks(yf, I["L3_ffn_W_gat"]), w, "copy", hs, stride=row)
    transfer(nc, "att", [(att[:, 0:w], I["L3_ffn_att_src"].partition_broadcast(P)),
                         (att[:, w:2 * w], I["L3_ffn_att_dst"].partition_broadcast(P)),
                         (att[:, 2 * w:3 * w], I["L3_ffn_b_gat"].partition_broadcast(P))])

    def parts(step, V):
        t3 = as_tiles(tmp, w)
        for k, dst in ((0, h3[:, :, w:row]), (1, n3[:, :, 0:gh])):
            step(V.tensor_tensor(t3, h3[:, :, 0:w], att[:, k * w:(k + 1) * w].unsqueeze(1).broadcast_to([P, T, w]), ALU.mult))
            step(V.tensor_reduce(dst, heads_of(t3), AX.X, ALU.add))
        step(V.tensor_copy(as_tiles(best, gh), h3[:, :, w:row]))
    vector_steps(nc, "parts", parts)
    transfer(nc, "store_gat", [(by_tile(table, row), h3)])
    gather_all(nc, c, "rows3", table, row, rec, chunks, stored)
    values = stored[:, w:]
    segment_max(nc, c, "max3", values, row, gh, rec, blk, chunks, best, True)

    def maxima(step, V):
        b3, e3 = as_tiles(best, gh), as_tiles(e_self, gh)
        step(V.tensor_tensor(b3, b3, n3[:, :, 0:gh], ALU.add))
        step(V.scalar_tensor_tensor(n3[:, :, gh:2 * gh], b3, 0.2, b3, ALU.mult, ALU.max))
        step(V.tensor_tensor(e3, h3[:, :, w:row], n3[:, :, 0:gh], ALU.add))
        step(V.scalar_tensor_tensor(as_tiles(p_self, gh), e3, 0.2, e3, ALU.mult, ALU.max))
        step(V.tensor_tensor(e3, as_tiles(p_self, gh), n3[:, :, gh:2 * gh], ALU.subtract))
    vector_steps(nc, "maxima", maxima)
    exponential(nc, "exp_self", e_self, p_self)
    softmax_sum(nc, c, "att3", gh, ge, rec, blk, chunks, acc, node, 2 * gh, None, None, stored, True)

    def scores(step, V):
        p3, t3 = as_tiles(p_self, gh), as_tiles(tmp, w)
        step(V.tensor_tensor(a3[:, :, w:row], a3[:, :, w:row], p3, ALU.add))
        step(V.tensor_scalar(as_tiles(e_self, gh), a3[:, :, w:row], 1e-16, None, ALU.add))
        step(V.reciprocal(e_self[:], e_self[:]))
        for h in range(gh):
            k = slice(h * ge, (h + 1) * ge)
            step(V.tensor_tensor(t3[:, :, k], h3[:, :, k], p3[:, :, h:h + 1].broadcast_to([P, T, ge]), ALU.mult))
            step(V.tensor_tensor(t3[:, :, k], t3[:, :, k], a3[:, :, k], ALU.add))
            step(V.tensor_tensor(t3[:, :, k], t3[:, :, k], as_tiles(e_self, gh)[:, :, h:h + 1].broadcast_to([P, T, ge]), ALU.mult))
        step(V.tensor_tensor(t3, t3, att[:, 2 * w:3 * w].unsqueeze(1).broadcast_to([P, T, w]), ALU.add))
    vector_steps(nc, "scores3", scores)
    with Stage(nc, "ln_gat") as s2:
        mean, var, inv = s2.sb("mean", [P, T]), s2.sb("var", [P, T]), s2.sb("inv", [P, T])
        sq = s2.sb("sq", [P, T * w])
        gb = s2.sb("gb", [P, 2 * w])
        sc = s2.sb("sc", [P, T * ge])
        t3 = as_tiles(tmp, w)
        transfer(nc, "gb", [(gb[:, 0:w], I["L3_ffn_ln_gamma"].partition_broadcast(P)),
                            (gb[:, w:2 * w], I["L3_ffn_ln_beta"].partition_broadcast(P))])

        def variance(step, V):
            step(V.tensor_reduce(mean[:], t3, AX.X, ALU.add))
            step(V.tensor_scalar(mean[:], mean[:], 1.0 / w, None, ALU.mult))
            step(V.tensor_tensor(t3, t3, mean[:].unsqueeze(2).broadcast_to([P, T, w]), ALU.subtract))
            step(V.tensor_tensor(sq[:], tmp[:], tmp[:], ALU.mult))
            step(V.tensor_reduce(var[:], as_tiles(sq, w), AX.X, ALU.add))
            step(V.tensor_scalar(var[:], var[:], 1.0 / w, EPS, ALU.mult, ALU.add))
        vector_steps(nc, "variance", variance)
        root(nc, "root_gat", var, inv)

        def average(step, V):
            step(V.tensor_tensor(t3, t3, inv[:].unsqueeze(2).broadcast_to([P, T, w]), ALU.mult))
            step(V.tensor_tensor(t3, t3, gb[:, 0:w].unsqueeze(1).broadcast_to([P, T, w]), ALU.mult))
            step(V.tensor_tensor(t3, t3, gb[:, w:2 * w].unsqueeze(1).broadcast_to([P, T, w]), ALU.add))
            s3 = as_tiles(sc, ge)
            step(V.tensor_tensor(s3, t3[:, :, 0:ge], t3[:, :, ge:2 * ge], ALU.add))
            for h in range(2, gh):
                step(V.tensor_tensor(s3, s3, t3[:, :, h * ge:(h + 1) * ge], ALU.add))
            step(V.tensor_scalar(sc[:], sc[:], 1.0 / gh, None, ALU.mult))
        vector_steps(nc, "average", average)
        top_two(nc, c, "gate3", sc, T, ge, gate)


def from_chunks(t, w):
    wide = w.shape[1] // DC
    return [(t, 128, k, w[:, k * wide:(k + 1) * wide]) for k in range(DC)]


def exponential(nc, name, src, dst):
    with Stage(nc, name) as s:
        done = s.sem("done")
        with s.block() as block:
            @block.scalar
            def _(act):
                nc.scalar.activation(dst[:], src[:], ACT.Exp).then_inc(done, 1)



def lay_out(inputs):
    import numpy as np
    a = {k: np.ascontiguousarray(v) for k, v in inputs.items()}
    o = {"x": a["x"]}

    def rows(w):
        w = w.reshape(-1, 128, w.shape[-1])
        return w.transpose(1, 0, 2).reshape(128, -1)

    def experts(w):
        return np.stack([rows(e) for e in w])

    def columns(b):
        return b.reshape(-1, 128).T

    o["src"], o["dst"] = a["src"].reshape(125, -1), a["dst"].reshape(125, -1)
    o["edge_weight"] = a["edge_weight"].reshape(125, -1)
    o["edge3_src"], o["edge3_dst"] = a["L3_ffn_edge_index"][0].reshape(128, -1), a["L3_ffn_edge_index"][1].reshape(128, -1)
    for k in ("L0_gnn_W_neigh", "L0_gnn_W_self"):
        o[k] = rows(a[k].T)
    o["L1_ffn_Wg"] = rows(a["L1_ffn_Wg"].T)
    for k in ("L0_ffn_gate_w", "L1_gnn_Wq", "L1_gnn_Wk", "L1_gnn_Wv", "L1_gnn_Wo_w", "L2_gnn_W", "L2_gnn_W1",
              "L2_gnn_W2", "L2_ffn_Wr", "L3_gnn_W1", "L3_ffn_W_gat"):
        o[k] = rows(a[k])
    for k in ("L3_gnn_W2", "L3_gnn_Wfc"):
        o[k] = a[k]
    for k in ("L0_gnn_b_self", "L0_ffn_gate_b", "L1_gnn_Wo_b", "L1_ffn_bg", "L2_gnn_b1", "L2_gnn_b2", "L3_gnn_bfc"):
        o[k] = a[k].reshape(1, -1)
    for k in ("L1_gnn_ln1_g", "L1_gnn_ln1_b", "L1_gnn_ln2_g", "L1_gnn_ln2_b", "L2_ffn_br", "L2_ffn_gamma", "L2_ffn_beta",
              "L3_ffn_att_src", "L3_ffn_att_dst", "L3_ffn_b_gat", "L3_ffn_ln_gamma", "L3_ffn_ln_beta"):
        o[k] = a[k].reshape(-1)
    o["L2_gnn_b"] = a["L2_gnn_b"].reshape(-1, 128).T
    for k in ("b1", "g1", "be1", "b2", "g2", "be2"):
        o[f"L3_gnn_{k}"] = a[f"L3_gnn_{k}"].reshape(-1, 1)
    for pre, w1, w2 in (("L0_ffn", "w1", "w2"), ("L2_ffn", "W1", "W2"), ("L3_ffn", "W1", "W2")):
        o[f"{pre}_{w1}"], o[f"{pre}_{w2}"] = experts(a[f"{pre}_{w1}"]), experts(a[f"{pre}_{w2}"])
    o["L1_ffn_W1"], o["L1_ffn_W2"] = experts(a["L1_ffn_W1"].transpose(0, 2, 1)), experts(a["L1_ffn_W2"].transpose(0, 2, 1))
    o["L1_gnn_ffn_w1"], o["L1_gnn_ffn_w2"] = experts(a["L1_gnn_ffn_w1"][None]), experts(a["L1_gnn_ffn_w2"][None])
    for pre in ("L0_ffn", "L1_ffn", "L2_ffn", "L3_ffn"):
        o[f"{pre}_b1"], o[f"{pre}_b2"] = columns(a[f"{pre}_b1"]), a[f"{pre}_b2"]
    o["L1_gnn_ffn_b1"], o["L1_gnn_ffn_b2"] = columns(a["L1_gnn_ffn_b1"][None]), a["L1_gnn_ffn_b2"][None]
    return {k: np.ascontiguousarray(v) for k, v in o.items()}


def kernel(**inputs):
    import concourse.bacc as _bacc
    from concourse.bass_utils import run_bass_kernel_spmd as _run

    nc = _bacc.Bacc("TRN2", target_bir_lowering=False, num_devices=1)
    arrays = {f"in_{k}": v for k, v in lay_out(inputs).items()}
    aps = {k[3:]: nc.dram_tensor(k, v.shape, mybir.dt.from_np(v.dtype), kind="ExternalInput").ap()
           for k, v in arrays.items()}
    out = nc.dram_tensor("out", (N, D), F32, kind="ExternalOutput").ap()
    model(nc, aps, out)
    r = _run(nc, [arrays], core_ids=[0])
    return r.results[0]["out"]
```

```python
from contextlib import ExitStack

import concourse.bass as bass
from concourse import mybir

F32 = mybir.dt.float32
BF16 = mybir.dt.bfloat16
I32 = mybir.dt.int32
ALU = mybir.AluOpType
ACT = mybir.ActivationFunctionType
AX = mybir.AxisListType

N = 3125
P = 125
T = N // P
D = 256
DC = D // 128
EC = 128
RING = 5
FIELDS = 4
EPS = 1e-5
GROUP = RING * P
PIECES = ((0, 375), (375, 250))


def chunk_bound(edges):
    most = (edges + T * (EC - 1)) // EC
    return -(-most // 8) * 8


class Stage:

    count = 0

    def __init__(self, nc, name):
        Stage.count += 1
        self.nc, self.name, self.ctx, self.sems = nc, f"{name}{Stage.count}", ExitStack(), []

    def __enter__(self):
        self.ctx.__enter__()
        return self

    def __exit__(self, *e):
        if self.sems and e[0] is None:
            self.nc.clear_and_free_semaphores(self.sems)
            self.nc.all_engine_barrier()
        return self.ctx.__exit__(*e)

    def sb(self, name, shape, dt=F32):
        return self.ctx.enter_context(self.nc.sbuf_tensor(f"{self.name}_{name}", shape, dt))

    def ps(self, name, shape, dt=F32):
        return self.ctx.enter_context(self.nc.psum_tensor(f"{self.name}_{name}", shape, dt))

    def sem(self, name):
        self.sems.append(self.nc.alloc_semaphore(f"{self.name}_{name}"))
        return self.sems[-1]

    def block(self):
        return self.nc.Block(self.name)


class Steps:

    def __init__(self, eng, sem):
        self.eng, self.sem, self.n, self.at = eng, sem, 0, None

    def __call__(self, ins):
        ins.then_inc(self.sem, 1)
        self.n += 1
        self.eng.wait_ge(self.sem, self.n if self.at is None else self.at + self.n)

    def loop(self, i, per):
        self.base, self.at, self.n = (self.n, self.n + i * per, 0)

    def leave(self, count, per):
        assert self.n == per, (self.n, per)
        self.n, self.at = self.base + count * per, None


def bcast(ap, shape):
    return ap.broadcast_to(shape)


def tile_of(t, width):
    return bass.ds(t * width, width)



def constants(nc, c, I):
    with Stage(nc, "const") as s:
        zero = s.sem("zero")
        made = s.sem("made")
        with s.block() as block:
            @block.gpsimd
            def _(pool):
                nc.gpsimd.memset(c["ident"][:], 0.0).then_inc(zero, 1)
                nc.gpsimd.iota(c["iota"][:], pattern=[[1, 128]], base=0, channel_multiplier=0,
                               allow_small_or_imprecise_dtypes=True).then_inc(made, 1)
                nc.gpsimd.memset(c["ones"][:], 1.0).then_inc(made, 1)
                pool.wait_ge(zero, 1)
                nc.gpsimd.affine_select(out=c["ident"][:], in_=c["ident"][:], compare_op=ALU.not_equal,
                                        fill=1.0, base=0, pattern=[[-1, 128]],
                                        channel_multiplier=1).then_inc(made, 1)



def transfer(nc, name, pairs):
    with Stage(nc, name) as s:
        by_sync, by_act = s.sem("by_sync"), s.sem("by_act")
        with s.block() as block:
            @block.sync
            def _(sp):
                for dst, src in pairs[0::2]:
                    sp.dma_start(dst, src).then_inc(by_sync, 16)
                sp.wait_ge(by_sync, 16 * len(pairs[0::2]))

            @block.scalar
            def _(act):
                for dst, src in pairs[1::2]:
                    act.dma_start(dst, src).then_inc(by_act, 16)
                if len(pairs) > 1:
                    act.wait_ge(by_act, 16 * len(pairs[1::2]))


def by_tile(dram, width):
    return dram.rearrange("(t p) f -> p t f", p=P)


def as_tiles(sb, width):
    return sb[:].rearrange("p (t f) -> p t f", f=width)



def bucket(nc, c, name, key_d, other_d, weight_d, parts, cols, loops, chunks, sorted_d, rec, blk):
    iters, groups, per = loops
    assert iters * groups * per == cols
    with Stage(nc, name) as s:
        key_i = s.sb("key_i", [parts, cols], I32)
        other_i = s.sb("other_i", [parts, cols], I32)
        key = s.sb("key", [parts, cols])
        thr = s.sb("thr", [128, T + 1])
        member = s.sb("member", [parts, T * cols], BF16)
        before = s.sb("before", [parts, T * cols])
        above = s.sb("above", [parts, cols])
        zeros = s.sb("zeros", [parts, cols])
        carry = s.sb("carry", [parts, 1])
        ones_b = s.sb("ones_b", [parts, parts], BF16)
        tri = s.sb("tri", [parts, parts], BF16)
        first = s.sb("first", [parts, T])
        ends = s.sb("ends", [parts, T])
        count_f = s.sb("count_f", [parts, T])
        count_i = s.sb("count_i", [parts, T], I32)
        cstart = s.sb("cstart", [parts, T])
        cend = s.sb("cend", [parts, T])
        adj = s.sb("adj", [parts, T])
        pos = s.sb("pos", [parts, cols])
        sub = s.sb("sub", [parts, cols])
        q1 = s.sb("q1", [parts, cols])
        q2 = s.sb("q2", [parts, cols])
        pos_i = s.sb("pos_i", [parts, cols], I32)
        row_i = s.sb("row_i", [parts, cols], I32)
        slot_i = s.sb("slot_i", [parts, cols], I32)
        records = s.sb("records", [parts, cols * FIELDS])
        blk_f = s.sb("blk_f", [1, chunks])
        citer = s.sb("citer", [1, chunks])
        rec_s = [s.sb(f"rec_s{g}", [parts, per * FIELDS]) for g in range(groups)]
        dst_s = [s.sb(f"dst_s{g}", [parts, per], I32) for g in range(groups)]
        ps = [s.ps(f"ps{h}", [parts, 512]) for h in range(2)]
        loaded = s.sem("loaded")
        steps = s.sem("steps")
        made = s.sem("made")
        blank = s.sem("blank")
        blanked = s.sem("blanked")
        masks = s.sem("masks")
        totals = s.sem("totals")
        summed = s.sem("summed")
        ranks = s.sem("ranks")
        ranked = s.sem("ranked")
        staged = [s.sem(f"staged{g}") for g in range(groups)]
        sent = [s.sem(f"sent{g}") for g in range(groups)]
        back = s.sem("back")
        go = s.sem("go")
        rec4 = records[:].rearrange("p (c f) -> p c f", f=FIELDS)

        with s.block() as block:
            @block.sync
            def _(sp):
                sp.dma_start(key_i[:], key_d).then_inc(loaded, 16)
                sp.dma_start(other_i[:], other_d).then_inc(loaded, 16)
                if weight_d is not None:
                    sp.dma_start(sub[:], weight_d).then_inc(loaded, 16)
                sp.wait_ge(blank, 2)
                sp.dma_start(sorted_d.rearrange("(p c) f -> p (c f)", p=EC), rec[:]).then_inc(blanked, 16)
                for g in range(groups):
                    sp.wait_ge(sent[g], 16 * per * iters)
                sp.dma_start(rec[:], sorted_d.rearrange("(p c) f -> p (c f)", p=EC)).then_inc(back, 16)
                sp.wait_ge(back, 16)

            @block.gpsimd
            def _(pool):
                nc.gpsimd.iota(thr[:], pattern=[[P, T + 1]], base=0, channel_multiplier=0,
                               allow_small_or_imprecise_dtypes=True).then_inc(made, 1)
                nc.gpsimd.iota(citer[:], pattern=[[1, chunks]], base=0, channel_multiplier=0,
                               allow_small_or_imprecise_dtypes=True).then_inc(made, 1)
                nc.gpsimd.memset(tri[:], -1.0).then_inc(made, 1)
                nc.gpsimd.memset(ones_b[:], 1.0).then_inc(made, 1)
                pool.wait_ge(made, 4)
                nc.gpsimd.affine_select(out=tri[:], in_=tri[:], compare_op=ALU.is_ge, fill=0.0, base=0,
                                        pattern=[[-1, parts]], channel_multiplier=1).then_inc(made, 1)
                pool.wait_ge(blanked, 16)
                with pool.Fori(0, iters) as i:
                    for g in range(groups):
                        pool.wait_ge(staged[g], 2 * i + 2)
                        pool.sem_inc(go, 1)
                        for k in range(per):
                            pool.indirect_dma_start(
                                sorted_d, bass.IndirectOffsetOnAxis(ap=dst_s[g][:, k:k + 1], axis=0),
                                rec_s[g][:, k * FIELDS:(k + 1) * FIELDS], None).then_inc(sent[g], 16)

            @block.tensor
            def _(pe):
                pe.wait_ge(made, 5)
                pe.wait_ge(masks, T + 1)
                with pe.Fori(0, T) as b:
                    pe.wait_ge(summed, b + 1)
                    nc.tensor.matmul(ps[0][:, 0:cols], ones_b[:], member[:, tile_of(b, cols)],
                                     start=True, stop=True).then_inc(totals, 1)
                with pe.Fori(0, T) as b:
                    pe.wait_ge(ranked, b + 1)
                    nc.tensor.matmul(ps[1][:, 0:cols], tri[:], member[:, tile_of(b, cols)],
                                     start=True, stop=True).then_inc(ranks, 1)

            @block.vector
            def _(dve):
                step = Steps(dve, steps)
                for sem in (masks, summed, ranked):
                    dve.sem_inc(sem, 1)
                nc.vector.memset(rec[:], 0.0).then_inc(blank, 1)
                dve.wait_ge(blank, 1)
                nc.vector.memset(rec[:].rearrange("p (c f) -> p c f", f=FIELDS)[:, :, 1], -1.0).then_inc(blank, 1)
                dve.wait_ge(loaded, 32 if weight_d is None else 48)
                dve.wait_ge(made, 5)
                step(nc.vector.tensor_copy(key[:], key_i[:]))
                step(nc.vector.memset(records[:], 1.0))
                step(nc.vector.tensor_copy(rec4[:, :, 0], other_i[:]))
                if weight_d is not None:
                    step(nc.vector.tensor_copy(rec4[:, :, 2], sub[:]))
                step(nc.vector.memset(zeros[:], 0.0))
                step(nc.vector.memset(carry[:], 0.0))
                step(nc.vector.memset(pos[:], 0.0))
                step(nc.vector.tensor_copy(sub[:], key[:]))
                with dve.Fori(0, T) as b:
                    step.loop(b, 1)
                    dve.wait_ge(masks, b + 1)
                    step(nc.vector.tensor_scalar(above[:], key[:], thr[0:parts, bass.ds(b, 1)], None, ALU.is_ge))
                    nc.vector.scalar_tensor_tensor(member[:, tile_of(b, cols)], key[:],
                                                   thr[0:parts, bass.ds(b + 1, 1)], above[:],
                                                   ALU.is_lt, ALU.mult).then_inc(masks, 1)
                step.leave(T, 1)
                with dve.Fori(0, T) as b:
                    step.loop(b, 1)
                    dve.wait_ge(totals, b + 1)
                    step(nc.vector.tensor_tensor_scan(before[:, tile_of(b, cols)], zeros[:], ps[0][:, 0:cols],
                                                      carry[:], ALU.add, ALU.add))
                    nc.vector.tensor_copy(carry[:], before[:, bass.ds(b * cols + cols - 1, 1)]).then_inc(summed, 1)
                    dve.wait_ge(summed, b + 2)
                step.leave(T, 1)
                last = before[:].rearrange("p (b c) -> p b c", c=cols)[:, :, cols - 1]
                step(nc.vector.tensor_copy(ends[:], last))
                step(nc.vector.memset(first[:], 0.0))
                step(nc.vector.tensor_copy(first[:, 1:T], ends[:, 0:T - 1]))
                step(nc.vector.tensor_tensor(count_f[:], ends[:], first[:], ALU.subtract))
                step(nc.vector.tensor_scalar(count_f[:], count_f[:], float(EC - 1), None, ALU.add))
                step(nc.vector.tensor_copy(count_i[:], count_f[:]))
                step(nc.vector.tensor_scalar(count_i[:], count_i[:], 7, None, ALU.arith_shift_right))
                step(nc.vector.tensor_copy(count_f[:], count_i[:]))
                step(nc.vector.tensor_tensor_scan(cend[:], zeros[:, 0:T], count_f[:], 0.0, ALU.add, ALU.add))
                step(nc.vector.tensor_tensor(cstart[:], cend[:], count_f[:], ALU.subtract))
                step(nc.vector.scalar_tensor_tensor(adj[:], cstart[:], float(EC), first[:], ALU.mult, ALU.subtract))
                step(nc.vector.memset(blk_f[:], -1.0))
                for b in range(T):
                    step(nc.vector.scalar_tensor_tensor(blk_f[:], citer[:], cstart[0:1, b:b + 1], blk_f[:],
                                                        ALU.is_ge, ALU.add))
                step(nc.vector.tensor_copy(blk[:], blk_f[:]))
                with dve.Fori(0, T) as b:
                    step.loop(b, 3)
                    dve.wait_ge(ranks, b + 1)
                    nc.vector.scalar_tensor_tensor(q1[:], ps[1][:, 0:cols], adj[:, bass.ds(b, 1)],
                                                   before[:, tile_of(b, cols)], ALU.add, ALU.add).then_inc(ranked, 1)
                    dve.wait_ge(ranked, b + 2)
                    step(nc.vector.tensor_tensor(q2[:], q1[:], member[:, tile_of(b, cols)], ALU.mult))
                    step(nc.vector.tensor_tensor(pos[:], pos[:], q2[:], ALU.add))
                    step(nc.vector.scalar_tensor_tensor(q2[:], member[:, tile_of(b, cols)],
                                                        thr[0:parts, bass.ds(b, 1)], sub[:], ALU.mult, ALU.subtract))
                    nc.vector.tensor_scalar(sub[:], q2[:], -1.0, None, ALU.mult).then_inc(masks, 1)
                    dve.wait_ge(masks, T + 2 + b)
                step.leave(T, 3)
                step(nc.vector.tensor_copy(rec4[:, :, 1], sub[:]))
                step(nc.vector.tensor_tensor(rec4[:, :, 3], key[:], sub[:], ALU.subtract))
                step(nc.vector.tensor_copy(pos_i[:], pos[:]))
                step(nc.vector.tensor_scalar(row_i[:], pos_i[:], EC - 1, None, ALU.bitwise_and))
                step(nc.vector.tensor_scalar(slot_i[:], pos_i[:], 7, None, ALU.arith_shift_right))
                step(nc.vector.tensor_copy(q1[:], row_i[:]))
                step(nc.vector.tensor_copy(q2[:], slot_i[:]))
                step(nc.vector.scalar_tensor_tensor(pos[:], q1[:], float(chunks), q2[:], ALU.mult, ALU.add))
                step(nc.vector.tensor_copy(pos_i[:], pos[:]))

                def fill(i):
                    for g in range(groups):
                        if not isinstance(i, int):
                            dve.wait_ge(sent[g], 16 * per * i)
                        at = (i * groups + g) * per
                        nc.vector.tensor_copy(rec_s[g][:], records[:, bass.ds(at * FIELDS, per * FIELDS)]).then_inc(staged[g], 1)
                        nc.vector.tensor_copy(dst_s[g][:], pos_i[:, bass.ds(at, per)]).then_inc(staged[g], 1)

                fill(0)
                with dve.Fori(1, iters) as i:
                    fill(i)



BATCH = 4
SLOTS = 4


class Step:

    def __init__(self, i, r):
        self.turn, self.slot, self.k = i + r // SLOTS, r % SLOTS, i * SLOTS + r
        self.i, self.r = i, r

    def ahead(self, by, steps):
        later = Step(self.i, self.r + by)
        return None if isinstance(later.k, int) and later.k >= steps else later

    def chunks(self, width):
        return bass.ds(self.k * BATCH * width, BATCH * width)


def edge_steps(eng, steps, body):
    loops = (steps - SLOTS) // SLOTS
    with eng.Fori(0, loops) as i:
        for r in range(SLOTS):
            body(Step(i, r))
    for k in range(loops * SLOTS, steps):
        body(Step(k // SLOTS, k % SLOTS))


def done(sem_step, back=0):
    return SLOTS + sem_step.k + 1 - back


def with_ahead(step, by, steps, fn):
    later = step.ahead(by, steps)
    if later is not None:
        fn(later)


def stage_records(nc, act, rec, rec_s, idx_s, staged, step):
    src = rec[:, step.chunks(FIELDS)]
    if idx_s is not None:
        nc.scalar.copy(idx_s[step.slot][:], src.rearrange("p (u f) -> p u f", f=FIELDS)[:, :, 0]).then_inc(staged, 1)
    nc.scalar.copy(rec_s[step.slot][:], src).then_inc(staged, 1 if idx_s is not None else 2)


def gather_rows(nc, pool, steps, table, idx_s, rows, width, staged, used, landed, go):
    def body(st):
        pool.wait_ge(staged, 2 * st.k + 2)
        pool.sem_inc(go, 1)
        pool.wait_ge(used, done(st, SLOTS))
        pool.sem_inc(go, 1)
        for u in range(BATCH):
            pool.indirect_dma_start(rows[st.slot][:].rearrange("p (u f) -> p u f", u=BATCH)[:, u, 0:width], None, table,
                                    bass.IndirectOffsetOnAxis(ap=idx_s[st.slot][:, u:u + 1], axis=0)
                                    ).then_inc(landed[st.slot], 16)
    edge_steps(pool, steps, body)


def one_hots(nc, c, out, rec_s, step):
    for u in range(BATCH):
        k = u * FIELDS
        ins = nc.vector.tensor_scalar(out[step.slot][:, u * 128:u * 128 + P], c["iota"][:, 0:P],
                                      rec_s[step.slot][:, k + 1:k + 2], rec_s[step.slot][:, k + 2:k + 3],
                                      ALU.is_equal, ALU.mult)
    return ins


def tiles_of(nc, eng, engine, blk, step):
    _, tiles = nc.values_load_multi_w_load_instructions(
        blk[0:1, step.chunks(1)], engines=(engine,), min_val=0, max_val=T - 1,
        skip_runtime_bounds_check_because="bucket() writes tiles 0..T-1 only")
    return tiles


def segment_sum(nc, c, name, table, width, rec, blk, chunks, acc, count):
    wide = width + (1 if count else 0)
    steps = chunks // BATCH
    with Stage(nc, name) as s:
        rec_s = [s.sb(f"rec_s{h}", [EC, BATCH * FIELDS]) for h in range(SLOTS)]
        idx_s = [s.sb(f"idx_s{h}", [EC, BATCH], I32) for h in range(SLOTS)]
        rows = [s.sb(f"rows{h}", [EC, BATCH * wide]) for h in range(SLOTS)]
        oh = [s.sb(f"oh{h}", [EC, BATCH * 128]) for h in range(SLOTS)]
        ps = [s.ps(f"ps{h}", [P, BATCH * 512]) for h in range(2)]
        landed = [s.sem(f"landed{h}") for h in range(SLOTS)]
        staged, zeroed, go, counted = s.sem("staged"), s.sem("zeroed"), s.sem("go"), s.sem("counted")
        onehots, used, added = s.sem("onehots"), s.sem("used"), s.sem("added")
        adds = s.sem("adds")
        with s.block() as block:
            @block.scalar
            def _(act):
                def body(st):
                    act.wait_ge(used, done(st, SLOTS))
                    act.wait_ge(onehots, done(st, SLOTS))
                    stage_records(nc, act, rec, rec_s, idx_s, staged, st)
                edge_steps(act, steps, body)

            @block.gpsimd
            def _(pool):
                gather_rows(nc, pool, steps, table, idx_s, rows, width, staged, used, landed, go)

            @block.vector
            def _(dve):
                dve.sem_inc(onehots, SLOTS)
                dve.sem_inc(added, SLOTS)
                if count:
                    for r in rows:
                        nc.vector.memset(r[:].rearrange("p (u f) -> p u f", u=BATCH)[:, :, width], 1.0).then_inc(counted, 1)
                nc.vector.memset(acc[:], 0.0).then_inc(zeroed, 1)
                dve.wait_ge(zeroed, 1)

                def make(st):
                    dve.wait_ge(staged, 2 * st.k + 2)
                    dve.wait_ge(used, done(st, SLOTS))
                    one_hots(nc, c, oh, rec_s, st).then_inc(onehots, 1)

                def body(st):
                    with_ahead(st, 2, steps, make)
                    tiles = tiles_of(nc, dve, mybir.EngineType.DVE, blk, st)
                    dve.wait_ge(used, done(st))
                    for u, b in enumerate(tiles):
                        to = acc[:, bass.ds(b * wide, wide)]
                        last = u == BATCH - 1
                        nc.vector.tensor_tensor(to, to, ps[st.slot % 2][:, u * 512:u * 512 + wide], ALU.add
                                                ).then_inc(added if last else adds, 1)
                        dve.wait_ge(added if last else adds, done(st) if last else (BATCH - 1) * st.k + u + 1)

                for k in range(2):
                    make(Step(0, k))
                edge_steps(dve, steps, body)

            @block.tensor
            def _(pe):
                pe.sem_inc(used, SLOTS)
                if count:
                    pe.wait_ge(counted, SLOTS)

                def body(st):
                    pe.wait_ge(landed[st.slot], 16 * BATCH * (st.turn + 1))
                    pe.wait_ge(onehots, done(st))
                    pe.wait_ge(added, done(st, 2))
                    for u in range(BATCH):
                        ins = nc.tensor.matmul(ps[st.slot % 2][:, u * 512:u * 512 + wide], oh[st.slot][:, u * 128:u * 128 + P],
                                               rows[st.slot][:, u * wide:(u + 1) * wide], start=True, stop=True)
                    ins.then_inc(used, 1)
                edge_steps(pe, steps, body)


def degree(nc, c, name, rec, chunks, deg):
    steps = chunks // BATCH
    with Stage(nc, name) as s:
        first = s.sb("first", [EC, T])
        zeros = s.sb("zeros", [EC, P])
        rec_s = [s.sb(f"rec_s{h}", [EC, BATCH * FIELDS]) for h in range(SLOTS)]
        oh = [s.sb(f"oh{h}", [EC, BATCH * 128]) for h in range(SLOTS)]
        tile = [s.sb(f"tile{h}", [EC, BATCH * T]) for h in range(SLOTS)]
        ps = s.ps("ps", [P, 512])
        made, staged, done_all, taken = s.sem("made"), s.sem("staged"), s.sem("done_all"), s.sem("taken")
        onehots, used = s.sem("onehots"), s.sem("used")
        with s.block() as block:
            @block.gpsimd
            def _(pool):
                nc.gpsimd.iota(first[:], pattern=[[P, T]], base=0, channel_multiplier=0,
                               allow_small_or_imprecise_dtypes=True).then_inc(made, 1)
                nc.gpsimd.memset(zeros[:], 0.0).then_inc(made, 1)

            @block.scalar
            def _(act):
                def body(st):
                    act.wait_ge(onehots, done(st, SLOTS))
                    stage_records(nc, act, rec, rec_s, None, staged, st)
                edge_steps(act, steps, body)

            @block.vector
            def _(dve):
                dve.sem_inc(onehots, SLOTS)
                dve.wait_ge(made, 2)

                def body(st):
                    dve.wait_ge(staged, 2 * st.k + 2)
                    dve.wait_ge(used, done(st, SLOTS))
                    one_hots(nc, c, oh, rec_s, st)
                    at = rec_s[st.slot][:].rearrange("p (u f) -> p u f", u=BATCH)[:, :, 3:4]
                    nc.vector.tensor_tensor(tile[st.slot][:].rearrange("p (u t) -> p u t", u=BATCH),
                                            first[:].unsqueeze(1).broadcast_to([EC, BATCH, T]),
                                            at.broadcast_to([EC, BATCH, T]), ALU.is_equal).then_inc(onehots, 1)
                edge_steps(dve, steps, body)
                dve.wait_ge(done_all, 1)
                nc.vector.tensor_copy(deg[:], ps[:, 0:T]).then_inc(taken, 1)
                dve.wait_ge(taken, 1)

            @block.tensor
            def _(pe):
                pe.sem_inc(used, SLOTS)
                pe.wait_ge(made, 2)
                nc.tensor.matmul(ps[:, 0:T], zeros[:], zeros[:, 0:T], start=True, stop=False, skip_group_check=True)

                def body(st):
                    pe.wait_ge(onehots, done(st))
                    for u in range(BATCH):
                        ins = nc.tensor.matmul(ps[:, 0:T], oh[st.slot][:, u * 128:u * 128 + P], tile[st.slot][:, u * T:(u + 1) * T],
                                               start=False, stop=False, skip_group_check=True)
                    ins.then_inc(used, 1)
                edge_steps(pe, steps, body)
                nc.tensor.matmul(ps[:, 0:T], zeros[:], zeros[:, 0:T], start=False, stop=True,
                                 skip_group_check=True).then_inc(done_all, 1)


def turn_one_hots(nc, c, ps_t, oh, step):
    for u in range(BATCH):
        ins = nc.tensor.transpose(ps_t[step.slot % 2][:, u * EC:(u + 1) * EC], oh[step.slot][:, u * 128:u * 128 + P], c["ident"][:])
    return ins


def edge_scores(nc, c, name, k_table, q, rec, blk, chunks, heads, scale, scores):
    steps = chunks // BATCH
    with Stage(nc, name) as s:
        rec_s = [s.sb(f"rec_s{h}", [EC, BATCH * FIELDS]) for h in range(SLOTS)]
        idx_s = [s.sb(f"idx_s{h}", [EC, BATCH], I32) for h in range(SLOTS)]
        rows = [s.sb(f"rows{h}", [EC, BATCH * D]) for h in range(SLOTS)]
        oh = [s.sb(f"oh{h}", [EC, BATCH * 128]) for h in range(SLOTS)]
        oht = [s.sb(f"oht{h}", [P, BATCH * EC]) for h in range(2)]
        prod = [s.sb(f"prod{h}", [EC, BATCH * D]) for h in range(2)]
        ps_t = [s.ps(f"ps_t{h}", [P, 512]) for h in range(2)]
        ps_q = [s.ps(f"ps_q{h}", [EC, BATCH * D]) for h in range(2)]
        landed = [s.sem(f"landed{h}") for h in range(SLOTS)]
        staged, go = s.sem("staged"), s.sem("go")
        onehots, turned, kept = s.sem("onehots"), s.sem("turned"), s.sem("kept")
        spread, multiplied, reduced = s.sem("spread"), s.sem("multiplied"), s.sem("reduced")
        with s.block() as block:
            @block.scalar
            def _(act):
                act.sem_inc(kept, SLOTS)

                def stage(st):
                    act.wait_ge(multiplied, done(st, SLOTS))
                    act.wait_ge(onehots, done(st, SLOTS))
                    stage_records(nc, act, rec, rec_s, idx_s, staged, st)

                def body(st):
                    act.wait_ge(turned, done(st))
                    act.wait_ge(spread, done(st, 2))
                    nc.scalar.copy(oht[st.slot % 2][:], ps_t[st.slot % 2][:]).then_inc(kept, 1)
                    with_ahead(st, 3, steps, stage)

                for k in range(3):
                    stage(Step(0, k))
                edge_steps(act, steps, body)

            @block.gpsimd
            def _(pool):
                gather_rows(nc, pool, steps, k_table, idx_s, rows, D, staged, multiplied, landed, go)

            @block.vector
            def _(dve):
                dve.sem_inc(onehots, SLOTS)
                dve.sem_inc(multiplied, SLOTS)
                dve.sem_inc(reduced, SLOTS)

                def make(st):
                    dve.wait_ge(staged, 2 * st.k + 2)
                    dve.wait_ge(turned, done(st, SLOTS))
                    one_hots(nc, c, oh, rec_s, st).then_inc(onehots, 1)

                def body(st):
                    with_ahead(st, 2, steps, make)
                    dve.wait_ge(spread, done(st))
                    dve.wait_ge(landed[st.slot], 16 * BATCH * (st.turn + 1))
                    dve.wait_ge(reduced, done(st, 2))
                    nc.vector.scalar_tensor_tensor(prod[st.slot % 2][:], ps_q[st.slot % 2][:], float(scale), rows[st.slot][:],
                                                   ALU.mult, ALU.mult).then_inc(multiplied, 1)
                    dve.wait_ge(multiplied, done(st))
                    nc.vector.tensor_reduce(scores[:, st.chunks(heads)],
                                            prod[st.slot % 2][:].rearrange("p (h d) -> p h d", h=BATCH * heads),
                                            AX.X, ALU.add).then_inc(reduced, 1)
                for k in range(2):
                    make(Step(0, k))
                edge_steps(dve, steps, body)

            @block.tensor
            def _(pe):
                pe.sem_inc(turned, SLOTS)
                pe.sem_inc(spread, SLOTS)

                def turn(st):
                    pe.wait_ge(onehots, done(st))
                    pe.wait_ge(kept, done(st, 2))
                    turn_one_hots(nc, c, ps_t, oh, st).then_inc(turned, 1)

                def body(st):
                    with_ahead(st, 1, steps, turn)
                    tiles = tiles_of(nc, pe, mybir.EngineType.PE, blk, st)
                    pe.wait_ge(kept, done(st))
                    pe.wait_ge(multiplied, done(st, 2))
                    for u, b in enumerate(tiles):
                        ins = nc.tensor.matmul(ps_q[st.slot % 2][:, u * D:(u + 1) * D], oht[st.slot % 2][:, u * EC:(u + 1) * EC],
                                               q[:, bass.ds(b * D, D)], start=True, stop=True)
                    ins.then_inc(spread, 1)

                turn(Step(0, 0))
                edge_steps(pe, steps, body)


BIG = 1e30


def segment_max(nc, c, name, values, stride, heads, by_act, rec, blk, chunks, best, table, stored):
    steps = chunks // BATCH
    with Stage(nc, name) as s:
        rec_s = [s.sb(f"rec_s{h}", [EC, BATCH * FIELDS]) for h in range(SLOTS)]
        val_s = [s.sb(f"val_s{h}", [EC, BATCH * heads]) for h in range(SLOTS)] if table is None else None
        idx_s = [s.sb(f"idx_s{h}", [EC, BATCH], I32) for h in range(SLOTS)] if table is not None else None
        rows = [s.sb(f"rows{h}", [EC, BATCH * stride]) for h in range(SLOTS)] if table is not None else None
        away = [s.sb(f"away{h}", [EC, BATCH * 128]) for h in range(SLOTS)]
        shifted = [s.sb(f"shifted{h}", [EC, BATCH * heads * 128]) for h in range(2)]
        top = [s.sb(f"top{h}", [P, BATCH * heads]) for h in range(2)]
        ps = [s.ps(f"ps{u}", [P, heads * EC]) for u in range(BATCH)]
        landed = [s.sem(f"landed{h}") for h in range(SLOTS)] if table is not None else None
        staged, go, merges = s.sem("staged"), s.sem("go"), s.sem("merges")
        aways, by_s, by_v, merged = s.sem("aways"), s.sem("by_s"), s.sem("by_v"), s.sem("merged")
        kept = s.sem("kept")
        turned = [s.sem(f"turned{u}") for u in range(BATCH)]
        reduced = [s.sem(f"reduced{u}") for u in range(BATCH)]

        def value(st, u, h):
            if table is None:
                return val_s[st.slot][:, u * heads + h:u * heads + h + 1]
            return rows[st.slot][:, (u + 1) * stride - heads + h:(u + 1) * stride - heads + h + 1]

        def of_values(st, h0):
            if table is None:
                return val_s[st.slot][:].rearrange("p (u h) -> p u h", u=BATCH)[:, :, h0:heads]
            return rows[st.slot][:].rearrange("p (u f) -> p u f", u=BATCH)[:, :, stride - heads + h0:stride]

        def pieces(st):
            return shifted[st.slot % 2][:].rearrange("p (u h n) -> p u h n", u=BATCH, h=heads)

        def there(eng, st):
            if table is None:
                eng.wait_ge(staged, 2 * st.k + 2)
            else:
                eng.wait_ge(landed[st.slot], 16 * BATCH * (st.turn + 1))

        with s.block() as block:
            @block.scalar
            def _(act):
                act.sem_inc(by_s, SLOTS)
                if table is not None:
                    act.sem_inc(kept, SLOTS)

                def stage(st):
                    act.wait_ge(aways, done(st, SLOTS))
                    act.wait_ge(by_v, done(st, SLOTS))
                    act.wait_ge(by_s, done(st, SLOTS))
                    if table is None:
                        nc.scalar.copy(val_s[st.slot][:], values[:, st.chunks(stride)]).then_inc(staged, 1)
                        nc.scalar.copy(rec_s[st.slot][:], rec[:, st.chunks(FIELDS)]).then_inc(staged, 1)
                    else:
                        stage_records(nc, act, rec, rec_s, idx_s, staged, st)

                def body(st):
                    there(act, st)
                    act.wait_ge(aways, done(st))
                    for u in range(BATCH):
                        if u == 0:
                            act.wait_ge(turned[BATCH - 1], done(st, 2))
                        for h in range(by_act):
                            ins = nc.scalar.activation(pieces(st)[:, u, h, 0:P], away[st.slot][:, u * 128:u * 128 + P],
                                                       ACT.Identity, bias=value(st, u, h), scale=1.0)
                    ins.then_inc(by_s, 1)
                    if table is not None:
                        nc.scalar.copy(stored[:, st.chunks(stride)], rows[st.slot][:]).then_inc(kept, 1)
                    with_ahead(st, 3, steps, stage)

                for k in range(3):
                    stage(Step(0, k))
                edge_steps(act, steps, body)

            if table is not None:
                @block.gpsimd
                def _(pool):
                    def body(st):
                        pool.wait_ge(staged, 2 * st.k + 2)
                        pool.sem_inc(go, 1)
                        pool.wait_ge(kept, done(st, SLOTS))
                        pool.sem_inc(go, 1)
                        pool.wait_ge(by_v, done(st, SLOTS))
                        pool.sem_inc(go, 1)
                        for u in range(BATCH):
                            pool.indirect_dma_start(rows[st.slot][:, u * stride:(u + 1) * stride], None, table,
                                                    bass.IndirectOffsetOnAxis(ap=idx_s[st.slot][:, u:u + 1], axis=0)
                                                    ).then_inc(landed[st.slot], 16)
                    edge_steps(pool, steps, body)

            @block.vector
            def _(dve):
                for sem in (aways, by_v, merged, *reduced):
                    dve.sem_inc(sem, SLOTS)

                def make(st):
                    dve.wait_ge(staged, 2 * st.k + 2)
                    dve.wait_ge(by_s, done(st, SLOTS))
                    for u in range(BATCH):
                        ins = nc.vector.tensor_scalar(away[st.slot][:, u * 128:u * 128 + P], c["iota"][:, 0:P],
                                                      rec_s[st.slot][:, u * FIELDS + 1:u * FIELDS + 2], -BIG,
                                                      ALU.not_equal, ALU.mult)
                    ins.then_inc(aways, 1)

                def shift(st):
                    there(dve, st)
                    dve.wait_ge(aways, done(st))
                    dve.wait_ge(turned[BATCH - 1], done(st, 2))
                    for u in range(BATCH):
                        ins = nc.vector.tensor_tensor(
                            pieces(st)[:, u, by_act:heads, 0:P],
                            away[st.slot][:, u * 128:u * 128 + P].unsqueeze(1).broadcast_to([EC, heads - by_act, P]),
                            of_values(st, by_act)[:, u, :].unsqueeze(2).broadcast_to([EC, heads - by_act, P]), ALU.add)
                    ins.then_inc(by_v, 1)

                def body(st):
                    with_ahead(st, 2, steps, make)
                    with_ahead(st, 1, steps, shift)
                    tiles = tiles_of(nc, dve, mybir.EngineType.DVE, blk, st)
                    for u in range(BATCH):
                        dve.wait_ge(turned[u], done(st))
                        nc.vector.tensor_reduce(top[st.slot % 2][:, u * heads:(u + 1) * heads],
                                                ps[u][:].rearrange("p (h e) -> p h e", e=EC),
                                                AX.X, ALU.max).then_inc(reduced[u], 1)
                    dve.wait_ge(reduced[BATCH - 1], done(st))
                    for u, b in enumerate(tiles):
                        to = best[:, bass.ds(b * heads, heads)]
                        last = u == BATCH - 1
                        nc.vector.tensor_tensor(to, to, top[st.slot % 2][:, u * heads:(u + 1) * heads], ALU.max
                                                ).then_inc(merged if last else merges, 1)
                        dve.wait_ge(merged if last else merges, done(st) if last else (BATCH - 1) * st.k + u + 1)

                for k in range(2):
                    make(Step(0, k))
                shift(Step(0, 0))
                edge_steps(dve, steps, body)

            @block.tensor
            def _(pe):
                for sem in turned:
                    pe.sem_inc(sem, SLOTS)

                def body(st):
                    pe.wait_ge(by_s, done(st))
                    pe.wait_ge(by_v, done(st))
                    for u in range(BATCH):
                        pe.wait_ge(reduced[u], done(st, 1))
                        for h in range(heads):
                            ins = nc.tensor.transpose(ps[u][:, h * EC:(h + 1) * EC], pieces(st)[:, u, h, 0:P], c["ident"][:])
                        ins.then_inc(turned[u], 1)
                edge_steps(pe, steps, body)


def softmax_sum(nc, c, name, heads, hd, rec, blk, chunks, acc, per_node, pn, table, scores, stored, leaky):
    vw = heads * hd
    wide = vw + heads
    steps = chunks // BATCH
    with Stage(nc, name) as s:
        rec_s = [s.sb(f"rec_s{h}", [EC, BATCH * FIELDS]) for h in range(SLOTS)]
        idx_s = [s.sb(f"idx_s{h}", [EC, BATCH], I32) for h in range(SLOTS)] if table is not None else None
        rows = [s.sb(f"rows{h}", [EC, BATCH * vw]) for h in range(SLOTS)] if table is not None else None
        oh = [s.sb(f"oh{h}", [EC, BATCH * 128]) for h in range(SLOTS)]
        oht = [s.sb(f"oht{h}", [P, BATCH * EC]) for h in range(2)]
        arg = [s.sb(f"arg{h}", [EC, BATCH * heads]) for h in range(SLOTS)]
        arg2 = s.sb("partial", [EC, BATCH * heads])
        msg = [s.sb(f"msg{h}", [EC, BATCH * wide]) for h in range(SLOTS)]
        ps_t = [s.ps(f"ps_t{h}", [P, 512]) for h in range(2)]
        ps_n = [s.ps(f"ps_n{h}", [EC, 512]) for h in range(2)]
        ps_a = s.ps("ps_a", [P, BATCH * 512])
        landed = [s.sem(f"landed{h}") for h in range(SLOTS)]
        staged, zeroed, go, inner = s.sem("staged"), s.sem("zeroed"), s.sem("go"), s.sem("inner")
        onehots, turned, kept, spread = s.sem("onehots"), s.sem("turned"), s.sem("kept"), s.sem("spread")
        args, exps, msgs = s.sem("args"), s.sem("exps"), s.sem("msgs")
        summed = [s.sem(f"summed{u}") for u in range(BATCH)]
        added = [s.sem(f"added{u}") for u in range(BATCH)]

        def weights(st):
            return msg[st.slot][:].rearrange("p (u f) -> p u f", u=BATCH)[:, :, vw:wide]

        with s.block() as block:
            @block.scalar
            def _(act):
                act.sem_inc(kept, SLOTS)
                act.sem_inc(exps, SLOTS)

                def stage(st):
                    act.wait_ge(onehots, done(st, SLOTS))
                    if table is not None:
                        act.wait_ge(msgs, done(st, SLOTS))
                    stage_records(nc, act, rec, rec_s, idx_s, staged, st)

                def keep(st):
                    act.wait_ge(turned, done(st))
                    act.wait_ge(spread, done(st, 2))
                    nc.scalar.copy(oht[st.slot % 2][:], ps_t[st.slot % 2][:]).then_inc(kept, 1)

                def exponentiate(st):
                    act.wait_ge(args, done(st))
                    act.wait_ge(summed[BATCH - 1], done(st, SLOTS))
                    nc.scalar.activation(weights(st), arg[st.slot][:].rearrange("p (u h) -> p u h", u=BATCH),
                                         ACT.Exp).then_inc(exps, 1)

                def body(st):
                    with_ahead(st, 3, steps, keep)
                    with_ahead(st, 2, steps, exponentiate)
                    with_ahead(st, 4, steps, stage)

                for k in range(4):
                    stage(Step(0, k))
                for k in range(3):
                    keep(Step(0, k))
                for k in range(2):
                    exponentiate(Step(0, k))
                edge_steps(act, steps, body)

            if table is not None:
                @block.gpsimd
                def _(pool):
                    gather_rows(nc, pool, steps, table, idx_s, rows, vw, staged, msgs, landed, go)

            @block.vector
            def _(dve):
                for sem in (onehots, args, msgs, *added):
                    dve.sem_inc(sem, SLOTS)
                nc.vector.memset(acc[:], 0.0).then_inc(zeroed, 1)
                dve.wait_ge(zeroed, 1)

                def make(st):
                    dve.wait_ge(staged, 2 * st.k + 2)
                    dve.wait_ge(summed[BATCH - 1], done(st, SLOTS))
                    one_hots(nc, c, oh, rec_s, st).then_inc(onehots, 1)

                def argue(st):
                    dve.wait_ge(spread, done(st))
                    dve.wait_ge(exps, done(st, SLOTS))
                    node = ps_n[st.slot % 2][:, 0:BATCH * pn].rearrange("p (u f) -> p u f", u=BATCH)
                    w = arg[st.slot][:].rearrange("p (u h) -> p u h", u=BATCH)
                    a = arg2[:].rearrange("p (u h) -> p u h", u=BATCH)
                    if not leaky:
                        nc.vector.tensor_tensor(w, scores[:, st.chunks(heads)].rearrange("p (u h) -> p u h", u=BATCH), node,
                                                ALU.subtract).then_inc(args, 1)
                        return
                    from_source = stored[:, st.chunks(wide)].rearrange("p (u f) -> p u f", u=BATCH)[:, :, vw:wide]
                    nc.vector.tensor_tensor(a, from_source, node[:, :, 0:heads], ALU.add).then_inc(inner, 1)
                    dve.wait_ge(inner, 3 * st.k + 1)
                    nc.vector.scalar_tensor_tensor(w, a, 0.2, a, ALU.mult, ALU.max).then_inc(inner, 1)
                    dve.wait_ge(inner, 3 * st.k + 2)
                    nc.vector.tensor_tensor(a, w, node[:, :, heads:2 * heads], ALU.subtract).then_inc(inner, 1)
                    dve.wait_ge(inner, 3 * st.k + 3)
                    nc.vector.tensor_scalar(w, a, 0.0, None, ALU.min).then_inc(args, 1)
                    dve.wait_ge(args, done(st))

                def multiply(st):
                    dve.wait_ge(exps, done(st))
                    if table is not None:
                        dve.wait_ge(landed[st.slot], 16 * BATCH * (st.turn + 1))
                        vals = rows[st.slot][:].rearrange("p (u f) -> p u f", u=BATCH)
                    else:
                        vals = stored[:, st.chunks(wide)].rearrange("p (u f) -> p u f", u=BATCH)[:, :, 0:vw]
                    nc.vector.tensor_tensor(
                        msg[st.slot][:].rearrange("p (u f) -> p u f", u=BATCH)[:, :, 0:vw].rearrange("p u (h d) -> p u h d", d=hd),
                        vals.rearrange("p u (h d) -> p u h d", d=hd),
                        weights(st).unsqueeze(3).broadcast_to([EC, BATCH, heads, hd]), ALU.mult).then_inc(msgs, 1)

                def body(st):
                    with_ahead(st, 3, steps, make)
                    with_ahead(st, 2, steps, argue)
                    with_ahead(st, 1, steps, multiply)
                    tiles = tiles_of(nc, dve, mybir.EngineType.DVE, blk, st)
                    for u, b in enumerate(tiles):
                        dve.wait_ge(summed[u], done(st))
                        to = acc[:, bass.ds(b * wide, wide)]
                        nc.vector.tensor_tensor(to, to, ps_a[:, u * 512:u * 512 + wide], ALU.add).then_inc(added[u], 1)
                        dve.wait_ge(added[u], done(st))

                for k in range(3):
                    make(Step(0, k))
                for k in range(2):
                    argue(Step(0, k))
                multiply(Step(0, 0))
                edge_steps(dve, steps, body)

            @block.tensor
            def _(pe):
                for sem in (turned, spread, *summed):
                    pe.sem_inc(sem, SLOTS)

                def turn(st):
                    pe.wait_ge(onehots, done(st))
                    pe.wait_ge(kept, done(st, 2))
                    turn_one_hots(nc, c, ps_t, oh, st).then_inc(turned, 1)

                def node_rows(st):
                    tiles = tiles_of(nc, pe, mybir.EngineType.PE, blk, st)
                    pe.wait_ge(kept, done(st))
                    pe.wait_ge(args, done(st, 2))
                    for u, b in enumerate(tiles):
                        ins = nc.tensor.matmul(ps_n[st.slot % 2][:, u * pn:(u + 1) * pn], oht[st.slot % 2][:, u * EC:(u + 1) * EC],
                                               per_node[:, bass.ds(b * pn, pn)], start=True, stop=True)
                    ins.then_inc(spread, 1)

                def body(st):
                    with_ahead(st, 3, steps, turn)
                    with_ahead(st, 2, steps, node_rows)
                    pe.wait_ge(msgs, done(st))
                    for u in range(BATCH):
                        pe.wait_ge(added[u], done(st, 1))
                        nc.tensor.matmul(ps_a[:, u * 512:u * 512 + wide], oh[st.slot][:, u * 128:u * 128 + P],
                                         msg[st.slot][:, u * wide:(u + 1) * wide], start=True, stop=True).then_inc(summed[u], 1)

                for k in range(3):
                    turn(Step(0, k))
                    if k < 2:
                        node_rows(Step(0, k))
                edge_steps(pe, steps, body)



def tiles_loop(eng, body):
    with eng.Fori(0, T // RING) as i:
        for u in range(RING):
            body(i * RING + u, u)


def layernorm(nc, name, src, dst, gamma=None, beta=None):
    with Stage(nc, name) as s:
        stats = s.sb("stats", [P, T * 6])
        mv = s.sb("mv", [P, T * 2])
        var = s.sb("var", [P, T])
        std = s.sb("std", [P, T])
        rstd = s.sb("rstd", [P, T])
        gb = s.sb("gb", [P, 2 * D]) if gamma is not None else None
        loaded, steps, eps_added, rooted = s.sem("loaded"), s.sem("steps"), s.sem("eps_added"), s.sem("rooted")
        with s.block() as block:
            if gamma is not None:
                @block.sync
                def _(sp):
                    sp.dma_start(gb[:, 0:D], gamma.partition_broadcast(P)).then_inc(loaded, 16)
                    sp.dma_start(gb[:, D:2 * D], beta.partition_broadcast(P)).then_inc(loaded, 16)

            @block.scalar
            def _(act):
                act.wait_ge(eps_added, 1)
                nc.scalar.activation(std[:], var[:], ACT.Sqrt).then_inc(rooted, 1)

            @block.vector
            def _(dve):
                step = Steps(dve, steps)
                tiles_loop(dve, lambda t, u: nc.vector.bn_stats(stats[:, tile_of(t, 6)], src[:, tile_of(t, D)]
                                                                ).then_inc(steps, 1))
                step.n = T
                dve.wait_ge(steps, T)
                for t in range(T):
                    nc.vector.bn_aggr(mv[:, 2 * t:2 * t + 2], stats[:, 6 * t:6 * t + 6]).then_inc(steps, 1)
                step.n = 2 * T
                dve.wait_ge(steps, 2 * T)
                mv2 = mv[:].rearrange("p (t k) -> p t k", k=2)
                nc.vector.tensor_scalar(var[:], mv2[:, :, 1], EPS, None, ALU.add).then_inc(eps_added, 1)
                dve.wait_ge(rooted, 1)
                step(nc.vector.reciprocal(rstd[:], std[:]))
                tiles_loop(dve, lambda t, u: nc.vector.tensor_scalar(
                    dst[:, tile_of(t, D)], src[:, tile_of(t, D)], mv[:, bass.ds(2 * t, 1)], rstd[:, bass.ds(t, 1)],
                    ALU.subtract, ALU.mult).then_inc(steps, 1))
                step.n += T
                dve.wait_ge(steps, step.n)
                if gamma is not None:
                    dve.wait_ge(loaded, 32)
                    full = as_tiles(dst, D)
                    step(nc.vector.tensor_tensor(full, full, gb[:, 0:D].unsqueeze(1).broadcast_to([P, T, D]), ALU.mult))
                    step(nc.vector.tensor_tensor(full, full, gb[:, D:2 * D].unsqueeze(1).broadcast_to([P, T, D]), ALU.add))


def turn_tiles(nc, c, name, src, width, dst, stride=None, scale=None):
    stride = stride or width
    cw = min(width, 128)
    nch = width // cw
    with Stage(nc, name) as s:
        tile = [s.sb(f"tile{u}", [P, width]) for u in range(RING)]
        ps = [s.ps(f"ps{u}", [cw, nch * P]) for u in range(RING)]
        copied = s.sem("copied")
        turned = s.sem("turned")
        stored = s.sem("stored")
        go = s.sem("go")
        with s.block() as block:
            @block.scalar
            def _(act):
                def body(t, u):
                    act.wait_ge(turned, t + 1)
                    nc.scalar.copy(tile[u][:], src[:, bass.ds(t * stride, width)]).then_inc(copied, 1)
                tiles_loop(act, body)

            @block.tensor
            def _(pe):
                pe.sem_inc(turned, RING)

                def body(t, u):
                    pe.wait_ge(copied, t + 1)
                    pe.wait_ge(stored, t + 1)
                    pe.sem_inc(go, 1)
                    for k in range(nch):
                        ins = nc.tensor.transpose(ps[u][:, k * P:(k + 1) * P], tile[u][:, k * cw:(k + 1) * cw],
                                                  c["ident"][0:P, 0:P])
                    ins.then_inc(turned, 1)
                tiles_loop(pe, body)

            @block.vector
            def _(dve):
                dve.sem_inc(stored, RING)

                def body(t, u):
                    dve.wait_ge(turned, RING + t + 1)
                    for k in range(nch):
                        ins = nc.vector.tensor_copy(dst[0:cw, bass.ds(t * P + k * N, P)], ps[u][:, k * P:(k + 1) * P])
                    ins.then_inc(stored, 1)
                tiles_loop(dve, body)


def project(nc, c, name, sources, wide, mode, dst, bias=None, scale=None, stride=None):
    stride = stride or wide
    with Stage(nc, name) as s:
        w = [s.sb(f"w{k}", [kp, wide]) for k, (_, kp, _, _) in enumerate(sources)]
        lhs = [s.sb(f"lhs{u}", [128, len(sources) * P]) for u in range(RING)]
        brow = s.sb("brow", [1, wide]) if bias is not None else None
        ps = [s.ps(f"ps{u}", [P, 512]) for u in range(RING)]
        loaded = s.sem("loaded")
        copied = s.sem("copied")
        multiplied = s.sem("multiplied")
        stored = s.sem("stored")
        with s.block() as block:
            @block.sync
            def _(sp):
                for k, (_, _, _, wd) in enumerate(sources):
                    sp.dma_start(w[k][:], wd).then_inc(loaded, 16)
                if bias is not None:
                    sp.dma_start(brow[:], bias).then_inc(loaded, 16)

            @block.scalar
            def _(act):
                def body(t, u):
                    act.wait_ge(multiplied, t + 1)
                    for k, (src, kp, ch, _) in enumerate(sources):
                        nc.scalar.copy(lhs[u][0:kp, k * P:(k + 1) * P], src[0:kp, bass.ds(t * P + ch * N, P)]).then_inc(copied, 1)
                tiles_loop(act, body)

            @block.tensor
            def _(pe):
                pe.sem_inc(multiplied, RING)
                pe.wait_ge(loaded, 16 * (len(sources) + (bias is not None)))

                def body(t, u):
                    pe.wait_ge(copied, (t + 1) * len(sources))
                    pe.wait_ge(stored, t + 1)
                    if bias is not None:
                        nc.tensor.matmul(ps[u][:, 0:wide], c["ones"][0:1, 0:P], brow[:], start=True, stop=False)
                    for k, (_, kp, _, _) in enumerate(sources):
                        ins = nc.tensor.matmul(ps[u][:, 0:wide], lhs[u][0:kp, k * P:(k + 1) * P], w[k][:],
                                               start=(k == 0 and bias is None), stop=(k == len(sources) - 1))
                    ins.then_inc(multiplied, 1)
                tiles_loop(pe, body)

            @block.vector
            def _(dve):
                dve.sem_inc(stored, RING)

                def body(t, u):
                    dve.wait_ge(multiplied, RING + t + 1)
                    out = ps[u][:, 0:wide]
                    to = dst[:, bass.ds(t * stride, wide)]
                    if mode == "copy":
                        ins = nc.vector.tensor_copy(to, out)
                    elif mode == "scale":
                        ins = nc.vector.tensor_scalar(to, out, scale[:, bass.ds(t, 1)], None, ALU.mult)
                    elif mode == "add":
                        ins = nc.vector.tensor_tensor(to, to, out, ALU.add)
                    elif mode == "relu_add":
                        ins = nc.vector.scalar_tensor_tensor(to, out, 0.0, to, ALU.max, ALU.add)
                    ins.then_inc(stored, 1)
                tiles_loop(dve, body)



def network(nc, c, name, xt, experts, hidden, act_fn, w1_d, b1_d, w2_d, b2_d, gate, acc, picked=None):
    fc = hidden // 128
    jh = fc // 2
    twin = min(experts, 2)
    steps_per = T // RING
    PRIME = 4 * steps_per
    with Stage(nc, name) as s:
        w1 = [s.sb(f"w1_{e}", [128, DC * hidden]) for e in range(twin)]
        w2 = [s.sb(f"w2_{e}", [128, fc * D]) for e in range(twin)]
        b1 = s.sb("b1", [128, experts * fc])
        b2 = s.sb("b2", [experts, D])
        gt = s.sb("gt", [experts, RING * P]) if gate is not None else None
        gs = [s.sb(f"gs{u}", [P, experts]) for u in range(RING)] if gate is not None else None
        h = [s.sb(f"h{q}", [128, jh * GROUP]) for q in range(2)]
        ps_h = [s.ps(f"ps_h{r}", [128, 1024]) for r in range(2)]
        ps_y = s.ps("ps_y", [P, 3 * 512])
        w_in = [s.sem(f"w_in{e}") for e in range(twin)]
        small = s.sem("small")
        hidden_ready = s.sem("hidden_ready")
        activated = s.sem("activated")
        multiplied = s.sem("multiplied")
        summed = s.sem("summed")
        go, g_copied, g_turned, g_kept, biased, bias_kept = (s.sem(n) for n in (
            "go", "g_copied", "g_turned", "g_kept", "biased", "bias_kept"))

        def ycols(k):
            return ps_y[:, (k // 2) * 512 + (k % 2) * D:(k // 2) * 512 + (k % 2) * D + D]

        with s.block() as block:
            @block.sync
            def _(sp):
                def weights_of(ex):
                    if picked is None:
                        return ex
                    return sp.value_load(picked[0:1, bass.ds(ex, 1)], min_val=0, max_val=w1_d.shape[0] - 1)

                for k in range(experts):
                    ex = weights_of(k)
                    sp.dma_start(b1[:, k * fc:(k + 1) * fc], b1_d[bass.ds(ex, 1), :, :].rearrange("e p f -> (e p) f")).then_inc(small, 16)
                    sp.dma_start(b2[k:k + 1, :], b2_d[bass.ds(ex, 1), :]).then_inc(small, 16)
                with sp.Fori(0, experts // twin) as eo:
                    for e in range(twin):
                        ex = eo * twin + e
                        into = weights_of(ex)
                        sp.wait_ge(multiplied, 2 * steps_per * (ex + 1))
                        sp.dma_start(w1[e][:], w1_d[bass.ds(into, 1), :, :].rearrange("e p f -> (e p) f")).then_inc(w_in[e], 16)
                        sp.dma_start(w2[e][:], w2_d[bass.ds(into, 1), :, :].rearrange("e p f -> (e p) f")).then_inc(w_in[e], 16)

            @block.scalar
            def _(act):
                act.sem_inc(activated, 2)
                act.wait_ge(small, 32 * experts)
                if gate is not None:
                    def copy_gate(t, u):
                        act.wait_ge(g_turned, t + 1)
                        nc.scalar.copy(gs[u][:], gate[0:P, bass.ds(t * experts, experts)]).then_inc(g_copied, 1)
                    tiles_loop(act, copy_gate)
                with act.Fori(0, experts // twin) as eo:
                    for e in range(twin):
                        ex = eo * twin + e
                        with act.Fori(0, steps_per) as g:
                            st = ex * steps_per + g
                            for q in range(2):
                                act.wait_ge(multiplied, PRIME + 2 * st + q - 1)
                                for j in range(jh):
                                    act.wait_ge(hidden_ready, 2 * jh * st + q * jh + j + 1)
                                    for m, (m0, mn) in enumerate(PIECES):
                                        ins = nc.scalar.activation(
                                            h[q][:, j * GROUP + m0:j * GROUP + m0 + mn],
                                            ps_h[j % 2][:, 512 * m:512 * m + mn], act_fn,
                                            bias=b1[:, bass.ds(ex * fc + q * jh + j, 1)])
                                    ins.then_inc(activated, 1)

            @block.tensor
            def _(pe):
                pe.sem_inc(multiplied, PRIME)
                pe.wait_ge(small, 32 * experts)
                if gate is not None:
                    pe.sem_inc(g_turned, RING)

                    def bias_part(t, u):
                        pe.wait_ge(g_copied, t + 1)
                        pe.wait_ge(bias_kept, t + 1)
                        nc.tensor.transpose(ps_h[0][0:experts, 0:P], gs[u][:], c["ident"][0:P, 0:P]).then_inc(g_turned, 1)
                        pe.wait_ge(g_kept, t + 1)
                        nc.tensor.matmul(ps_h[1][0:P, 0:D], gt[:, u * P:(u + 1) * P], b2[:], start=True, stop=True).then_inc(biased, 1)
                    tiles_loop(pe, bias_part)
                    pe.wait_ge(bias_kept, T + 1)
                with pe.Fori(0, experts // twin) as eo:
                    for e in range(twin):
                        ex = eo * twin + e
                        pe.wait_ge(w_in[e], 32 * (eo + 1))
                        pe.sem_inc(go, 1)
                        with pe.Fori(0, steps_per) as g:
                            st = ex * steps_per + g
                            for q in range(2):
                                for j in range(jh):
                                    pe.wait_ge(activated, 2 * jh * st + q * jh + j + 1)
                                    f0 = (q * jh + j) * 128
                                    for m, (m0, mn) in enumerate(PIECES):
                                        for k in range(DC):
                                            ins = nc.tensor.matmul(
                                                ps_h[j % 2][:, 512 * m:512 * m + mn],
                                                w1[e][:, k * hidden + f0:k * hidden + f0 + 128],
                                                xt[:, bass.ds(g * GROUP + (k * N + m0), mn)],
                                                start=(k == 0), stop=(k == DC - 1))
                                    ins.then_inc(hidden_ready, 1)
                            for q in range(2):
                                pe.wait_ge(activated, 2 + 2 * jh * st + (q + 1) * jh)
                                if q == 0:
                                    pe.wait_ge(summed, st + 1)
                                for k in range(RING):
                                    for j in range(jh):
                                        ins = nc.tensor.matmul(
                                            ycols(k), h[q][:, j * GROUP + k * P:j * GROUP + (k + 1) * P],
                                            w2[e][:, (q * jh + j) * D:(q * jh + j + 1) * D],
                                            start=(q == 0 and j == 0 and k % 2 == 0), stop=(q == 1 and j == jh - 1),
                                            skip_group_check=True)
                                ins.then_inc(multiplied, 1)

            @block.vector
            def _(dve):
                dve.sem_inc(summed, 1)
                dve.wait_ge(small, 32 * experts)
                if gate is not None:
                    dve.sem_inc(bias_kept, 1)

                    def keep_bias(t, u):
                        dve.wait_ge(g_turned, RING + t + 1)
                        nc.vector.tensor_copy(gt[:, u * P:(u + 1) * P], ps_h[0][0:experts, 0:P]).then_inc(g_kept, 1)
                        dve.wait_ge(biased, t + 1)
                        nc.vector.tensor_copy(acc[:, tile_of(t, D)], ps_h[1][0:P, 0:D]).then_inc(bias_kept, 1)
                    tiles_loop(dve, keep_bias)
                    dve.wait_ge(bias_kept, T + 1)
                with dve.Fori(0, experts) as ex:
                    with dve.Fori(0, steps_per) as g:
                        st = ex * steps_per + g
                        dve.wait_ge(multiplied, PRIME + 2 * st + 2)
                        dve.wait_ge(summed, st + 1)
                        for k in range(RING):
                            to = acc[:, bass.ds(g * (RING * D) + k * D, D)]
                            if gate is None:
                                ins = nc.vector.tensor_copy(to, ycols(k))
                            else:
                                ins = nc.vector.scalar_tensor_tensor(
                                    to, ycols(k), gate[0:P, bass.ds(g * (RING * experts) + k * experts + ex, 1)], to,
                                    ALU.mult, ALU.add)
                        ins.then_inc(summed, 1)



ST = 128


def pair_loop(eng, groups, body):
    body(0, True, False)
    with eng.Fori(1, groups // 2 - 1) as i:
        body(i, False, False)
    body(groups // 2 - 1, False, True)


def dispatch(nc, c, name, picks, experts, tiles, groups, capacity, slot_d, slots, which, pos, kept):
    g = tiles * ST
    q = groups * tiles
    wide = T * experts
    with Stage(nc, name) as s:
        sel, inside, totals, before, rank, tmp = (s.sb(k, [P, wide]) for k in ("sel", "inside", "totals", "before", "rank", "tmp"))
        zeros, past, lost = s.sb("zeros", [P, T]), s.sb("past", [P, T]), s.sb("lost", [P, T])
        ends, ng, start = s.sb("ends", [P, experts]), s.sb("ng", [P, experts]), s.sb("start", [P, experts])
        posf, row_f, lin = s.sb("posf", [P, T]), s.sb("row_f", [P, T]), s.sb("lin", [P, T])
        row_i, slot_i, node_i = s.sb("row_i", [P, T], I32), s.sb("slot_i", [P, T], I32), s.sb("node_i", [P, T], I32)
        to_i = [s.sb(f"to_i{k}", [P, T], I32) for k in range(len(picks))]
        blank = s.sb("blank", [ST, q], I32)
        giter, which_f = s.sb("giter", [1, groups]), s.sb("which_f", [1, groups])
        upto = s.sb("upto", [P, P])
        ps = [s.ps(f"ps{k}", [P, 512]) for k in range(2)]
        steps, made, hot, counted, ready, blanked, sent, back = (s.sem(k) for k in (
            "steps", "made", "hot", "counted", "ready", "blanked", "sent", "back"))

        def view(x):
            return x[:].rearrange("p (t e) -> p t e", e=experts)

        def per_expert(x):
            return x[:].unsqueeze(1).broadcast_to([P, T, experts])

        with s.block() as block:
            @block.sync
            def _(sp):
                sp.wait_ge(made, 6)
                sp.dma_start(slot_d[0:ST * q, :].rearrange("(p c) f -> p (c f)", p=ST), blank[:]).then_inc(blanked, 16)
                sp.wait_ge(sent, 16 * T * len(picks))
                sp.dma_start(slots[:], slot_d[0:ST * q, :].rearrange("(p c) f -> p (c f)", p=ST)).then_inc(back, 16)
                sp.wait_ge(back, 16)

            @block.gpsimd
            def _(pool):
                nc.gpsimd.memset(upto[:], 1.0).then_inc(made, 1)
                nc.gpsimd.memset(blank[:], 0).then_inc(made, 1)
                nc.gpsimd.iota(node_i[:], pattern=[[P, T]], base=0, channel_multiplier=1).then_inc(made, 1)
                nc.gpsimd.iota(past[:], pattern=[[P, T]], base=ST * q, channel_multiplier=1,
                               allow_small_or_imprecise_dtypes=True).then_inc(made, 1)
                nc.gpsimd.iota(giter[:], pattern=[[1, groups]], base=0, channel_multiplier=0,
                               allow_small_or_imprecise_dtypes=True).then_inc(made, 1)
                pool.wait_ge(made, 5)
                nc.gpsimd.affine_select(out=upto[:], in_=upto[:], compare_op=ALU.is_ge, fill=0.0, base=0,
                                        pattern=[[1, P]], channel_multiplier=-1).then_inc(made, 1)
                pool.wait_ge(blanked, 16)
                pool.wait_ge(ready, 1)
                for k in range(len(picks)):
                    for t in range(T):
                        pool.indirect_dma_start(slot_d, bass.IndirectOffsetOnAxis(ap=to_i[k][:, t:t + 1], axis=0),
                                                node_i[:, t:t + 1], None).then_inc(sent, 16)

            @block.tensor
            def _(pe):
                pe.wait_ge(made, 6)
                pe.wait_ge(hot, 1)
                nc.tensor.matmul(ps[0][:, 0:wide], upto[:], sel[:], start=True, stop=True).then_inc(counted, 1)
                nc.tensor.matmul(ps[1][:, 0:wide], c["ones"][0:P, 0:P], sel[:], start=True, stop=True).then_inc(counted, 1)

            @block.vector
            def _(dve):
                step = Steps(dve, steps)
                V = nc.vector
                step(V.memset(zeros[:], 0.0))
                step(V.tensor_copy(sel[:], picks[0][:]))
                for k in picks[1:]:
                    step(V.tensor_tensor(sel[:], sel[:], k[:], ALU.add))
                dve.sem_inc(hot, 1)
                dve.wait_ge(counted, 2)
                step(V.tensor_copy(inside[:], ps[0][:, 0:wide]))
                step(V.tensor_copy(totals[:], ps[1][:, 0:wide]))
                for e in range(experts):
                    step(V.tensor_tensor_scan(view(before)[:, :, e], zeros[:], view(totals)[:, :, e], 0.0, ALU.add, ALU.add))
                step(V.tensor_tensor(rank[:], before[:], totals[:], ALU.subtract))
                step(V.tensor_tensor(rank[:], rank[:], inside[:], ALU.add))
                step(V.tensor_scalar(rank[:], rank[:], -1.0, None, ALU.add))
                if capacity is None:
                    step(V.tensor_copy(ends[:], view(before)[:, T - 1, :]))
                    step(V.memset(ng[:], 0.0))
                    for k in range(-(-N // g)):
                        step(V.scalar_tensor_tensor(ng[:], ends[:], float(k * g), ng[:], ALU.is_gt, ALU.add))
                    step(V.tensor_tensor_scan(ends[:], zeros[:, 0:experts], ng[:], 0.0, ALU.add, ALU.add))
                    step(V.tensor_tensor(start[:], ends[:], ng[:], ALU.subtract))
                    step(V.memset(which_f[:], -1.0))
                    for e in range(experts):
                        step(V.scalar_tensor_tensor(which_f[:], giter[:], start[0:1, e:e + 1], which_f[:], ALU.is_ge, ALU.add))
                    step(V.tensor_copy(which[:], which_f[:]))
                else:
                    for e in range(experts):
                        step(V.memset(start[:, e:e + 1], float(e)))
                step(V.tensor_scalar(start[:], start[:], float(g), None, ALU.mult))
                step(V.tensor_tensor(view(sel), view(rank), per_expert(start), ALU.add))
                dve.wait_ge(made, 6)
                for k, pick in enumerate(picks):
                    step(V.tensor_tensor(tmp[:], sel[:], pick[:], ALU.mult))
                    step(V.tensor_reduce(posf[:], view(tmp), AX.X, ALU.add))
                    if capacity is not None:
                        step(V.scalar_tensor_tensor(tmp[:], rank[:], float(capacity), pick[:], ALU.is_lt, ALU.mult))
                        step(V.tensor_reduce(kept[:], view(tmp), AX.X, ALU.add))
                        step(V.tensor_tensor(posf[:], posf[:], kept[:], ALU.mult))
                    step(V.tensor_copy(pos[k][:], posf[:]))
                    step(V.tensor_scalar(row_i[:], pos[k][:], ST - 1, None, ALU.bitwise_and))
                    step(V.tensor_scalar(slot_i[:], pos[k][:], 7, None, ALU.arith_shift_right))
                    step(V.tensor_copy(row_f[:], row_i[:]))
                    step(V.tensor_copy(posf[:], slot_i[:]))
                    step(V.scalar_tensor_tensor(lin[:], row_f[:], float(q), posf[:], ALU.mult, ALU.add))
                    if capacity is not None:
                        step(V.scalar_tensor_tensor(lost[:], kept[:], 0.0, past[:], ALU.is_equal, ALU.mult))
                        step(V.tensor_tensor(lin[:], lin[:], kept[:], ALU.mult))
                        step(V.tensor_tensor(lin[:], lin[:], lost[:], ALU.add))
                    step(V.tensor_copy(to_i[k][:], lin[:]))
                dve.sem_inc(ready, 1)


def routed(nc, c, name, y_d, slots, which, hidden, act_fn, w1_d, b1_d, w2_d, b2_d, tiles, groups, out_d):
    fc = hidden // 128
    jh = fc // 2
    g = tiles * ST
    with Stage(nc, name) as s:
        w1 = [s.sb(f"w1_{e}", [128, DC * hidden]) for e in range(2)]
        w2 = [s.sb(f"w2_{e}", [128, fc * D]) for e in range(2)]
        b1 = [s.sb(f"b1_{e}", [128, fc]) for e in range(2)]
        b2 = [s.sb(f"b2_{e}", [ST, D]) for e in range(2)]
        idx = [s.sb(f"idx{e}", [ST, tiles], I32) for e in range(2)]
        rows = [s.sb(f"rows{k}", [ST, D]) for k in range(2 * tiles)]
        xt = [s.sb(f"xt{e}", [128, DC * g]) for e in range(2)]
        h = [s.sb(f"h{q}", [128, jh * g]) for q in range(2)]
        y = [s.sb(f"y{e}", [ST, tiles * D]) for e in range(2)]
        ps_t = [s.ps(f"ps_t{k}", [128, 512]) for k in range(2)]
        ps_h = [s.ps(f"ps_h{k}", [128, 512]) for k in range(2)]
        ps_y = s.ps("ps_y", [ST, tiles // 2 * 512])
        w_in = [s.sem(f"w_in{e}") for e in range(2)]
        landed = [s.sem(f"landed{k}") for k in range(2 * tiles)]
        out_done = [s.sem(f"out_done{e}") for e in range(2)]
        idx_ready, hidden_ready, go = s.sem("idx_ready"), s.sem("hidden_ready"), s.sem("go")
        turned = s.sem("turned")
        kept = s.sem("kept")
        activated = s.sem("activated")
        multiplied = s.sem("multiplied")
        summed = s.sem("summed")

        with s.block() as block:
            @block.sync
            def _(sp):
                def store(i, e):
                    n = 2 * i + e
                    sp.wait_ge(summed, n + 3)
                    sp.sem_inc(go, 1)
                    sp.dma_start(out_d[bass.ds(n * g, g), :].rearrange("(k p) f -> p k f", p=ST),
                                 y[e][:].rearrange("p (k f) -> p k f", f=D)).then_inc(out_done[e], 16)

                def body(i, first, last):
                    for e in range(2):
                        n = 2 * i + e
                        sp.wait_ge(multiplied, 2 * n + 2)
                        sp.sem_inc(go, 1)
                        sp.wait_ge(summed, n + 1)
                        sp.sem_inc(go, 1)
                        if which is None:
                            ex = n
                        else:
                            ex = sp.value_load(which[0:1, bass.ds(n, 1)], min_val=0, max_val=w1_d.shape[0] - 1)
                        for dst, src in ((w1[e], w1_d), (w2[e], w2_d), (b1[e], b1_d)):
                            sp.dma_start(dst[:], src[bass.ds(ex, 1), :, :].rearrange("e p f -> (e p) f")).then_inc(w_in[e], 16)
                        sp.dma_start(b2[e][:], b2_d[bass.ds(ex, 1), :].rearrange("e f -> (e f)").partition_broadcast(ST)).then_inc(w_in[e], 16)
                        if not first:
                            store(i - 1, e)
                pair_loop(sp, groups, body)
                for e in range(2):
                    store(groups // 2 - 1, e)
                for e in range(2):
                    sp.wait_ge(out_done[e], 16 * (groups // 2))

            @block.gpsimd
            def _(pool):
                def body(i, first, last):
                    for e in range(2):
                        n = 2 * i + e
                        pool.wait_ge(turned, tiles * (n + 1))
                        nc.gpsimd.tensor_copy(idx[e][:], slots[:, bass.ds(n * tiles, tiles)]).then_inc(idx_ready, 1)
                        pool.wait_ge(idx_ready, n + 1)
                        pool.sem_inc(go, 1)
                        for k in range(tiles):
                            pool.indirect_dma_start(rows[e * tiles + k][:], None, y_d,
                                                    bass.IndirectOffsetOnAxis(ap=idx[e][:, k:k + 1], axis=0)
                                                    ).then_inc(landed[e * tiles + k], 16)
                pair_loop(pool, groups, body)

            @block.scalar
            def _(act):
                act.sem_inc(activated, 2)

                def body(i, first, last):
                    for e in range(2):
                        n = 2 * i + e
                        act.wait_ge(w_in[e], 64 * (i + 1))
                        for q in range(2):
                            act.wait_ge(multiplied, 2 * n + q + 3)
                            for j in range(jh):
                                act.wait_ge(hidden_ready, fc * n + q * jh + j + 1)
                                nc.scalar.activation(h[q][:, j * g:(j + 1) * g], ps_h[j % 2][:, 0:g], act_fn,
                                                     bias=b1[e][:, q * jh + j:q * jh + j + 1]).then_inc(activated, 1)
                pair_loop(act, groups, body)

            @block.tensor
            def _(pe):
                pe.sem_inc(turned, 2 * tiles)
                pe.sem_inc(multiplied, 4)

                def turn(i, e):
                    n = 2 * i + e
                    for k in range(tiles):
                        pe.wait_ge(landed[e * tiles + k], 16 * (i + 1))
                        pe.wait_ge(kept, tiles * n + k + 1)
                        for d in range(DC):
                            ins = nc.tensor.transpose(ps_t[k % 2][:, d * ST:(d + 1) * ST], rows[e * tiles + k][:, d * 128:(d + 1) * 128],
                                                      c["ident"][:])
                        ins.then_inc(turned, 1)

                def body(i, first, last):
                    for e in range(2):
                        n = 2 * i + e
                        pe.wait_ge(kept, 2 + tiles * (n + 1))
                        pe.wait_ge(w_in[e], 64 * (i + 1))
                        for q in range(2):
                            for j in range(jh):
                                pe.wait_ge(activated, fc * n + q * jh + j + 1)
                                f0 = (q * jh + j) * 128
                                for d in range(DC):
                                    ins = nc.tensor.matmul(ps_h[j % 2][:, 0:g], w1[e][:, d * hidden + f0:d * hidden + f0 + 128],
                                                           xt[e][:, d * g:(d + 1) * g], start=(d == 0), stop=(d == DC - 1))
                                ins.then_inc(hidden_ready, 1)
                        if not (last and e == 1):
                            turn(i + e, 1 - e)
                        for q in range(2):
                            pe.wait_ge(activated, 2 + fc * n + (q + 1) * jh)
                            if q == 0:
                                pe.wait_ge(summed, n + 2)
                            for k in range(tiles):
                                for j in range(jh):
                                    ins = nc.tensor.matmul(
                                        ps_y[:, k * D:(k + 1) * D], h[q][:, j * g + k * ST:j * g + (k + 1) * ST],
                                        w2[e][:, (q * jh + j) * D:(q * jh + j + 1) * D],
                                        start=(q == 0 and j == 0 and k % 2 == 0), stop=(q == 1 and j == jh - 1),
                                        skip_group_check=True)
                            ins.then_inc(multiplied, 1)
                turn(0, 0)
                pair_loop(pe, groups, body)

            @block.vector
            def _(dve):
                dve.sem_inc(kept, 2)
                dve.sem_inc(summed, 2)

                def keep(i, e):
                    n = 2 * i + e
                    for k in range(tiles):
                        dve.wait_ge(turned, 2 * tiles + tiles * n + k + 1)
                        nc.vector.tensor_copy(xt[e][:].rearrange("p (d m) -> p d m", d=DC)[:, :, k * ST:(k + 1) * ST],
                                              ps_t[k % 2][:, 0:DC * ST].rearrange("p (d m) -> p d m", d=DC)).then_inc(kept, 1)

                def body(i, first, last):
                    for e in range(2):
                        n = 2 * i + e
                        if not (last and e == 1):
                            keep(i + e, 1 - e)
                        dve.wait_ge(multiplied, 6 + 2 * n)
                        dve.wait_ge(w_in[e], 64 * (i + 1))
                        if not first:
                            dve.wait_ge(out_done[e], 16 * i)
                        nc.vector.tensor_tensor(y[e][:].rearrange("p (k f) -> p k f", f=D),
                                                ps_y[:].rearrange("p (k f) -> p k f", f=D),
                                                b2[e][:].unsqueeze(1).broadcast_to([ST, tiles, D]), ALU.add).then_inc(summed, 1)
                keep(0, 0)
                pair_loop(dve, groups, body)


def combine(nc, name, out_d, pos, weights, acc):
    ring = 8
    items = [(t, k) for t in range(T) for k in range(len(pos))]
    with Stage(nc, name) as s:
        rows = [s.sb(f"rows{u}", [P, D]) for u in range(ring)]
        landed = [s.sem(f"landed{u}") for u in range(ring)]
        used = s.sem("used")
        with s.block() as block:
            @block.gpsimd
            def _(pool):
                for n, (t, k) in enumerate(items):
                    if n >= ring:
                        pool.wait_ge(used, n - ring + 1)
                    pool.indirect_dma_start(rows[n % ring][:], None, out_d,
                                            bass.IndirectOffsetOnAxis(ap=pos[k][:, t:t + 1], axis=0)).then_inc(landed[n % ring], 16)

            @block.vector
            def _(dve):
                for n, (t, k) in enumerate(items):
                    dve.wait_ge(landed[n % ring], 16 * (n // ring + 1))
                    to = acc[:, t * D:(t + 1) * D]
                    if len(pos) == 1:
                        nc.vector.tensor_scalar(to, rows[n % ring][:], weights[k][:, t:t + 1], None, ALU.mult).then_inc(used, 1)
                    else:
                        if k > 0:
                            dve.wait_ge(used, n)
                        nc.vector.scalar_tensor_tensor(to, rows[n % ring][:], weights[k][:, t:t + 1], to,
                                                       ALU.mult, ALU.add).then_inc(used, 1)



def first_of(nc, step, eq, out, seen, experts):
    step(nc.vector.memset(seen[:], 0.0))
    for e in range(experts):
        step(nc.vector.tensor_tensor(out[:, :, e], eq[:, :, e], seen[:], ALU.is_gt))
        step(nc.vector.tensor_tensor(seen[:], seen[:], eq[:, :, e], ALU.max))


def top_two(nc, c, name, scores, n, experts, one, two, w1, w2):
    with Stage(nc, name) as s:
        eq = s.sb("eq", [P, n * experts])
        rest = s.sb("rest", [P, n * experts])
        seen, m1, m2, gap, ex, den = (s.sb(k, [P, n]) for k in ("seen", "m1", "m2", "gap", "ex", "den"))
        steps, exps = s.sem("steps"), s.sem("exps")
        gap_ready = s.sem("gap_ready")

        def view(x):
            return x[:, 0:n * experts].rearrange("p (t e) -> p t e", e=experts)

        def wide(x):
            return x[:].unsqueeze(2).broadcast_to([P, n, experts])

        with s.block() as block:
            @block.scalar
            def _(act):
                act.wait_ge(gap_ready, 1)
                nc.scalar.activation(ex[:], gap[:], ACT.Exp).then_inc(exps, 1)

            @block.vector
            def _(dve):
                step = Steps(dve, steps)
                V = nc.vector
                sc = view(scores)
                step(V.tensor_reduce(m1[:], sc, AX.X, ALU.max))
                step(V.tensor_tensor(view(eq), sc, wide(m1), ALU.is_equal))
                first_of(nc, step, view(eq), view(one), seen, experts)
                step(V.scalar_tensor_tensor(rest[:], one[:], -3e38, scores[:, 0:n * experts], ALU.mult, ALU.add))
                step(V.tensor_reduce(m2[:], view(rest), AX.X, ALU.max))
                step(V.tensor_tensor(view(eq), view(rest), wide(m2), ALU.is_equal))
                first_of(nc, step, view(eq), view(two), seen, experts)
                V.tensor_tensor(gap[:], m2[:], m1[:], ALU.subtract).then_inc(gap_ready, 1)
                dve.wait_ge(exps, 1)
                step(V.tensor_scalar(den[:], ex[:], 1.0, None, ALU.add))
                step(V.reciprocal(w1[:], den[:]))
                step(V.tensor_tensor(w2[:], ex[:], w1[:], ALU.mult))


def top_one(nc, c, name, logits, experts, one, pm):
    with Stage(nc, name) as s:
        shift, ex, probs, eq = (s.sb(k, [P, T * experts]) for k in ("shift", "ex", "probs", "eq"))
        mx, tot, inv, seen = (s.sb(k, [P, T]) for k in ("mx", "tot", "inv", "seen"))
        steps, exps, shifted = (s.sem(k) for k in ("steps", "exps", "shifted"))

        def view(x):
            return x[:].rearrange("p (t e) -> p t e", e=experts)

        def wide(x):
            return x[:].unsqueeze(2).broadcast_to([P, T, experts])

        with s.block() as block:
            @block.scalar
            def _(act):
                act.wait_ge(shifted, 1)
                nc.scalar.activation(ex[:], shift[:], ACT.Exp).then_inc(exps, 1)

            @block.vector
            def _(dve):
                step = Steps(dve, steps)
                V = nc.vector
                step(V.tensor_reduce(mx[:], view(logits), AX.X, ALU.max))
                V.tensor_tensor(view(shift), view(logits), wide(mx), ALU.subtract).then_inc(shifted, 1)
                dve.wait_ge(exps, 1)
                step(V.tensor_reduce(tot[:], view(ex), AX.X, ALU.add))
                step(V.reciprocal(inv[:], tot[:]))
                step(V.tensor_tensor(view(probs), view(ex), wide(inv), ALU.mult))
                step(V.tensor_reduce(pm[:], view(probs), AX.X, ALU.max))
                step(V.tensor_tensor(view(eq), view(probs), wide(pm), ALU.is_equal))
                first_of(nc, step, view(eq), view(one), seen, experts)


def finite(nc, name, y):
    top = 3.4028234663852886e38
    w = RING * D
    with Stage(nc, name) as s:
        mask, low, nan = (s.sb(k, [P, w], I32) for k in ("mask", "low", "nan"))
        fill = s.sb("fill", [P, 3])
        steps = s.sem("steps")

        def filled(k):
            return fill[:, k:k + 1].broadcast_to([P, w])

        with s.block() as block:
            @block.vector
            def _(dve):
                step = Steps(dve, steps)
                V = nc.vector
                for k, v in enumerate((1e4, -1e4, 0.0)):
                    step(V.memset(fill[:, k:k + 1], v))
                for g in range(T // RING):
                    yt = y[:, g * w:(g + 1) * w]
                    step(V.tensor_scalar(mask[:], yt, top, None, ALU.is_gt))
                    step(V.tensor_scalar(low[:], yt, -top, None, ALU.is_lt))
                    step(V.tensor_tensor(nan[:], yt, yt, ALU.not_equal))
                    step(V.copy_predicated(yt, mask[:], filled(0)))
                    step(V.copy_predicated(yt, low[:], filled(1)))
                    step(V.copy_predicated(yt, nan[:], filled(2)))


def global_scores(nc, c, name, yt_feat, wr_d, br_d, experts, capacity, scores):
    with Stage(nc, name) as s:
        wr = s.sb("wr", [128, DC * experts])
        br = s.sb("br", [P, experts])
        tot = s.sb("tot", [128, DC])
        mean = s.sb("mean", [128, DC * P])
        lg, ex, rw, load, scale, low, a2, ex2 = (s.sb(k, [P, experts]) for k in ("lg", "ex", "rw", "load", "scale", "low", "a2", "ex2"))
        mx, sm, inv = (s.sb(k, [P, 1]) for k in ("mx", "sm", "inv"))
        ps = s.ps("ps", [P, 512])
        loaded, steps, averaged, routed, asked, exps = (s.sem(k) for k in ("loaded", "steps", "averaged", "routed", "asked", "exps"))
        with s.block() as block:
            @block.sync
            def _(sp):
                sp.dma_start(wr[:], wr_d).then_inc(loaded, 16)
                sp.dma_start(br[:], br_d.partition_broadcast(P)).then_inc(loaded, 16)

            @block.scalar
            def _(act):
                act.wait_ge(asked, 1)
                nc.scalar.activation(ex[:], lg[:], ACT.Exp).then_inc(exps, 1)
                act.wait_ge(asked, 2)
                nc.scalar.activation(ex2[:], a2[:], ACT.Exp).then_inc(exps, 1)

            @block.tensor
            def _(pe):
                pe.wait_ge(loaded, 32)
                pe.wait_ge(averaged, 1)
                for k in range(DC):
                    ins = nc.tensor.matmul(ps[:, 0:experts], mean[:, k * P:(k + 1) * P], wr[:, k * experts:(k + 1) * experts],
                                           start=(k == 0), stop=(k == DC - 1))
                ins.then_inc(routed, 1)

            @block.vector
            def _(dve):
                step = Steps(dve, steps)
                V = nc.vector
                step(V.tensor_reduce(tot[:], yt_feat[:].rearrange("p (k n) -> p k n", k=DC), AX.X, ALU.add))
                V.tensor_scalar(mean[:].rearrange("p (k m) -> p k m", k=DC),
                                tot[:].unsqueeze(2).broadcast_to([128, DC, P]), 1.0 / N, None, ALU.mult).then_inc(averaged, 1)
                dve.wait_ge(loaded, 32)
                dve.wait_ge(routed, 1)
                step(V.tensor_tensor(lg[:], ps[:, 0:experts], br[:], ALU.add))
                step(V.tensor_reduce(mx[:], lg[:], AX.X, ALU.max))
                step(V.tensor_scalar(lg[:], lg[:], mx[:, 0:1], None, ALU.subtract))
                dve.sem_inc(asked, 1)
                dve.wait_ge(exps, 1)
                step(V.tensor_reduce(sm[:], ex[:], AX.X, ALU.add))
                step(V.reciprocal(inv[:], sm[:]))
                step(V.tensor_scalar(rw[:], ex[:], inv[:, 0:1], None, ALU.mult))
                step(V.tensor_scalar(load[:], rw[:], float(N), float(capacity), ALU.mult, ALU.max))
                step(V.reciprocal(scale[:], load[:]))
                step(V.tensor_scalar(scale[:], scale[:], float(capacity), None, ALU.mult))
                step(V.tensor_scalar(low[:], load[:], float(capacity), None, ALU.is_le))
                step(V.tensor_tensor(scale[:], scale[:], low[:], ALU.max))
                step(V.tensor_tensor(a2[:], rw[:], scale[:], ALU.mult))
                step(V.tensor_reduce(mx[:], a2[:], AX.X, ALU.max))
                step(V.tensor_scalar(a2[:], a2[:], mx[:, 0:1], None, ALU.subtract))
                dve.sem_inc(asked, 1)
                dve.wait_ge(exps, 2)
                step(V.tensor_reduce(sm[:], ex2[:], AX.X, ALU.add))
                step(V.reciprocal(inv[:], sm[:]))
                step(V.tensor_scalar(scores[:], ex2[:], inv[:, 0:1], None, ALU.mult))



def vector_steps(nc, name, fn):
    with Stage(nc, name) as s:
        steps = s.sem("steps")
        with s.block() as block:
            @block.vector
            def _(dve):
                fn(Steps(dve, steps), nc.vector)


def root(nc, name, x, out):
    with Stage(nc, name) as s:
        r = s.sb("r", list(x.shape))
        rooted, inverted = s.sem("rooted"), s.sem("inverted")
        with s.block() as block:
            @block.scalar
            def _(act):
                nc.scalar.activation(r[:], x[:], ACT.Sqrt).then_inc(rooted, 1)

            @block.vector
            def _(dve):
                dve.wait_ge(rooted, 1)
                nc.vector.reciprocal(out[:], r[:]).then_inc(inverted, 1)


def batch_norm_relu(nc, name, xt, ch, bias_d, gamma_d, beta_d):
    with Stage(nc, name) as s:
        col = s.sb("col", [ch, 3])
        stats = s.sb("stats", [ch, T * 6])
        mv = s.sb("mv", [ch, 2])
        var, std, rstd = (s.sb(k, [ch, 1]) for k in ("var", "std", "rstd"))
        loaded, steps, ready, rooted, normed, done = (s.sem(k) for k in ("loaded", "steps", "ready", "rooted", "normed", "done"))
        with s.block() as block:
            @block.sync
            def _(sp):
                for k, v in enumerate((bias_d, gamma_d, beta_d)):
                    sp.dma_start(col[:, k:k + 1], v).then_inc(loaded, 16)

            @block.scalar
            def _(act):
                act.wait_ge(ready, 1)
                nc.scalar.activation(std[:], var[:], ACT.Sqrt).then_inc(rooted, 1)
                act.wait_ge(normed, 1)
                nc.scalar.activation(xt[:], xt[:], ACT.Relu, bias=col[:, 2:3], scale=col[:, 1:2]).then_inc(done, 1)

            @block.vector
            def _(dve):
                step = Steps(dve, steps)
                dve.wait_ge(loaded, 48)
                step(nc.vector.tensor_scalar(xt[:], xt[:], col[:, 0:1], None, ALU.add))
                tiles_loop(dve, lambda t, u: nc.vector.bn_stats(stats[:, tile_of(t, 6)], xt[:, tile_of(t, P)]).then_inc(steps, 1))
                step.n += T
                dve.wait_ge(steps, step.n)
                step(nc.vector.bn_aggr(mv[:], stats[:]))
                nc.vector.tensor_scalar(var[:], mv[:, 1:2], EPS, None, ALU.add).then_inc(ready, 1)
                dve.wait_ge(rooted, 1)
                step(nc.vector.reciprocal(rstd[:], std[:]))
                nc.vector.tensor_scalar(xt[:], xt[:], mv[:, 0:1], rstd[:, 0:1], ALU.subtract, ALU.mult).then_inc(normed, 1)
                dve.wait_ge(normed, 1)



def model(nc, I, out, probes=None):
    E0 = 53125
    E3 = 32768
    CH0, CH3 = chunk_bound(E0), chunk_bound(E3)
    heads, hd = 8, 32
    gh, ge = 4, 4
    capacity = -(-N * 5 // (4 * 8))

    def dram(name, shape):
        return nc.dram_tensor(name, shape, F32, kind="Internal").ap()

    def slot_table(name, tiles):
        return nc.dram_tensor(name, [ST * tiles + N, 1], I32, kind="Internal").ap()

    with Stage(nc, "model") as m:
        x = m.sb("x", [P, T * D])
        c = {"ident": m.sb("ident", [128, 128]), "iota": m.sb("iota", [128, 128]), "ones": m.sb("ones", [128, 128])}
        count = m.sb("count", [P, T])
        inv2 = m.sb("inv2", [P, T])
        inv3 = m.sb("inv3", [P, T])

        def chunks_of(w):
            wide = w.shape[1] // DC
            return [w[:, k * wide:(k + 1) * wide] for k in range(DC)]

        def from_features(t, w):
            return [(t, 128, k, wk) for k, wk in enumerate(chunks_of(w))]

        def probe(k):
            if probes is not None and k in probes:
                transfer(nc, "probe", [(by_tile(probes[k], D), as_tiles(x, D))])

        y_d = dram("y", [N, D])
        constants(nc, c, I)
        transfer(nc, "load_x", [(as_tiles(x, D), by_tile(I["x"], D))])

        with Stage(nc, "graph") as g:
            rec_d, blk_d = g.sb("rec_d", [128, CH0 * FIELDS]), g.sb("blk_d", [1, CH0], I32)
            rec_s, blk_s = g.sb("rec_s", [128, CH0 * FIELDS]), g.sb("blk_s", [1, CH0], I32)
            bucket(nc, c, "by_dst", I["dst"], I["src"], None, 125, 425, (5, 5, 17), CH0,
                   dram("sorted_dst", [CH0 * EC, FIELDS]), rec_d, blk_d)
            bucket(nc, c, "by_src", I["src"], I["dst"], I["edge_weight"], 125, 425, (5, 5, 17), CH0,
                   dram("sorted_src", [CH0 * EC, FIELDS]), rec_s, blk_s)

            with Stage(nc, "l0g") as s:
                yf = s.sb("yf", [128, DC * N])
                mf = s.sb("mf", [128, DC * N])
                with Stage(nc, "l0y") as s2:
                    y = s2.sb("y", [P, T * D])
                    layernorm(nc, "ln0", x, y)
                    transfer(nc, "store_y0", [(by_tile(y_d, D), as_tiles(y, D))])
                    turn_tiles(nc, c, "turn0", y, D, yf)
                with Stage(nc, "l0a") as s2:
                    acc = s2.sb("acc", [P, T * (D + 1)])
                    inv = s2.sb("inv", [P, T])
                    segment_sum(nc, c, "sum0", y_d, D, rec_d, blk_d, CH0, acc, True)
                    a3 = as_tiles(acc, D + 1)

                    def mean(step, V):
                        step(V.tensor_copy(count[:], a3[:, :, D]))
                        step(V.tensor_scalar(inv[:], count[:], 1.0, None, ALU.max))
                        step(V.reciprocal(inv[:], inv[:]))
                        step(V.tensor_tensor(a3[:, :, 0:D], a3[:, :, 0:D], inv[:].unsqueeze(2).broadcast_to([P, T, D]), ALU.mult))
                        step(V.tensor_scalar(inv3[:], count[:], 1.0, 1.0, ALU.add, ALU.max))
                    vector_steps(nc, "mean0", mean)
                    root(nc, "root3", inv3, inv3)
                    turn_tiles(nc, c, "turn0b", acc, D, mf, stride=D + 1)
                project(nc, c, "out0", from_features(mf, I["L0_gnn_W_neigh"]) + from_features(yf, I["L0_gnn_W_self"]),
                        D, "add", x, bias=I["L0_gnn_b_self"])
            probe(1)

            with Stage(nc, "l0f") as s:
                one, pm, kept = s.sb("one", [P, T * 8]), s.sb("pm", [P, T]), s.sb("kept", [P, T])
                slots, pos = s.sb("slots", [ST, 8 * 4], I32), s.sb("pos", [P, T], I32)
                router(nc, c, "l0r", x, y_d, I["L0_ffn_gate_w"], I["L0_ffn_gate_b"], 8,
                       lambda lg: top_one(nc, c, "gate0", lg, 8, one, pm))
                assert capacity <= 4 * ST
                dispatch(nc, c, "disp0", [one], 8, 4, 8, capacity, slot_table("slots0", 8 * 4), slots, None, [pos], kept)
                out_d = dram("out0", [8 * 4 * ST, D])
                routed(nc, c, "net0", y_d, slots, None, 1024, ACT.Relu, I["L0_ffn_w1"], I["L0_ffn_b1"], I["L0_ffn_w2"],
                       I["L0_ffn_b2"], 4, 8, out_d)
                acc = s.sb("acc", [P, T * D])
                vector_steps(nc, "keep0", lambda step, V: step(V.tensor_tensor(pm[:], pm[:], kept[:], ALU.mult)))
                combine(nc, "comb0", out_d, [pos], [pm], acc)
                finite(nc, "finite0", acc)
                vector_steps(nc, "res0", lambda step, V: step(V.tensor_tensor(x[:], x[:], acc[:], ALU.add)))
            probe(2)

            k_d, v_d = dram("k", [N, D]), dram("v", [N, D])
            with Stage(nc, "l1g") as s:
                y = s.sb("y", [P, T * D])
                attended = s.sb("attended", [P, T * (D + heads)])
                layernorm(nc, "ln1", x, y)
                with Stage(nc, "l1e") as s1:
                    scores = s1.sb("scores", [EC, CH0 * heads])
                    best = s1.sb("best", [P, T * heads])
                    with Stage(nc, "l1q") as s2:
                        q = s2.sb("q", [P, T * D])
                        with Stage(nc, "l1kv") as s3:
                            yf = s3.sb("yf", [128, DC * N])
                            turn_tiles(nc, c, "turn1", y, D, yf)
                            for wname, table in (("L1_gnn_Wk", k_d), ("L1_gnn_Wv", v_d)):
                                project(nc, c, "kv", from_features(yf, I[wname]), D, "copy", q)
                                transfer(nc, "store_kv", [(by_tile(table, D), as_tiles(q, D))])
                            project(nc, c, "q", from_features(yf, I["L1_gnn_Wq"]), D, "copy", q)
                        edge_scores(nc, c, "scores", k_d, q, rec_d, blk_d, CH0, heads, hd ** -0.5, scores)
                    vector_steps(nc, "max0", lambda step, V: step(V.memset(best[:], 0.0)))
                    segment_max(nc, c, "max1", scores, heads, heads, 6, rec_d, blk_d, CH0, best, None, None)
                    softmax_sum(nc, c, "att1", heads, hd, rec_d, blk_d, CH0, attended, best, heads, v_d, scores, None, False)
                af = s.sb("af", [128, DC * N])
                inv = s.sb("inv", [P, T * heads])

                def normalise(step, V):
                    a = as_tiles(attended, D + heads)
                    i3 = inv[:].rearrange("p (t h) -> p t h", h=heads)
                    step(V.tensor_scalar(i3, a[:, :, D:D + heads], 1e-8, None, ALU.add))
                    step(V.reciprocal(inv[:], inv[:]))
                    for h in range(heads):
                        v = a[:, :, h * hd:(h + 1) * hd]
                        step(V.tensor_tensor(v, v, i3[:, :, h:h + 1].broadcast_to([P, T, hd]), ALU.mult))
                vector_steps(nc, "norm1", normalise)
                turn_tiles(nc, c, "turn1a", attended, D, af, stride=D + heads)
                project(nc, c, "out1", from_features(af, I["L1_gnn_Wo_w"]), D, "add", y, bias=I["L1_gnn_Wo_b"])
                layernorm(nc, "ln1a", y, y, I["L1_gnn_ln1_g"], I["L1_gnn_ln1_b"])
                turn_tiles(nc, c, "turn1h", y, D, af)
                acc = attended[:, 0:T * D]
                network(nc, c, "net1", af, 1, 512, ACT.Gelu, I["L1_gnn_ffn_w1"], I["L1_gnn_ffn_b1"], I["L1_gnn_ffn_w2"],
                        I["L1_gnn_ffn_b2"], c["ones"], acc)
                vector_steps(nc, "res1", lambda step, V: step(V.tensor_tensor(y[:], y[:], acc, ALU.add)))
                layernorm(nc, "ln1b", y, y, I["L1_gnn_ln2_g"], I["L1_gnn_ln2_b"])
                vector_steps(nc, "res1b", lambda step, V: step(V.tensor_tensor(x[:], x[:], y[:], ALU.add)))
            probe(3)

            with Stage(nc, "l1f") as s:
                one, two = s.sb("one", [P, T * 8]), s.sb("two", [P, T * 8])
                pw1, pw2 = s.sb("pw1", [P, T]), s.sb("pw2", [P, T])
                router(nc, c, "l1r", x, y_d, I["L1_ffn_Wg"], I["L1_ffn_bg"], 8,
                       lambda lg: top_two(nc, c, "gate1", lg, T, 8, one, two, pw1, pw2))
                two_of(nc, c, "l1n", s, dram, slot_table, y_d, one, two, pw1, pw2, 8, 1024, ACT.Relu,
                       I["L1_ffn_W1"], I["L1_ffn_b1"], I["L1_ffn_W2"], I["L1_ffn_b2"], x)
            probe(4)

            z_d = dram("z", [N, D])
            with Stage(nc, "l2g") as s:
                yf = s.sb("yf", [128, DC * N])
                acc = s.sb("acc", [P, T * D])
                with Stage(nc, "l2d") as s2:
                    deg = s2.sb("deg", [P, T])
                    guard = s2.sb("guard", [P, T])
                    degree(nc, c, "deg2", rec_s, CH0, deg)

                    def guarded(step, V):
                        step(V.tensor_scalar(deg[:], deg[:], 1.0, None, ALU.add))
                        step(V.tensor_scalar(guard[:], deg[:], 0.0, None, ALU.is_gt))
                        step(V.tensor_scalar(deg[:], deg[:], 1e-38, None, ALU.max))
                    vector_steps(nc, "guard2", guarded)
                    root(nc, "root2", deg, inv2)
                    vector_steps(nc, "guard2b", lambda step, V: step(V.tensor_tensor(inv2[:], inv2[:], guard[:], ALU.mult)))
                with Stage(nc, "l2y") as s2:
                    y = s2.sb("y", [P, T * D])
                    layernorm(nc, "ln2", x, y)
                    turn_tiles(nc, c, "turn2", y, D, yf)
                with Stage(nc, "l2z") as s2:
                    z = s2.sb("z", [P, T * D])
                    project(nc, c, "z2", from_features(yf, I["L2_gnn_W"]), D, "scale", z, scale=inv2)
                    transfer(nc, "store_z2", [(by_tile(z_d, D), as_tiles(z, D))])
                    segment_sum(nc, c, "sum2", z_d, D, rec_s, blk_s, CH0, acc, False)

                    def finish(step, V):
                        step(V.tensor_tensor(acc[:], acc[:], z[:], ALU.add))
                        step(V.tensor_tensor(as_tiles(acc, D), as_tiles(acc, D), inv2[:].unsqueeze(2).broadcast_to([P, T, D]), ALU.mult))
                    vector_steps(nc, "self2", finish)
                turn_tiles(nc, c, "turn2b", acc, D, yf)
                column_add(nc, "b2", yf, I["L2_gnn_b"])
                vector_steps(nc, "zero2", lambda step, V: step(V.memset(acc[:], 0.0)))
                project(nc, c, "head2", from_features(yf, I["L2_gnn_W1"]), D, "relu_add", acc, bias=I["L2_gnn_b1"])
                turn_tiles(nc, c, "turn2c", acc, D, yf)
                project(nc, c, "head2b", from_features(yf, I["L2_gnn_W2"]), D, "add", x, bias=I["L2_gnn_b2"])
            probe(5)

            with Stage(nc, "l2f") as s:
                yf = s.sb("yf", [128, DC * N])
                y = s.sb("y", [P, T * D])
                acc = s.sb("acc", [P, T * D])
                scores, picked, gate = s.sb("scores", [P, 8]), s.sb("picked", [1, 2], I32), s.sb("gate", [P, T * 2])
                layernorm(nc, "ln2f", x, y)
                turn_tiles(nc, c, "turn2f", y, D, yf)
                global_scores(nc, c, "route2", yf, I["L2_ffn_Wr"], I["L2_ffn_br"], 8, capacity, scores)
                with Stage(nc, "l2p") as s2:
                    one, two, pw1, pw2 = s2.sb("one", [P, 8]), s2.sb("two", [P, 8]), s2.sb("pw1", [P, 1]), s2.sb("pw2", [P, 1])
                    tmp, num = s2.sb("tmp", [P, 8]), s2.sb("num", [P, 2])
                    top_two(nc, c, "gate2", scores, 1, 8, one, two, pw1, pw2)

                    def picks(step, V):
                        g3 = gate[:].rearrange("p (t e) -> p t e", e=2)
                        for k, (pick, w) in enumerate(((one, pw1), (two, pw2))):
                            step(V.tensor_tensor(tmp[:], pick[:], c["iota"][0:P, 0:8], ALU.mult))
                            step(V.tensor_reduce(num[:, k:k + 1], tmp[:], AX.X, ALU.add))
                            step(V.tensor_copy(g3[:, :, k], w[:].broadcast_to([P, T])))
                        step(V.tensor_copy(picked[:], num[0:1, :]))
                    vector_steps(nc, "picks2", picks)
                network(nc, c, "net2", yf, 2, 512, ACT.Gelu, I["L2_ffn_W1"], I["L2_ffn_b1"], I["L2_ffn_W2"], I["L2_ffn_b2"], gate, acc,
                        picked)
                vector_steps(nc, "res2", lambda step, V: step(V.tensor_tensor(y[:], y[:], acc[:], ALU.add)))
                layernorm(nc, "ln2b", y, y, I["L2_ffn_gamma"], I["L2_ffn_beta"])
                vector_steps(nc, "res2b", lambda step, V: step(V.tensor_tensor(x[:], x[:], y[:], ALU.add)))
            probe(6)

            z1_d, z2_d = dram("z1", [N, 128]), dram("z2t", [N, 64])
            with Stage(nc, "l3g") as s:
                yf = s.sb("yf", [128, DC * N])
                x1f, x2f = s.sb("x1f", [128, N]), s.sb("x2f", [64, N])
                with Stage(nc, "l3y") as s2:
                    y = s2.sb("y", [P, T * D])
                    layernorm(nc, "ln3", x, y)
                    turn_tiles(nc, c, "turn3", y, D, yf)
                for k, (wide, srcs, table, xf) in enumerate((
                        (128, from_features(yf, I["L3_gnn_W1"]), z1_d, x1f),
                        (64, [(x1f, 128, 0, I["L3_gnn_W2"])], z2_d, x2f))):
                    with Stage(nc, "l3z") as s2:
                        z, acc = s2.sb("z", [P, T * wide]), s2.sb("acc", [P, T * wide])
                        project(nc, c, "z3", srcs, wide, "scale", z, scale=inv3)
                        transfer(nc, "store_z3", [(by_tile(table, wide), as_tiles(z, wide))])
                        segment_sum(nc, c, "sum3", table, wide, rec_d, blk_d, CH0, acc, False)

                        def finish(step, V):
                            step(V.tensor_tensor(acc[:], acc[:], z[:], ALU.add))
                            step(V.tensor_tensor(as_tiles(acc, wide), as_tiles(acc, wide),
                                                 inv3[:].unsqueeze(2).broadcast_to([P, T, wide]), ALU.mult))
                        vector_steps(nc, "self3", finish)
                        turn_tiles(nc, c, "turn3b", acc, wide, xf)
                    batch_norm_relu(nc, "bn3", xf, wide, I[f"L3_gnn_b{k + 1}"], I[f"L3_gnn_g{k + 1}"], I[f"L3_gnn_be{k + 1}"])
                wfc = I["L3_gnn_Wfc"]
                project(nc, c, "out3", [(yf, 128, 0, wfc[0:128, :]), (yf, 128, 1, wfc[128:256, :]),
                                        (x1f, 128, 0, wfc[256:384, :]), (x2f, 64, 0, wfc[384:448, :])],
                        D, "relu_add", x, bias=I["L3_gnn_bfc"])
            probe(7)

        with Stage(nc, "l3f") as s:
            one, two = s.sb("one", [P, T * ge]), s.sb("two", [P, T * ge])
            pw1, pw2 = s.sb("pw1", [P, T]), s.sb("pw2", [P, T])
            with Stage(nc, "gat") as s2:
                yf = s2.sb("yf", [128, DC * N])
                with Stage(nc, "l3fy") as s3:
                    y = s3.sb("y", [P, T * D])
                    layernorm(nc, "ln3f", x, y)
                    transfer(nc, "store_y3", [(by_tile(y_d, D), as_tiles(y, D))])
                    turn_tiles(nc, c, "turn3f", y, D, yf)
                attention_gate(nc, c, I, s2, dram, yf, CH3, gh, ge, one, two, pw1, pw2)
            two_of(nc, c, "l3n", s, dram, slot_table, y_d, one, two, pw1, pw2, ge, 512, ACT.Gelu,
                   I["L3_ffn_W1"], I["L3_ffn_b1"], I["L3_ffn_W2"], I["L3_ffn_b2"], x)
        transfer(nc, "store_out", [(by_tile(out, D), as_tiles(x, D))])


def router(nc, c, name, x, y_d, w_d, b_d, experts, choose):
    with Stage(nc, name) as s:
        y, yf, logits = s.sb("y", [P, T * D]), s.sb("yf", [128, DC * N]), s.sb("logits", [P, T * experts])
        layernorm(nc, "ln", x, y)
        transfer(nc, "store_y", [(by_tile(y_d, D), as_tiles(y, D))])
        turn_tiles(nc, c, "turn", y, D, yf)
        project(nc, c, "route", from_chunks(yf, w_d), experts, "copy", logits, bias=b_d)
        choose(logits)


def two_of(nc, c, name, s, dram, slot_table, y_d, one, two, pw1, pw2, experts, hidden, act_fn, w1_d, b1_d, w2_d, b2_d, x):
    tiles = 2
    groups = (2 * N + experts * (tiles * ST - 1)) // (tiles * ST)
    groups += groups % 2
    slots, which = s.sb("slots", [ST, groups * tiles], I32), s.sb("which", [1, groups], I32)
    pos = [s.sb(f"pos{k}", [P, T], I32) for k in range(2)]
    dispatch(nc, c, name + "d", [one, two], experts, tiles, groups, None, slot_table(name + "slots", groups * tiles), slots,
             which, pos, None)
    out_d = dram(name + "out", [groups * tiles * ST, D])
    routed(nc, c, name, y_d, slots, which, hidden, act_fn, w1_d, b1_d, w2_d, b2_d, tiles, groups, out_d)
    combine(nc, name + "c", out_d, pos, [pw1, pw2], x)


def column_add(nc, name, xf, bias_d):
    with Stage(nc, name) as s:
        col = s.sb("col", [128, DC])
        loaded, steps = s.sem("loaded"), s.sem("steps")
        with s.block() as block:
            @block.sync
            def _(sp):
                sp.dma_start(col[:], bias_d).then_inc(loaded, 16)

            @block.vector
            def _(dve):
                step = Steps(dve, steps)
                dve.wait_ge(loaded, 16)
                for k in range(DC):
                    v = xf[:, k * N:(k + 1) * N]
                    step(nc.vector.tensor_scalar(v, v, col[:, k:k + 1], None, ALU.add))


def attention_gate(nc, c, I, s, dram, yf, chunks, gh, ge, one, two, pw1, pw2):
    w = gh * ge
    rec, blk = s.sb("rec", [128, chunks * FIELDS]), s.sb("blk", [1, chunks], I32)
    bucket(nc, c, "by_dst3", I["edge3_dst"], I["edge3_src"], None, 128, 256, (4, 4, 16), chunks,
           dram("sorted3", [chunks * EC, FIELDS]), rec, blk)
    row = w + gh
    hs = s.sb("hs", [P, T * row])
    best = s.sb("best", [P, T * gh])
    node = s.sb("node", [P, T * 2 * gh])
    att = s.sb("att", [P, 3 * w])
    tmp = s.sb("tmp", [P, T * w])
    e_self, p_self = s.sb("e_self", [P, T * gh]), s.sb("p_self", [P, T * gh])
    acc = s.sb("acc", [P, T * row])
    stored = s.sb("stored", [EC, chunks * row])
    table = dram("gat", [N, row])
    h3, n3, a3 = as_tiles(hs, row), as_tiles(node, 2 * gh), as_tiles(acc, row)

    def heads_of(v):
        return v.rearrange("p t (h e) -> p t h e", h=gh)

    project(nc, c, "h_gat", from_chunks(yf, I["L3_ffn_W_gat"]), w, "copy", hs, stride=row)
    transfer(nc, "att", [(att[:, 0:w], I["L3_ffn_att_src"].partition_broadcast(P)),
                         (att[:, w:2 * w], I["L3_ffn_att_dst"].partition_broadcast(P)),
                         (att[:, 2 * w:3 * w], I["L3_ffn_b_gat"].partition_broadcast(P))])

    def parts(step, V):
        t3 = as_tiles(tmp, w)
        for k, dst in ((0, h3[:, :, w:row]), (1, n3[:, :, 0:gh])):
            step(V.tensor_tensor(t3, h3[:, :, 0:w], att[:, k * w:(k + 1) * w].unsqueeze(1).broadcast_to([P, T, w]), ALU.mult))
            step(V.tensor_reduce(dst, heads_of(t3), AX.X, ALU.add))
        step(V.tensor_copy(as_tiles(best, gh), h3[:, :, w:row]))
    vector_steps(nc, "parts", parts)
    transfer(nc, "store_gat", [(by_tile(table, row), h3)])
    segment_max(nc, c, "max3", None, row, gh, 3, rec, blk, chunks, best, table, stored)

    def maxima(step, V):
        b3, e3 = as_tiles(best, gh), as_tiles(e_self, gh)
        step(V.tensor_tensor(b3, b3, n3[:, :, 0:gh], ALU.add))
        step(V.scalar_tensor_tensor(n3[:, :, gh:2 * gh], b3, 0.2, b3, ALU.mult, ALU.max))
        step(V.tensor_tensor(e3, h3[:, :, w:row], n3[:, :, 0:gh], ALU.add))
        step(V.scalar_tensor_tensor(as_tiles(p_self, gh), e3, 0.2, e3, ALU.mult, ALU.max))
        step(V.tensor_tensor(e3, as_tiles(p_self, gh), n3[:, :, gh:2 * gh], ALU.subtract))
    vector_steps(nc, "maxima", maxima)
    exponential(nc, "exp_self", e_self, p_self)
    softmax_sum(nc, c, "att3", gh, ge, rec, blk, chunks, acc, node, 2 * gh, None, None, stored, True)

    def scores(step, V):
        p3, t3 = as_tiles(p_self, gh), as_tiles(tmp, w)
        step(V.tensor_tensor(a3[:, :, w:row], a3[:, :, w:row], p3, ALU.add))
        step(V.tensor_scalar(as_tiles(e_self, gh), a3[:, :, w:row], 1e-16, None, ALU.add))
        step(V.reciprocal(e_self[:], e_self[:]))
        for h in range(gh):
            k = slice(h * ge, (h + 1) * ge)
            step(V.tensor_tensor(t3[:, :, k], h3[:, :, k], p3[:, :, h:h + 1].broadcast_to([P, T, ge]), ALU.mult))
            step(V.tensor_tensor(t3[:, :, k], t3[:, :, k], a3[:, :, k], ALU.add))
            step(V.tensor_tensor(t3[:, :, k], t3[:, :, k], as_tiles(e_self, gh)[:, :, h:h + 1].broadcast_to([P, T, ge]), ALU.mult))
        step(V.tensor_tensor(t3, t3, att[:, 2 * w:3 * w].unsqueeze(1).broadcast_to([P, T, w]), ALU.add))
    vector_steps(nc, "scores3", scores)
    with Stage(nc, "ln_gat") as s2:
        mean, var, inv = s2.sb("mean", [P, T]), s2.sb("var", [P, T]), s2.sb("inv", [P, T])
        sq = s2.sb("sq", [P, T * w])
        gb = s2.sb("gb", [P, 2 * w])
        sc = s2.sb("sc", [P, T * ge])
        t3 = as_tiles(tmp, w)
        transfer(nc, "gb", [(gb[:, 0:w], I["L3_ffn_ln_gamma"].partition_broadcast(P)),
                            (gb[:, w:2 * w], I["L3_ffn_ln_beta"].partition_broadcast(P))])

        def variance(step, V):
            step(V.tensor_reduce(mean[:], t3, AX.X, ALU.add))
            step(V.tensor_scalar(mean[:], mean[:], 1.0 / w, None, ALU.mult))
            step(V.tensor_tensor(t3, t3, mean[:].unsqueeze(2).broadcast_to([P, T, w]), ALU.subtract))
            step(V.tensor_tensor(sq[:], tmp[:], tmp[:], ALU.mult))
            step(V.tensor_reduce(var[:], as_tiles(sq, w), AX.X, ALU.add))
            step(V.tensor_scalar(var[:], var[:], 1.0 / w, EPS, ALU.mult, ALU.add))
        vector_steps(nc, "variance", variance)
        root(nc, "root_gat", var, inv)

        def average(step, V):
            step(V.tensor_tensor(t3, t3, inv[:].unsqueeze(2).broadcast_to([P, T, w]), ALU.mult))
            step(V.tensor_tensor(t3, t3, gb[:, 0:w].unsqueeze(1).broadcast_to([P, T, w]), ALU.mult))
            step(V.tensor_tensor(t3, t3, gb[:, w:2 * w].unsqueeze(1).broadcast_to([P, T, w]), ALU.add))
            s3 = as_tiles(sc, ge)
            step(V.tensor_tensor(s3, t3[:, :, 0:ge], t3[:, :, ge:2 * ge], ALU.add))
            for h in range(2, gh):
                step(V.tensor_tensor(s3, s3, t3[:, :, h * ge:(h + 1) * ge], ALU.add))
            step(V.tensor_scalar(sc[:], sc[:], 1.0 / gh, None, ALU.mult))
        vector_steps(nc, "average", average)
        top_two(nc, c, "gate3", sc, T, ge, one, two, pw1, pw2)


def from_chunks(t, w):
    wide = w.shape[1] // DC
    return [(t, 128, k, w[:, k * wide:(k + 1) * wide]) for k in range(DC)]


def exponential(nc, name, src, dst):
    with Stage(nc, name) as s:
        done = s.sem("done")
        with s.block() as block:
            @block.scalar
            def _(act):
                nc.scalar.activation(dst[:], src[:], ACT.Exp).then_inc(done, 1)



def lay_out(inputs):
    import numpy as np
    a = {k: np.ascontiguousarray(v) for k, v in inputs.items()}
    o = {"x": a["x"]}

    def rows(w):
        w = w.reshape(-1, 128, w.shape[-1])
        return w.transpose(1, 0, 2).reshape(128, -1)

    def experts(w):
        return np.stack([rows(e) for e in w])

    def columns(b):
        return b.reshape(b.shape[0], -1, 128).transpose(0, 2, 1)

    o["src"], o["dst"] = a["src"].reshape(125, -1), a["dst"].reshape(125, -1)
    o["edge_weight"] = a["edge_weight"].reshape(125, -1)
    o["edge3_src"], o["edge3_dst"] = a["L3_ffn_edge_index"][0].reshape(128, -1), a["L3_ffn_edge_index"][1].reshape(128, -1)
    for k in ("L0_gnn_W_neigh", "L0_gnn_W_self"):
        o[k] = rows(a[k].T)
    o["L1_ffn_Wg"] = rows(a["L1_ffn_Wg"].T)
    for k in ("L0_ffn_gate_w", "L1_gnn_Wq", "L1_gnn_Wk", "L1_gnn_Wv", "L1_gnn_Wo_w", "L2_gnn_W", "L2_gnn_W1",
              "L2_gnn_W2", "L2_ffn_Wr", "L3_gnn_W1", "L3_ffn_W_gat"):
        o[k] = rows(a[k])
    for k in ("L3_gnn_W2", "L3_gnn_Wfc"):
        o[k] = a[k]
    for k in ("L0_gnn_b_self", "L0_ffn_gate_b", "L1_gnn_Wo_b", "L1_ffn_bg", "L2_gnn_b1", "L2_gnn_b2", "L3_gnn_bfc"):
        o[k] = a[k].reshape(1, -1)
    for k in ("L1_gnn_ln1_g", "L1_gnn_ln1_b", "L1_gnn_ln2_g", "L1_gnn_ln2_b", "L2_ffn_br", "L2_ffn_gamma", "L2_ffn_beta",
              "L3_ffn_att_src", "L3_ffn_att_dst", "L3_ffn_b_gat", "L3_ffn_ln_gamma", "L3_ffn_ln_beta"):
        o[k] = a[k].reshape(-1)
    o["L2_gnn_b"] = a["L2_gnn_b"].reshape(-1, 128).T
    for k in ("b1", "g1", "be1", "b2", "g2", "be2"):
        o[f"L3_gnn_{k}"] = a[f"L3_gnn_{k}"].reshape(-1, 1)
    for pre, w1, w2 in (("L0_ffn", "w1", "w2"), ("L2_ffn", "W1", "W2"), ("L3_ffn", "W1", "W2")):
        o[f"{pre}_{w1}"], o[f"{pre}_{w2}"] = experts(a[f"{pre}_{w1}"]), experts(a[f"{pre}_{w2}"])
    o["L1_ffn_W1"], o["L1_ffn_W2"] = experts(a["L1_ffn_W1"].transpose(0, 2, 1)), experts(a["L1_ffn_W2"].transpose(0, 2, 1))
    o["L1_gnn_ffn_w1"], o["L1_gnn_ffn_w2"] = experts(a["L1_gnn_ffn_w1"][None]), experts(a["L1_gnn_ffn_w2"][None])
    for pre in ("L0_ffn", "L1_ffn", "L2_ffn", "L3_ffn"):
        o[f"{pre}_b1"], o[f"{pre}_b2"] = columns(a[f"{pre}_b1"]), a[f"{pre}_b2"]
    o["L1_gnn_ffn_b1"], o["L1_gnn_ffn_b2"] = columns(a["L1_gnn_ffn_b1"][None]), a["L1_gnn_ffn_b2"][None]
    return {k: np.ascontiguousarray(v) for k, v in o.items()}


def kernel(**inputs):
    import concourse.bacc as _bacc
    from concourse.bass_utils import run_bass_kernel_spmd as _run

    nc = _bacc.Bacc("TRN2", target_bir_lowering=False, num_devices=1)
    arrays = {f"in_{k}": v for k, v in lay_out(inputs).items()}
    aps = {k[3:]: nc.dram_tensor(k, v.shape, mybir.dt.from_np(v.dtype), kind="ExternalInput").ap()
           for k, v in arrays.items()}
    out = nc.dram_tensor("out", (N, D), F32, kind="ExternalOutput").ap()
    model(nc, aps, out)
    r = _run(nc, [arrays], core_ids=[0])
    return r.results[0]["out"]
```

```python
from contextlib import ExitStack

import concourse.bass as bass
from concourse import mybir

F32 = mybir.dt.float32
BF16 = mybir.dt.bfloat16
I32 = mybir.dt.int32
ALU = mybir.AluOpType
ACT = mybir.ActivationFunctionType
AX = mybir.AxisListType

N = 3125
P = 125
T = N // P
D = 256
DC = D // 128
EC = 128
RING = 5
FIELDS = 4
EPS = 1e-5
GROUP = RING * P
PIECES = ((0, 375), (375, 250))


def chunk_bound(edges):
    most = (edges + T * (EC - 1)) // EC
    return -(-most // 8) * 8


class Stage:

    count = 0

    def __init__(self, nc, name):
        Stage.count += 1
        self.nc, self.name, self.ctx, self.sems = nc, f"{name}{Stage.count}", ExitStack(), []

    def __enter__(self):
        self.ctx.__enter__()
        return self

    def __exit__(self, *e):
        if self.sems and e[0] is None:
            self.nc.clear_and_free_semaphores(self.sems)
            self.nc.all_engine_barrier()
        return self.ctx.__exit__(*e)

    def sb(self, name, shape, dt=F32):
        return self.ctx.enter_context(self.nc.sbuf_tensor(f"{self.name}_{name}", shape, dt))

    def ps(self, name, shape, dt=F32):
        return self.ctx.enter_context(self.nc.psum_tensor(f"{self.name}_{name}", shape, dt))

    def sem(self, name):
        self.sems.append(self.nc.alloc_semaphore(f"{self.name}_{name}"))
        return self.sems[-1]

    def block(self):
        return self.nc.Block(self.name)


class Steps:

    def __init__(self, eng, sem):
        self.eng, self.sem, self.n, self.at = eng, sem, 0, None

    def __call__(self, ins):
        ins.then_inc(self.sem, 1)
        self.n += 1
        self.eng.wait_ge(self.sem, self.n if self.at is None else self.at + self.n)

    def loop(self, i, per):
        self.base, self.at, self.n = (self.n, self.n + i * per, 0)

    def leave(self, count, per):
        assert self.n == per, (self.n, per)
        self.n, self.at = self.base + count * per, None


def tile_of(t, width):
    return bass.ds(t * width, width)



def constants(nc, c, I):
    with Stage(nc, "const") as s:
        zero = s.sem("zero")
        made = s.sem("made")
        with s.block() as block:
            @block.gpsimd
            def _(pool):
                nc.gpsimd.memset(c["ident"][:], 0.0).then_inc(zero, 1)
                nc.gpsimd.iota(c["iota"][:], pattern=[[1, 128]], base=0, channel_multiplier=0,
                               allow_small_or_imprecise_dtypes=True).then_inc(made, 1)
                nc.gpsimd.memset(c["ones"][:], 1.0).then_inc(made, 1)
                pool.wait_ge(zero, 1)
                nc.gpsimd.affine_select(out=c["ident"][:], in_=c["ident"][:], compare_op=ALU.not_equal,
                                        fill=1.0, base=0, pattern=[[-1, 128]],
                                        channel_multiplier=1).then_inc(made, 1)



def transfer(nc, name, pairs):
    with Stage(nc, name) as s:
        by_sync, by_act = s.sem("by_sync"), s.sem("by_act")
        with s.block() as block:
            @block.sync
            def _(sp):
                for dst, src in pairs[0::2]:
                    sp.dma_start(dst, src).then_inc(by_sync, 16)
                sp.wait_ge(by_sync, 16 * len(pairs[0::2]))

            @block.scalar
            def _(act):
                for dst, src in pairs[1::2]:
                    act.dma_start(dst, src).then_inc(by_act, 16)
                if len(pairs) > 1:
                    act.wait_ge(by_act, 16 * len(pairs[1::2]))


def by_tile(dram, width):
    return dram.rearrange("(t p) f -> p t f", p=P)


def as_tiles(sb, width):
    return sb[:].rearrange("p (t f) -> p t f", f=width)



class Table:

    def __init__(self, nc, s, name, parts, cols, loops, chunks):
        self.name, self.parts, self.cols, self.loops, self.chunks = name, parts, cols, loops, chunks
        assert loops[0] * loops[1] * loops[2] == cols
        self.rec = s.sb(name + "_rec", [128, chunks * FIELDS])
        self.blk = s.sb(name + "_blk", [1, chunks], I32)
        self.records = s.sb(name + "_records", [parts, cols * FIELDS])
        self.row = s.sb(name + "_row", [parts, cols], I32)
        self.sorted_d = nc.dram_tensor("sorted_" + name, [chunks * EC, FIELDS], F32, kind="Internal").ap()


def scatter(nc, s, table, first, count):
    iters, groups, per = table.loops
    assert first + count <= iters
    rec_s = [s.sb(f"{table.name}_rec{g}", [table.parts, per * FIELDS]) for g in range(groups)]
    dst_s = [s.sb(f"{table.name}_dst{g}", [table.parts, per], I32) for g in range(groups)]
    sent = [s.sem(f"{table.name}_sent{g}") for g in range(groups)]
    filled, go = s.sem(f"{table.name}_filled"), s.sem(f"{table.name}_go")

    def program(pool):
        def send(i, first_time):
            for g in range(groups):
                if not first_time:
                    pool.wait_ge(sent[g], 16 * per * i)
                    pool.sem_inc(go, 1)
                at = ((first + i) * groups + g) * per
                nc.gpsimd.tensor_copy(rec_s[g][:], table.records[:, bass.ds(at * FIELDS, per * FIELDS)]).then_inc(filled, 1)
                nc.gpsimd.tensor_copy(dst_s[g][:], table.row[:, bass.ds(at, per)]).then_inc(filled, 1)
                pool.wait_ge(filled, 2 * (i * groups + g) + 2)
                pool.sem_inc(go, 1)
                for k in range(per):
                    pool.indirect_dma_start(
                        table.sorted_d, bass.IndirectOffsetOnAxis(ap=dst_s[g][:, k:k + 1], axis=0),
                        rec_s[g][:, k * FIELDS:(k + 1) * FIELDS], None).then_inc(sent[g], 16)
        send(0, True)
        if count > 1:
            with pool.Fori(1, count) as i:
                send(i, False)
        for g in range(groups):
            pool.wait_ge(sent[g], 16 * per * count)
    return program


def scatters(nc, s, side):
    programs = [scatter(nc, s, *part) for part in side]

    def program(pool):
        for run in programs:
            run(pool)
    return program


def collect(nc, name, tables):
    transfer(nc, name, [(t.rec[:], t.sorted_d.rearrange("(p c) f -> p (c f)", p=EC)) for t in tables])


def bucket(nc, c, name, key_d, other_d, weight_d, table, side=(), moves=()):
    parts, cols, chunks, sorted_d = table.parts, table.cols, table.chunks, table.sorted_d
    rec, blk, records, row = table.rec, table.blk, table.records, table.row
    with Stage(nc, name) as s:
        key_i = s.sb("key_i", [parts, cols], I32)
        other_i = s.sb("other_i", [parts, cols], I32)
        key = s.sb("key", [parts, cols])
        thr = s.sb("thr", [128, T + 1])
        member = s.sb("member", [parts, T * cols], BF16)
        before = s.sb("before", [parts, T * cols])
        above = s.sb("above", [parts, cols])
        zeros = s.sb("zeros", [parts, cols])
        carry = s.sb("carry", [parts, 1])
        ones_b = s.sb("ones_b", [parts, parts], BF16)
        tri = s.sb("tri", [parts, parts], BF16)
        first = s.sb("first", [parts, T])
        ends = s.sb("ends", [parts, T])
        count_f = s.sb("count_f", [parts, T])
        count_i = s.sb("count_i", [parts, T], I32)
        cstart = s.sb("cstart", [parts, T])
        cend = s.sb("cend", [parts, T])
        adj = s.sb("adj", [parts, T])
        pos = s.sb("pos", [parts, cols])
        sub = s.sb("sub", [parts, cols])
        q1 = s.sb("q1", [parts, cols])
        q2 = s.sb("q2", [parts, cols])
        pos_i = s.sb("pos_i", [parts, cols], I32)
        row_i = s.sb("row_i", [parts, cols], I32)
        slot_i = s.sb("slot_i", [parts, cols], I32)
        blk_f = s.sb("blk_f", [1, chunks])
        citer = s.sb("citer", [1, chunks])
        ps = [s.ps(f"ps{h}", [parts, 512]) for h in range(2)]
        loaded = s.sem("loaded")
        steps = s.sem("steps")
        made = s.sem("made")
        blank = s.sem("blank")
        blanked = s.sem("blanked")
        moved = s.sem("moved")
        masks = s.sem("masks")
        totals = s.sem("totals")
        summed = s.sem("summed")
        ranks = s.sem("ranks")
        ranked = s.sem("ranked")
        program = scatters(nc, s, side)
        rec4 = records[:].rearrange("p (c f) -> p c f", f=FIELDS)

        with s.block() as block:
            @block.sync
            def _(sp):
                sp.dma_start(key_i[:], key_d).then_inc(loaded, 16)
                sp.dma_start(other_i[:], other_d).then_inc(loaded, 16)
                if weight_d is not None:
                    sp.dma_start(sub[:], weight_d).then_inc(loaded, 16)
                for dst, src in moves:
                    sp.dma_start(dst, src).then_inc(moved, 16)
                sp.wait_ge(blank, 2)
                sp.dma_start(sorted_d.rearrange("(p c) f -> p (c f)", p=EC), rec[:]).then_inc(blanked, 16)
                sp.wait_ge(blanked, 16)
                if moves:
                    sp.wait_ge(moved, 16 * len(moves))

            @block.gpsimd
            def _(pool):
                nc.gpsimd.iota(thr[:], pattern=[[P, T + 1]], base=0, channel_multiplier=0,
                               allow_small_or_imprecise_dtypes=True).then_inc(made, 1)
                nc.gpsimd.iota(citer[:], pattern=[[1, chunks]], base=0, channel_multiplier=0,
                               allow_small_or_imprecise_dtypes=True).then_inc(made, 1)
                nc.gpsimd.memset(tri[:], -1.0).then_inc(made, 1)
                nc.gpsimd.memset(ones_b[:], 1.0).then_inc(made, 1)
                pool.wait_ge(made, 4)
                nc.gpsimd.affine_select(out=tri[:], in_=tri[:], compare_op=ALU.is_ge, fill=0.0, base=0,
                                        pattern=[[-1, parts]], channel_multiplier=1).then_inc(made, 1)
                program(pool)

            @block.tensor
            def _(pe):
                pe.wait_ge(made, 5)
                pe.wait_ge(masks, T + 1)
                with pe.Fori(0, T) as b:
                    pe.wait_ge(summed, b + 1)
                    nc.tensor.matmul(ps[0][:, 0:cols], ones_b[:], member[:, tile_of(b, cols)],
                                     start=True, stop=True).then_inc(totals, 1)
                with pe.Fori(0, T) as b:
                    pe.wait_ge(ranked, b + 1)
                    nc.tensor.matmul(ps[1][:, 0:cols], tri[:], member[:, tile_of(b, cols)],
                                     start=True, stop=True).then_inc(ranks, 1)

            @block.vector
            def _(dve):
                step = Steps(dve, steps)
                for sem in (masks, summed, ranked):
                    dve.sem_inc(sem, 1)
                nc.vector.memset(rec[:], 0.0).then_inc(blank, 1)
                dve.wait_ge(blank, 1)
                nc.vector.memset(rec[:].rearrange("p (c f) -> p c f", f=FIELDS)[:, :, 1], -1.0).then_inc(blank, 1)
                dve.wait_ge(loaded, 32 if weight_d is None else 48)
                dve.wait_ge(made, 5)
                step(nc.vector.tensor_copy(key[:], key_i[:]))
                step(nc.vector.memset(records[:], 1.0))
                step(nc.vector.tensor_copy(rec4[:, :, 0], other_i[:]))
                if weight_d is not None:
                    step(nc.vector.tensor_copy(rec4[:, :, 2], sub[:]))
                step(nc.vector.memset(zeros[:], 0.0))
                step(nc.vector.memset(carry[:], 0.0))
                step(nc.vector.memset(pos[:], 0.0))
                step(nc.vector.tensor_copy(sub[:], key[:]))
                with dve.Fori(0, T) as b:
                    step.loop(b, 1)
                    dve.wait_ge(masks, b + 1)
                    step(nc.vector.tensor_scalar(above[:], key[:], thr[0:parts, bass.ds(b, 1)], None, ALU.is_ge))
                    nc.vector.scalar_tensor_tensor(member[:, tile_of(b, cols)], key[:],
                                                   thr[0:parts, bass.ds(b + 1, 1)], above[:],
                                                   ALU.is_lt, ALU.mult).then_inc(masks, 1)
                step.leave(T, 1)
                with dve.Fori(0, T) as b:
                    step.loop(b, 1)
                    dve.wait_ge(totals, b + 1)
                    step(nc.vector.tensor_tensor_scan(before[:, tile_of(b, cols)], zeros[:], ps[0][:, 0:cols],
                                                      carry[:], ALU.add, ALU.add))
                    nc.vector.tensor_copy(carry[:], before[:, bass.ds(b * cols + cols - 1, 1)]).then_inc(summed, 1)
                    dve.wait_ge(summed, b + 2)
                step.leave(T, 1)
                last = before[:].rearrange("p (b c) -> p b c", c=cols)[:, :, cols - 1]
                step(nc.vector.tensor_copy(ends[:], last))
                step(nc.vector.memset(first[:], 0.0))
                step(nc.vector.tensor_copy(first[:, 1:T], ends[:, 0:T - 1]))
                step(nc.vector.tensor_tensor(count_f[:], ends[:], first[:], ALU.subtract))
                step(nc.vector.tensor_scalar(count_f[:], count_f[:], float(EC - 1), None, ALU.add))
                step(nc.vector.tensor_copy(count_i[:], count_f[:]))
                step(nc.vector.tensor_scalar(count_i[:], count_i[:], 7, None, ALU.arith_shift_right))
                step(nc.vector.tensor_copy(count_f[:], count_i[:]))
                step(nc.vector.tensor_tensor_scan(cend[:], zeros[:, 0:T], count_f[:], 0.0, ALU.add, ALU.add))
                step(nc.vector.tensor_tensor(cstart[:], cend[:], count_f[:], ALU.subtract))
                step(nc.vector.scalar_tensor_tensor(adj[:], cstart[:], float(EC), first[:], ALU.mult, ALU.subtract))
                step(nc.vector.memset(blk_f[:], -1.0))
                for b in range(T):
                    step(nc.vector.scalar_tensor_tensor(blk_f[:], citer[:], cstart[0:1, b:b + 1], blk_f[:],
                                                        ALU.is_ge, ALU.add))
                step(nc.vector.tensor_copy(blk[:], blk_f[:]))
                with dve.Fori(0, T) as b:
                    step.loop(b, 3)
                    dve.wait_ge(ranks, b + 1)
                    nc.vector.scalar_tensor_tensor(q1[:], ps[1][:, 0:cols], adj[:, bass.ds(b, 1)],
                                                   before[:, tile_of(b, cols)], ALU.add, ALU.add).then_inc(ranked, 1)
                    dve.wait_ge(ranked, b + 2)
                    step(nc.vector.tensor_tensor(q2[:], q1[:], member[:, tile_of(b, cols)], ALU.mult))
                    step(nc.vector.tensor_tensor(pos[:], pos[:], q2[:], ALU.add))
                    step(nc.vector.scalar_tensor_tensor(q2[:], member[:, tile_of(b, cols)],
                                                        thr[0:parts, bass.ds(b, 1)], sub[:], ALU.mult, ALU.subtract))
                    nc.vector.tensor_scalar(sub[:], q2[:], -1.0, None, ALU.mult).then_inc(masks, 1)
                    dve.wait_ge(masks, T + 2 + b)
                step.leave(T, 3)
                step(nc.vector.tensor_copy(rec4[:, :, 1], sub[:]))
                step(nc.vector.tensor_tensor(rec4[:, :, 3], key[:], sub[:], ALU.subtract))
                step(nc.vector.tensor_copy(pos_i[:], pos[:]))
                step(nc.vector.tensor_scalar(row_i[:], pos_i[:], EC - 1, None, ALU.bitwise_and))
                step(nc.vector.tensor_scalar(slot_i[:], pos_i[:], 7, None, ALU.arith_shift_right))
                step(nc.vector.tensor_copy(q1[:], row_i[:]))
                step(nc.vector.tensor_copy(q2[:], slot_i[:]))
                step(nc.vector.scalar_tensor_tensor(pos[:], q1[:], float(chunks), q2[:], ALU.mult, ALU.add))
                step(nc.vector.tensor_copy(row[:], pos[:]))



BATCH = 4
SLOTS = 4


class Step:

    def __init__(self, i, r):
        self.turn, self.slot, self.k = i + r // SLOTS, r % SLOTS, i * SLOTS + r
        self.i, self.r = i, r

    def ahead(self, by, steps):
        later = Step(self.i, self.r + by)
        return None if isinstance(later.k, int) and later.k >= steps else later

    def chunks(self, width):
        return bass.ds(self.k * BATCH * width, BATCH * width)


def edge_steps(eng, steps, body):
    loops = (steps - SLOTS) // SLOTS
    with eng.Fori(0, loops) as i:
        for r in range(SLOTS):
            body(Step(i, r))
    for k in range(loops * SLOTS, steps):
        body(Step(k // SLOTS, k % SLOTS))


def done(step, back=0):
    return SLOTS + step.k + 1 - back


def with_ahead(step, by, steps, fn):
    later = step.ahead(by, steps)
    if later is not None:
        fn(later)


def stage_records(nc, act, rec, rec_s, idx_s, staged, step):
    src = rec[:, step.chunks(FIELDS)]
    if idx_s is not None:
        nc.scalar.copy(idx_s[step.slot][:], src.rearrange("p (u f) -> p u f", f=FIELDS)[:, :, 0]).then_inc(staged, 1)
    nc.scalar.copy(rec_s[step.slot][:], src).then_inc(staged, 1 if idx_s is not None else 2)


def gather_rows(nc, pool, steps, table, idx_s, rows, width, staged, used, landed, go):
    def body(st):
        pool.wait_ge(staged, 2 * st.k + 2)
        pool.sem_inc(go, 1)
        pool.wait_ge(used, done(st, SLOTS))
        pool.sem_inc(go, 1)
        for u in range(BATCH):
            pool.indirect_dma_start(rows[st.slot][:].rearrange("p (u f) -> p u f", u=BATCH)[:, u, 0:width], None, table,
                                    bass.IndirectOffsetOnAxis(ap=idx_s[st.slot][:, u:u + 1], axis=0)
                                    ).then_inc(landed[st.slot], 16)
    edge_steps(pool, steps, body)


def one_hots(nc, c, out, rec_s, step):
    for u in range(BATCH):
        ins = one_hot(nc, c, out, rec_s, step, u)
    return ins


def one_hot(nc, c, out, rec_s, step, u):
    k = u * FIELDS
    return nc.vector.tensor_scalar(out[step.slot][:, u * 128:u * 128 + P], c["iota"][:, 0:P],
                                   rec_s[step.slot][:, k + 1:k + 2], rec_s[step.slot][:, k + 2:k + 3],
                                   ALU.is_equal, ALU.mult)


def tiles_of(nc, eng, engine, blk, step):
    _, tiles = nc.values_load_multi_w_load_instructions(
        blk[0:1, step.chunks(1)], engines=(engine,), min_val=0, max_val=T - 1,
        skip_runtime_bounds_check_because="bucket() writes tiles 0..T-1 only")
    return tiles


def segment_sum(nc, c, name, table, width, rec, blk, chunks, acc, count):
    wide = width + (1 if count else 0)
    steps = chunks // BATCH
    with Stage(nc, name) as s:
        rec_s = [s.sb(f"rec_s{h}", [EC, BATCH * FIELDS]) for h in range(SLOTS)]
        idx_s = [s.sb(f"idx_s{h}", [EC, BATCH], I32) for h in range(SLOTS)]
        rows = [s.sb(f"rows{h}", [EC, BATCH * wide]) for h in range(SLOTS)]
        oh = [s.sb(f"oh{h}", [EC, BATCH * 128]) for h in range(SLOTS)]
        ps = [s.ps(f"ps{h}", [P, BATCH * 512]) for h in range(2)]
        landed = [s.sem(f"landed{h}") for h in range(SLOTS)]
        staged, zeroed, go, counted = s.sem("staged"), s.sem("zeroed"), s.sem("go"), s.sem("counted")
        onehots, used, added = s.sem("onehots"), s.sem("used"), s.sem("added")
        adds = s.sem("adds")
        with s.block() as block:
            @block.scalar
            def _(act):
                def body(st):
                    act.wait_ge(used, done(st, SLOTS))
                    act.wait_ge(onehots, done(st, SLOTS))
                    stage_records(nc, act, rec, rec_s, idx_s, staged, st)
                edge_steps(act, steps, body)

            @block.gpsimd
            def _(pool):
                gather_rows(nc, pool, steps, table, idx_s, rows, width, staged, used, landed, go)

            @block.vector
            def _(dve):
                dve.sem_inc(onehots, SLOTS)
                dve.sem_inc(added, SLOTS)
                if count:
                    for r in rows:
                        nc.vector.memset(r[:].rearrange("p (u f) -> p u f", u=BATCH)[:, :, width], 1.0).then_inc(counted, 1)
                nc.vector.memset(acc[:], 0.0).then_inc(zeroed, 1)
                dve.wait_ge(zeroed, 1)

                def make(st):
                    dve.wait_ge(staged, 2 * st.k + 2)
                    dve.wait_ge(used, done(st, SLOTS))
                    one_hots(nc, c, oh, rec_s, st).then_inc(onehots, 1)

                def body(st):
                    with_ahead(st, 2, steps, make)
                    tiles = tiles_of(nc, dve, mybir.EngineType.DVE, blk, st)
                    dve.wait_ge(used, done(st))
                    for u, b in enumerate(tiles):
                        to = acc[:, bass.ds(b * wide, wide)]
                        last = u == BATCH - 1
                        nc.vector.tensor_tensor(to, to, ps[st.slot % 2][:, u * 512:u * 512 + wide], ALU.add
                                                ).then_inc(added if last else adds, 1)
                        dve.wait_ge(added if last else adds, done(st) if last else (BATCH - 1) * st.k + u + 1)

                for k in range(2):
                    make(Step(0, k))
                edge_steps(dve, steps, body)

            @block.tensor
            def _(pe):
                pe.sem_inc(used, SLOTS)
                if count:
                    pe.wait_ge(counted, SLOTS)

                def body(st):
                    pe.wait_ge(landed[st.slot], 16 * BATCH * (st.turn + 1))
                    pe.wait_ge(onehots, done(st))
                    pe.wait_ge(added, done(st, 2))
                    for u in range(BATCH):
                        ins = nc.tensor.matmul(ps[st.slot % 2][:, u * 512:u * 512 + wide], oh[st.slot][:, u * 128:u * 128 + P],
                                               rows[st.slot][:, u * wide:(u + 1) * wide], start=True, stop=True)
                    ins.then_inc(used, 1)
                edge_steps(pe, steps, body)


def degree(nc, c, name, rec, chunks, deg):
    steps = chunks // BATCH
    with Stage(nc, name) as s:
        first = s.sb("first", [EC, T])
        zeros = s.sb("zeros", [EC, P])
        rec_s = [s.sb(f"rec_s{h}", [EC, BATCH * FIELDS]) for h in range(SLOTS)]
        oh = [s.sb(f"oh{h}", [EC, BATCH * 128]) for h in range(SLOTS)]
        tile = [s.sb(f"tile{h}", [EC, BATCH * T]) for h in range(SLOTS)]
        ps = s.ps("ps", [P, 512])
        made, staged, done_all, taken = s.sem("made"), s.sem("staged"), s.sem("done_all"), s.sem("taken")
        onehots, used = s.sem("onehots"), s.sem("used")
        with s.block() as block:
            @block.gpsimd
            def _(pool):
                nc.gpsimd.iota(first[:], pattern=[[P, T]], base=0, channel_multiplier=0,
                               allow_small_or_imprecise_dtypes=True).then_inc(made, 1)
                nc.gpsimd.memset(zeros[:], 0.0).then_inc(made, 1)

            @block.scalar
            def _(act):
                def body(st):
                    act.wait_ge(onehots, done(st, SLOTS))
                    stage_records(nc, act, rec, rec_s, None, staged, st)
                edge_steps(act, steps, body)

            @block.vector
            def _(dve):
                dve.sem_inc(onehots, SLOTS)
                dve.wait_ge(made, 2)

                def body(st):
                    dve.wait_ge(staged, 2 * st.k + 2)
                    dve.wait_ge(used, done(st, SLOTS))
                    one_hots(nc, c, oh, rec_s, st)
                    at = rec_s[st.slot][:].rearrange("p (u f) -> p u f", u=BATCH)[:, :, 3:4]
                    nc.vector.tensor_tensor(tile[st.slot][:].rearrange("p (u t) -> p u t", u=BATCH),
                                            first[:].unsqueeze(1).broadcast_to([EC, BATCH, T]),
                                            at.broadcast_to([EC, BATCH, T]), ALU.is_equal).then_inc(onehots, 1)
                edge_steps(dve, steps, body)
                dve.wait_ge(done_all, 1)
                nc.vector.tensor_copy(deg[:], ps[:, 0:T]).then_inc(taken, 1)
                dve.wait_ge(taken, 1)

            @block.tensor
            def _(pe):
                pe.sem_inc(used, SLOTS)
                pe.wait_ge(made, 2)
                nc.tensor.matmul(ps[:, 0:T], zeros[:], zeros[:, 0:T], start=True, stop=False, skip_group_check=True)

                def body(st):
                    pe.wait_ge(onehots, done(st))
                    for u in range(BATCH):
                        ins = nc.tensor.matmul(ps[:, 0:T], oh[st.slot][:, u * 128:u * 128 + P], tile[st.slot][:, u * T:(u + 1) * T],
                                               start=False, stop=False, skip_group_check=True)
                    ins.then_inc(used, 1)
                edge_steps(pe, steps, body)
                nc.tensor.matmul(ps[:, 0:T], zeros[:], zeros[:, 0:T], start=False, stop=True,
                                 skip_group_check=True).then_inc(done_all, 1)


def turn_one_hots(nc, c, ps_t, oh, step):
    for u in range(BATCH):
        ins = nc.tensor.transpose(ps_t[step.slot % 2][:, u * EC:(u + 1) * EC], oh[step.slot][:, u * 128:u * 128 + P], c["ident"][:])
    return ins


def edge_scores(nc, c, name, k_table, q, rec, blk, chunks, heads, scale, scores):
    steps = chunks // BATCH
    with Stage(nc, name) as s:
        rec_s = [s.sb(f"rec_s{h}", [EC, BATCH * FIELDS]) for h in range(SLOTS)]
        idx_s = [s.sb(f"idx_s{h}", [EC, BATCH], I32) for h in range(SLOTS)]
        rows = [s.sb(f"rows{h}", [EC, BATCH * D]) for h in range(SLOTS)]
        oh = [s.sb(f"oh{h}", [EC, BATCH * 128]) for h in range(SLOTS)]
        oht = [s.sb(f"oht{h}", [P, BATCH * EC]) for h in range(2)]
        prod = [s.sb(f"prod{h}", [EC, BATCH * D]) for h in range(2)]
        ps_t = [s.ps(f"ps_t{h}", [P, 512]) for h in range(2)]
        ps_q = [s.ps(f"ps_q{h}", [EC, BATCH * D]) for h in range(2)]
        landed = [s.sem(f"landed{h}") for h in range(SLOTS)]
        staged, go = s.sem("staged"), s.sem("go")
        onehots, turned, kept = s.sem("onehots"), s.sem("turned"), s.sem("kept")
        spread, multiplied, reduced = s.sem("spread"), s.sem("multiplied"), s.sem("reduced")
        with s.block() as block:
            @block.scalar
            def _(act):
                act.sem_inc(kept, SLOTS)

                def stage(st):
                    act.wait_ge(multiplied, done(st, SLOTS))
                    act.wait_ge(onehots, done(st, SLOTS))
                    stage_records(nc, act, rec, rec_s, idx_s, staged, st)

                def body(st):
                    act.wait_ge(turned, done(st))
                    act.wait_ge(spread, done(st, 2))
                    nc.scalar.copy(oht[st.slot % 2][:], ps_t[st.slot % 2][:]).then_inc(kept, 1)
                    with_ahead(st, 3, steps, stage)

                for k in range(3):
                    stage(Step(0, k))
                edge_steps(act, steps, body)

            @block.gpsimd
            def _(pool):
                gather_rows(nc, pool, steps, k_table, idx_s, rows, D, staged, multiplied, landed, go)

            @block.vector
            def _(dve):
                dve.sem_inc(onehots, SLOTS)
                dve.sem_inc(multiplied, SLOTS)
                dve.sem_inc(reduced, SLOTS)

                def make(st):
                    dve.wait_ge(staged, 2 * st.k + 2)
                    dve.wait_ge(turned, done(st, SLOTS))
                    one_hots(nc, c, oh, rec_s, st).then_inc(onehots, 1)

                def body(st):
                    with_ahead(st, 2, steps, make)
                    dve.wait_ge(spread, done(st))
                    dve.wait_ge(landed[st.slot], 16 * BATCH * (st.turn + 1))
                    dve.wait_ge(reduced, done(st, 2))
                    nc.vector.scalar_tensor_tensor(prod[st.slot % 2][:], ps_q[st.slot % 2][:], float(scale), rows[st.slot][:],
                                                   ALU.mult, ALU.mult).then_inc(multiplied, 1)
                    dve.wait_ge(multiplied, done(st))
                    nc.vector.tensor_reduce(scores[:, st.chunks(heads)],
                                            prod[st.slot % 2][:].rearrange("p (h d) -> p h d", h=BATCH * heads),
                                            AX.X, ALU.add).then_inc(reduced, 1)
                for k in range(2):
                    make(Step(0, k))
                edge_steps(dve, steps, body)

            @block.tensor
            def _(pe):
                pe.sem_inc(turned, SLOTS)
                pe.sem_inc(spread, SLOTS)

                def turn(st):
                    pe.wait_ge(onehots, done(st))
                    pe.wait_ge(kept, done(st, 2))
                    turn_one_hots(nc, c, ps_t, oh, st).then_inc(turned, 1)

                def body(st):
                    with_ahead(st, 1, steps, turn)
                    tiles = tiles_of(nc, pe, mybir.EngineType.PE, blk, st)
                    pe.wait_ge(kept, done(st))
                    pe.wait_ge(multiplied, done(st, 2))
                    for u, b in enumerate(tiles):
                        ins = nc.tensor.matmul(ps_q[st.slot % 2][:, u * D:(u + 1) * D], oht[st.slot % 2][:, u * EC:(u + 1) * EC],
                                               q[:, bass.ds(b * D, D)], start=True, stop=True)
                    ins.then_inc(spread, 1)

                turn(Step(0, 0))
                edge_steps(pe, steps, body)


BIG = 1e30


def segment_max(nc, c, name, values, stride, heads, rec, blk, chunks, best, table, stored, side=()):
    steps = chunks // BATCH
    room = 128 // BATCH
    assert 3 * heads <= room
    with Stage(nc, name) as s:
        rec_s = [s.sb(f"rec_s{h}", [EC, BATCH * FIELDS]) for h in range(SLOTS)]
        val_s = [s.sb(f"val_s{h}", [EC, BATCH * heads]) for h in range(SLOTS)] if table is None else None
        idx_s = [s.sb(f"idx_s{h}", [EC, BATCH], I32) for h in range(SLOTS)] if table is not None else None
        rows = [s.sb(f"rows{h}", [EC, BATCH * stride]) for h in range(SLOTS)] if table is not None else None
        away = [s.sb(f"away{h}", [EC, BATCH * 128], BF16) for h in range(SLOTS)]
        parts = [s.sb(f"parts{h}", [EC, 128], BF16) for h in range(2)]
        turned = [s.sb(f"turned{h}", [128, EC], BF16) for h in range(2)]
        rest = s.sb("rest", [EC, BATCH * heads])
        top = [s.sb(f"top{h}", [P, BATCH * heads]) for h in range(2)]
        select = s.sb("select", [128, BATCH * heads * 128], BF16)
        ident_b = s.sb("ident_b", [EC, EC], BF16)
        far = s.sb("far", [EC, 512], BF16)
        ps = [s.ps(f"ps{u}", [P, heads * EC]) for u in range(2)]
        ps_p = [s.ps(f"ps_p{u}", [128, 1024], BF16) for u in range(2)]
        landed = [s.sem(f"landed{h}") for h in range(SLOTS)] if table is not None else None
        staged, go, merges, splits = s.sem("staged"), s.sem("go"), s.sem("merges"), s.sem("splits")
        selects, made = s.sem("selects"), s.sem("made")
        aways, split, merged = s.sem("aways"), s.sem("split"), s.sem("merged")
        flipped, kept = s.sem("flipped"), s.sem("kept")
        saved = s.sem("saved")
        spread = [s.sem(f"spread{u}") for u in range(BATCH)]
        reduced = [s.sem(f"reduced{u}") for u in range(BATCH)]
        assert table is None or not side
        program = scatters(nc, s, side)
        with s.block() as block:
            @block.scalar
            def _(act):
                for sem in (aways, kept, *((saved,) if table is not None else ())):
                    act.sem_inc(sem, SLOTS)

                def stage(st):
                    act.wait_ge(aways, done(st, SLOTS))
                    act.wait_ge(split, done(st, SLOTS))
                    if table is None:
                        nc.scalar.copy(val_s[st.slot][:], values[:, st.chunks(stride)]).then_inc(staged, 1)
                        nc.scalar.copy(rec_s[st.slot][:], rec[:, st.chunks(FIELDS)]).then_inc(staged, 1)
                    else:
                        stage_records(nc, act, rec, rec_s, idx_s, staged, st)

                def make(st):
                    act.wait_ge(staged, 2 * st.k + 2)
                    act.wait_ge(spread[BATCH - 1], done(st, SLOTS))
                    for u in range(BATCH):
                        ins = nc.scalar.activation(away[st.slot][:, u * 128:u * 128 + P], c["iota"][:, 0:P], ACT.Square,
                                                   bias=rec_s[st.slot][:, u * FIELDS + 1:u * FIELDS + 2], scale=-1.0)
                    ins.then_inc(aways, 1)

                def keep(st):
                    act.wait_ge(flipped, done(st))
                    act.wait_ge(spread[BATCH - 1], done(st, 2))
                    nc.scalar.copy(turned[st.slot % 2][:], ps_p[st.slot % 2][:, 0:EC]).then_inc(kept, 1)

                def body(st):
                    with_ahead(st, 2, steps, make)
                    with_ahead(st, 1, steps, keep)
                    if table is not None:
                        act.wait_ge(landed[st.slot], 16 * BATCH * (st.turn + 1))
                        nc.scalar.copy(stored[:, st.chunks(stride)], rows[st.slot][:]).then_inc(saved, 1)
                    with_ahead(st, 4, steps, stage)

                for k in range(4):
                    stage(Step(0, k))
                for k in range(2):
                    make(Step(0, k))
                keep(Step(0, 0))
                edge_steps(act, steps, body)
                if table is not None:
                    act.wait_ge(saved, SLOTS + steps)

            @block.gpsimd
            def _(pool):
                nc.gpsimd.memset(select[:], 0.0).then_inc(selects, 1)
                for part in range(3):
                    pool.wait_ge(selects, part + 1)
                    view = select[:].rearrange("p (u h n) -> p u h n", u=BATCH, h=heads)
                    nc.gpsimd.affine_select(out=view, in_=view, compare_op=ALU.not_equal, fill=1.0, base=-part * heads,
                                            pattern=[[-room, BATCH], [-1, heads], [0, 128]],
                                            channel_multiplier=1).then_inc(selects, 1)
                if table is None:
                    program(pool)
                    return

                def body(st):
                    pool.wait_ge(staged, 2 * st.k + 2)
                    pool.sem_inc(go, 1)
                    pool.wait_ge(saved, done(st, SLOTS))
                    pool.sem_inc(go, 1)
                    pool.wait_ge(split, done(st, SLOTS))
                    pool.sem_inc(go, 1)
                    for u in range(BATCH):
                        pool.indirect_dma_start(rows[st.slot][:, u * stride:(u + 1) * stride], None, table,
                                                bass.IndirectOffsetOnAxis(ap=idx_s[st.slot][:, u:u + 1], axis=0)
                                                ).then_inc(landed[st.slot], 16)
                edge_steps(pool, steps, body)

            @block.vector
            def _(dve):
                for sem in (split, merged, *reduced):
                    dve.sem_inc(sem, SLOTS)
                nc.vector.tensor_copy(ident_b[:], c["ident"][:]).then_inc(made, 1)
                for k in range(512 // EC):
                    nc.vector.tensor_scalar(far[:, k * EC:(k + 1) * EC], c["ident"][:], -BIG, None, ALU.mult).then_inc(made, 1)
                for part in parts:
                    nc.vector.memset(part[:], 0.0).then_inc(made, 1)
                dve.wait_ge(made, 1 + 512 // EC + 2)

                def split_steps(st):
                    if table is None:
                        val = val_s[st.slot][:].rearrange("p (u h) -> p u h", u=BATCH)
                    else:
                        val = rows[st.slot][:].rearrange("p (u f) -> p u f", u=BATCH)[:, :, stride - heads:stride]
                    left = rest[:].rearrange("p (u h) -> p u h", u=BATCH)
                    out = parts[st.slot % 2][:].rearrange("p (u r) -> p u r", u=BATCH)
                    part = [out[:, :, n * heads:(n + 1) * heads] for n in range(3)]

                    def after_last(n, op, *args):
                        dve.wait_ge(splits, 4 * st.k + n)
                        op(*args).then_inc(split if n == 4 else splits, 1)

                    def begin():
                        if table is None:
                            dve.wait_ge(staged, 2 * st.k + 2)
                        else:
                            dve.wait_ge(landed[st.slot], 16 * BATCH * (st.turn + 1))
                        dve.wait_ge(flipped, done(st, 2))
                        dve.wait_ge(split, done(st, 1))
                        nc.vector.tensor_copy(part[0], val).then_inc(splits, 1)
                    return [begin,
                            lambda: after_last(1, nc.vector.tensor_tensor, left, val, part[0], ALU.subtract),
                            lambda: after_last(2, nc.vector.tensor_copy, part[1], left),
                            lambda: after_last(3, nc.vector.tensor_tensor, left, left, part[1], ALU.subtract),
                            lambda: after_last(4, nc.vector.tensor_copy, part[2], left)]

                def reduce(st, u):
                    dve.wait_ge(spread[u], done(st))
                    if u == 0:
                        dve.wait_ge(merged, done(st, 2))
                    nc.vector.tensor_reduce(top[st.slot % 2][:, u * heads:(u + 1) * heads],
                                            ps[u % 2][:].rearrange("p (h e) -> p h e", e=EC),
                                            AX.X, ALU.max).then_inc(reduced[u], 1)

                def merge(st, u, b):
                    if u == 0:
                        dve.wait_ge(reduced[BATCH - 1], done(st))
                        dve.wait_ge(merged, done(st, 1))
                    else:
                        dve.wait_ge(merges, (BATCH - 1) * st.k + u)
                    to = best[:, bass.ds(b * heads, heads)]
                    nc.vector.tensor_tensor(to, to, top[st.slot % 2][:, u * heads:(u + 1) * heads], ALU.max
                                            ).then_inc(merged if u == BATCH - 1 else merges, 1)

                def body(st):
                    later, after = st.ahead(1, steps), st.ahead(3, steps)
                    between = split_steps(after) if after is not None else []
                    if later is not None:
                        reduce(later, 0)
                    tiles = tiles_of(nc, dve, mybir.EngineType.DVE, blk, st)
                    for u, b in enumerate(tiles):
                        if later is not None and u > 0:
                            reduce(later, u)
                        merge(st, u, b)
                        for part in between[u:u + 1] if u < 3 else between[3:5]:
                            part()

                for k in range(3):
                    for part in split_steps(Step(0, k)):
                        part()
                for u in range(BATCH):
                    reduce(Step(0, 0), u)
                edge_steps(dve, steps, body)
                dve.wait_ge(merged, SLOTS + steps)

            @block.tensor
            def _(pe):
                for sem in (flipped, *spread):
                    pe.sem_inc(sem, SLOTS)
                pe.wait_ge(selects, 4)
                pe.wait_ge(made, 1 + 512 // EC + 2)

                def flip(st):
                    pe.wait_ge(split, done(st))
                    pe.wait_ge(kept, done(st, 2))
                    nc.tensor.transpose(ps_p[st.slot % 2][:, 0:EC], parts[st.slot % 2][:], ident_b[:]).then_inc(flipped, 1)

                def body(st):
                    pe.wait_ge(kept, done(st))
                    pe.wait_ge(aways, done(st))
                    for u in range(BATCH):
                        pe.wait_ge(reduced[(u + 2) % BATCH], done(st, 1 if u < 2 else 0))
                        for bank in range(heads * EC // 512):
                            nc.tensor.matmul(ps[u % 2][:, bank * 512:(bank + 1) * 512], away[st.slot][:, u * 128:u * 128 + P],
                                             far[:], start=True, stop=False, skip_group_check=True)
                            for h in range(bank * 4, bank * 4 + 4):
                                at = (u * heads + h) * 128
                                ins = nc.tensor.matmul(ps[u % 2][:, h * EC:(h + 1) * EC], select[:, at:at + P],
                                                       turned[st.slot % 2][:], start=False, stop=h % 4 == 3,
                                                       skip_group_check=True)
                        ins.then_inc(spread[u], 1)
                    with_ahead(st, 1, steps, flip)
                flip(Step(0, 0))
                edge_steps(pe, steps, body)


def softmax_sum(nc, c, name, heads, hd, rec, blk, chunks, acc, per_node, pn, table, scores, stored, leaky):
    vw = heads * hd
    wide = vw + heads
    steps = chunks // BATCH
    with Stage(nc, name) as s:
        rec_s = [s.sb(f"rec_s{h}", [EC, BATCH * FIELDS]) for h in range(SLOTS)]
        idx_s = [s.sb(f"idx_s{h}", [EC, BATCH], I32) for h in range(SLOTS)] if table is not None else None
        rows = [s.sb(f"rows{h}", [EC, BATCH * vw]) for h in range(SLOTS)] if table is not None else None
        oh = [s.sb(f"oh{h}", [EC, BATCH * 128]) for h in range(SLOTS)]
        oht = [s.sb(f"oht{h}", [P, BATCH * EC]) for h in range(2)]
        arg = [s.sb(f"arg{h}", [EC, BATCH * heads]) for h in range(SLOTS)]
        arg2 = s.sb("partial", [EC, BATCH * heads])
        msg = [s.sb(f"msg{h}", [EC, BATCH * wide]) for h in range(SLOTS)]
        ps_t = [s.ps(f"ps_t{h}", [P, 512]) for h in range(2)]
        ps_n = [s.ps(f"ps_n{h}", [EC, 512]) for h in range(2)]
        ps_a = s.ps("ps_a", [P, BATCH * 512])
        landed = [s.sem(f"landed{h}") for h in range(SLOTS)]
        staged, zeroed, go, inner = s.sem("staged"), s.sem("zeroed"), s.sem("go"), s.sem("inner")
        onehots, turned, kept, spread = s.sem("onehots"), s.sem("turned"), s.sem("kept"), s.sem("spread")
        args, exps = s.sem("args"), s.sem("exps")
        msgs = [s.sem(f"msgs{u}") for u in range(BATCH)]
        summed = [s.sem(f"summed{u}") for u in range(BATCH)]
        added = [s.sem(f"added{u}") for u in range(BATCH)]

        def weights(st):
            return msg[st.slot][:].rearrange("p (u f) -> p u f", u=BATCH)[:, :, vw:wide]

        with s.block() as block:
            @block.scalar
            def _(act):
                act.sem_inc(kept, SLOTS)
                act.sem_inc(exps, SLOTS)

                def stage(st):
                    act.wait_ge(onehots, done(st, SLOTS))
                    if table is not None:
                        act.wait_ge(msgs[BATCH - 1], done(st, SLOTS))
                    stage_records(nc, act, rec, rec_s, idx_s, staged, st)

                def keep(st):
                    act.wait_ge(turned, done(st))
                    act.wait_ge(spread, done(st, 2))
                    nc.scalar.copy(oht[st.slot % 2][:], ps_t[st.slot % 2][:]).then_inc(kept, 1)

                def exponentiate(st):
                    act.wait_ge(args, done(st))
                    act.wait_ge(summed[BATCH - 1], done(st, SLOTS))
                    nc.scalar.activation(weights(st), arg[st.slot][:].rearrange("p (u h) -> p u h", u=BATCH),
                                         ACT.Exp).then_inc(exps, 1)

                def body(st):
                    with_ahead(st, 1, steps, exponentiate)
                    with_ahead(st, 4, steps, stage)
                    with_ahead(st, 3, steps, keep)

                for k in range(4):
                    stage(Step(0, k))
                for k in range(3):
                    keep(Step(0, k))
                exponentiate(Step(0, 0))
                edge_steps(act, steps, body)

            if table is not None:
                @block.gpsimd
                def _(pool):
                    gather_rows(nc, pool, steps, table, idx_s, rows, vw, staged, msgs[BATCH - 1], landed, go)

            @block.vector
            def _(dve):
                for sem in (onehots, args, *msgs, *added):
                    dve.sem_inc(sem, SLOTS)
                nc.vector.memset(acc[:], 0.0).then_inc(zeroed, 1)
                dve.wait_ge(zeroed, 1)

                def make(st, u):
                    if u == 0:
                        dve.wait_ge(staged, 2 * st.k + 2)
                        dve.wait_ge(summed[BATCH - 1], done(st, SLOTS))
                    ins = one_hot(nc, c, oh, rec_s, st, u)
                    if u == BATCH - 1:
                        ins.then_inc(onehots, 1)

                def argue(st):
                    node = ps_n[st.slot % 2][:, 0:BATCH * pn].rearrange("p (u f) -> p u f", u=BATCH)
                    w = arg[st.slot][:].rearrange("p (u h) -> p u h", u=BATCH)
                    a = arg2[:].rearrange("p (u h) -> p u h", u=BATCH)

                    def begin(*op):
                        dve.wait_ge(spread, done(st))
                        dve.wait_ge(exps, done(st, SLOTS))
                        dve.wait_ge(args, done(st, 1))
                        nc.vector.tensor_tensor(*op).then_inc(inner if leaky else args, 1)

                    def after_last(n, op, *operands):
                        dve.wait_ge(inner, 3 * st.k + n)
                        op(*operands).then_inc(args if n == 3 else inner, 1)

                    if not leaky:
                        return [lambda: begin(w, scores[:, st.chunks(heads)].rearrange("p (u h) -> p u h", u=BATCH), node,
                                              ALU.subtract)]
                    from_source = stored[:, st.chunks(wide)].rearrange("p (u f) -> p u f", u=BATCH)[:, :, vw:wide]
                    return [lambda: begin(a, from_source, node[:, :, 0:heads], ALU.add),
                            lambda: after_last(1, nc.vector.scalar_tensor_tensor, w, a, 0.2, a, ALU.mult, ALU.max),
                            lambda: after_last(2, nc.vector.tensor_tensor, a, w, node[:, :, heads:2 * heads], ALU.subtract),
                            lambda: after_last(3, nc.vector.tensor_scalar, w, a, 0.0, None, ALU.min)]

                def ready(st):
                    dve.wait_ge(exps, done(st))
                    if table is not None:
                        dve.wait_ge(landed[st.slot], 16 * BATCH * (st.turn + 1))

                def multiply(st, u):
                    if table is not None:
                        vals = rows[st.slot][:, u * vw:(u + 1) * vw]
                    else:
                        vals = stored[:, bass.ds((st.k * BATCH + u) * wide, vw)]
                    nc.vector.tensor_tensor(
                        msg[st.slot][:, u * wide:u * wide + vw].rearrange("p (h d) -> p h d", d=hd),
                        vals.rearrange("p (h d) -> p h d", d=hd),
                        weights(st)[:, u, :].unsqueeze(2).broadcast_to([EC, heads, hd]), ALU.mult).then_inc(msgs[u], 1)

                def body(st):
                    later, third = st.ahead(1, steps), st.ahead(3, steps)
                    arguing = argue(later) if later is not None else []
                    for u in range(BATCH):
                        for part in arguing[u:u + 1]:
                            part()
                        if third is not None:
                            make(third, u)
                    tiles = tiles_of(nc, dve, mybir.EngineType.DVE, blk, st)
                    after = st.ahead(1, steps)
                    for u, b in enumerate(tiles):
                        dve.wait_ge(summed[u], done(st))
                        if u > 0:
                            dve.wait_ge(added[u - 1], done(st))
                        to = acc[:, bass.ds(b * wide, wide)]
                        nc.vector.tensor_tensor(to, to, ps_a[:, u * 512:u * 512 + wide], ALU.add).then_inc(added[u], 1)
                        if after is not None:
                            if u == 0:
                                ready(after)
                            multiply(after, u)
                    dve.wait_ge(added[BATCH - 1], done(st))

                for k in range(3):
                    for u in range(BATCH):
                        make(Step(0, k), u)
                for part in argue(Step(0, 0)):
                    part()
                ready(Step(0, 0))
                for u in range(BATCH):
                    multiply(Step(0, 0), u)
                edge_steps(dve, steps, body)

            @block.tensor
            def _(pe):
                for sem in (turned, spread, *summed):
                    pe.sem_inc(sem, SLOTS)

                def turn(st):
                    pe.wait_ge(onehots, done(st))
                    pe.wait_ge(kept, done(st, 2))
                    turn_one_hots(nc, c, ps_t, oh, st).then_inc(turned, 1)

                def node_rows(st):
                    tiles = tiles_of(nc, pe, mybir.EngineType.PE, blk, st)
                    pe.wait_ge(kept, done(st))
                    pe.wait_ge(args, done(st, 2))
                    for u, b in enumerate(tiles):
                        ins = nc.tensor.matmul(ps_n[st.slot % 2][:, u * pn:(u + 1) * pn], oht[st.slot % 2][:, u * EC:(u + 1) * EC],
                                               per_node[:, bass.ds(b * pn, pn)], start=True, stop=True)
                    ins.then_inc(spread, 1)

                def body(st):
                    for u in range(BATCH):
                        pe.wait_ge(msgs[u], done(st))
                        pe.wait_ge(added[u], done(st, 1))
                        nc.tensor.matmul(ps_a[:, u * 512:u * 512 + wide], oh[st.slot][:, u * 128:u * 128 + P],
                                         msg[st.slot][:, u * wide:(u + 1) * wide], start=True, stop=True).then_inc(summed[u], 1)
                    with_ahead(st, 3, steps, turn)
                    with_ahead(st, 2, steps, node_rows)

                for k in range(3):
                    turn(Step(0, k))
                    if k < 2:
                        node_rows(Step(0, k))
                edge_steps(pe, steps, body)



def tiles_loop(eng, body):
    with eng.Fori(0, T // RING) as i:
        for u in range(RING):
            body(i * RING + u, u)


def layernorm(nc, name, src, dst, gamma=None, beta=None):
    with Stage(nc, name) as s:
        stats = s.sb("stats", [P, T * 6])
        mv = s.sb("mv", [P, T * 2])
        var = s.sb("var", [P, T])
        std = s.sb("std", [P, T])
        rstd = s.sb("rstd", [P, T])
        gb = s.sb("gb", [P, 2 * D]) if gamma is not None else None
        loaded, steps, eps_added, rooted = s.sem("loaded"), s.sem("steps"), s.sem("eps_added"), s.sem("rooted")
        with s.block() as block:
            if gamma is not None:
                @block.sync
                def _(sp):
                    sp.dma_start(gb[:, 0:D], gamma.partition_broadcast(P)).then_inc(loaded, 16)
                    sp.dma_start(gb[:, D:2 * D], beta.partition_broadcast(P)).then_inc(loaded, 16)

            @block.scalar
            def _(act):
                act.wait_ge(eps_added, 1)
                nc.scalar.activation(std[:], var[:], ACT.Sqrt).then_inc(rooted, 1)

            @block.vector
            def _(dve):
                step = Steps(dve, steps)
                tiles_loop(dve, lambda t, u: nc.vector.bn_stats(stats[:, tile_of(t, 6)], src[:, tile_of(t, D)]
                                                                ).then_inc(steps, 1))
                step.n = T
                dve.wait_ge(steps, T)
                for t in range(T):
                    nc.vector.bn_aggr(mv[:, 2 * t:2 * t + 2], stats[:, 6 * t:6 * t + 6]).then_inc(steps, 1)
                step.n = 2 * T
                dve.wait_ge(steps, 2 * T)
                mv2 = mv[:].rearrange("p (t k) -> p t k", k=2)
                nc.vector.tensor_scalar(var[:], mv2[:, :, 1], EPS, None, ALU.add).then_inc(eps_added, 1)
                dve.wait_ge(rooted, 1)
                step(nc.vector.reciprocal(rstd[:], std[:]))
                tiles_loop(dve, lambda t, u: nc.vector.tensor_scalar(
                    dst[:, tile_of(t, D)], src[:, tile_of(t, D)], mv[:, bass.ds(2 * t, 1)], rstd[:, bass.ds(t, 1)],
                    ALU.subtract, ALU.mult).then_inc(steps, 1))
                step.n += T
                dve.wait_ge(steps, step.n)
                if gamma is not None:
                    dve.wait_ge(loaded, 32)
                    full = as_tiles(dst, D)
                    step(nc.vector.tensor_tensor(full, full, gb[:, 0:D].unsqueeze(1).broadcast_to([P, T, D]), ALU.mult))
                    step(nc.vector.tensor_tensor(full, full, gb[:, D:2 * D].unsqueeze(1).broadcast_to([P, T, D]), ALU.add))


def turn_tiles(nc, c, name, src, width, dst, stride=None, table=None):
    stride = stride or width
    cw = min(width, 128)
    nch = width // cw
    with Stage(nc, name) as s:
        tile = [s.sb(f"tile{u}", [P, width]) for u in range(RING)]
        ps = [s.ps(f"ps{u}", [cw, nch * P]) for u in range(RING)]
        copied = s.sem("copied")
        turned = s.sem("turned")
        stored = s.sem("stored")
        go = s.sem("go")
        tabled = s.sem("tabled")
        with s.block() as block:
            if table is not None:
                @block.sync
                def _(sp):
                    sp.dma_start(by_tile(table, width), as_tiles(src, width)).then_inc(tabled, 16)
                    sp.wait_ge(tabled, 16)

            @block.scalar
            def _(act):
                def body(t, u):
                    act.wait_ge(turned, t + 1)
                    nc.scalar.copy(tile[u][:], src[:, bass.ds(t * stride, width)]).then_inc(copied, 1)
                tiles_loop(act, body)

            @block.tensor
            def _(pe):
                pe.sem_inc(turned, RING)

                def body(t, u):
                    pe.wait_ge(copied, t + 1)
                    pe.wait_ge(stored, t + 1)
                    pe.sem_inc(go, 1)
                    for k in range(nch):
                        ins = nc.tensor.transpose(ps[u][:, k * P:(k + 1) * P], tile[u][:, k * cw:(k + 1) * cw],
                                                  c["ident"][0:P, 0:P])
                    ins.then_inc(turned, 1)
                tiles_loop(pe, body)

            @block.vector
            def _(dve):
                dve.sem_inc(stored, RING)

                def body(t, u):
                    dve.wait_ge(turned, RING + t + 1)
                    for k in range(nch):
                        ins = nc.vector.tensor_copy(dst[0:cw, bass.ds(t * P + k * N, P)], ps[u][:, k * P:(k + 1) * P])
                    ins.then_inc(stored, 1)
                tiles_loop(dve, body)


def project(nc, c, name, sources, wide, mode, dst, bias=None, scale=None, stride=None, table=None):
    stride = stride or wide
    with Stage(nc, name) as s:
        w = [s.sb(f"w{k}", [kp, wide]) for k, (_, kp, _, _) in enumerate(sources)]
        lhs = [s.sb(f"lhs{u}", [128, len(sources) * P]) for u in range(RING)]
        brow = s.sb("brow", [1, wide]) if bias is not None else None
        ps = [s.ps(f"ps{u}", [P, 512]) for u in range(RING)]
        loaded = s.sem("loaded")
        copied = s.sem("copied")
        multiplied = s.sem("multiplied")
        stored = s.sem("stored")
        tabled = s.sem("tabled")
        with s.block() as block:
            @block.sync
            def _(sp):
                for k, (_, _, _, wd) in enumerate(sources):
                    sp.dma_start(w[k][:], wd).then_inc(loaded, 16)
                if bias is not None:
                    sp.dma_start(brow[:], bias).then_inc(loaded, 16)
                if table is not None:
                    for t in range(0, T, RING):
                        sp.wait_ge(stored, RING + t + RING)
                        sp.dma_start(by_tile(table, wide)[:, t:t + RING, :], as_tiles(dst, stride)[:, t:t + RING, :]
                                     ).then_inc(tabled, 16)
                    sp.wait_ge(tabled, 16 * (T // RING))

            @block.scalar
            def _(act):
                def body(t, u):
                    act.wait_ge(multiplied, t + 1)
                    for k, (src, kp, ch, _) in enumerate(sources):
                        nc.scalar.copy(lhs[u][0:kp, k * P:(k + 1) * P], src[0:kp, bass.ds(t * P + ch * N, P)]).then_inc(copied, 1)
                tiles_loop(act, body)

            @block.tensor
            def _(pe):
                pe.sem_inc(multiplied, RING)
                pe.wait_ge(loaded, 16 * (len(sources) + (bias is not None)))

                def body(t, u):
                    pe.wait_ge(copied, (t + 1) * len(sources))
                    pe.wait_ge(stored, t + 1)
                    if bias is not None:
                        nc.tensor.matmul(ps[u][:, 0:wide], c["ones"][0:1, 0:P], brow[:], start=True, stop=False)
                    for k, (_, kp, _, _) in enumerate(sources):
                        ins = nc.tensor.matmul(ps[u][:, 0:wide], lhs[u][0:kp, k * P:(k + 1) * P], w[k][:],
                                               start=(k == 0 and bias is None), stop=(k == len(sources) - 1))
                    ins.then_inc(multiplied, 1)
                tiles_loop(pe, body)

            @block.vector
            def _(dve):
                dve.sem_inc(stored, RING)

                def body(t, u):
                    dve.wait_ge(multiplied, RING + t + 1)
                    out = ps[u][:, 0:wide]
                    to = dst[:, bass.ds(t * stride, wide)]
                    if mode == "copy":
                        ins = nc.vector.tensor_copy(to, out)
                    elif mode == "scale":
                        ins = nc.vector.tensor_scalar(to, out, scale[:, bass.ds(t, 1)], None, ALU.mult)
                    elif mode == "add":
                        ins = nc.vector.tensor_tensor(to, to, out, ALU.add)
                    elif mode == "relu_add":
                        ins = nc.vector.scalar_tensor_tensor(to, out, 0.0, to, ALU.max, ALU.add)
                    ins.then_inc(stored, 1)
                tiles_loop(dve, body)



def network(nc, c, name, xt, experts, hidden, act_fn, w1_d, b1_d, w2_d, b2_d, gate, acc, picked=None, side=()):
    fc = hidden // 128
    jh = fc // 2
    twin = min(experts, 2)
    steps_per = T // RING
    PRIME = 4 * steps_per
    with Stage(nc, name) as s:
        w1 = [s.sb(f"w1_{e}", [128, DC * hidden]) for e in range(twin)]
        w2 = [s.sb(f"w2_{e}", [128, fc * D]) for e in range(twin)]
        b1 = s.sb("b1", [128, experts * fc])
        b2 = s.sb("b2", [experts, D])
        gt = s.sb("gt", [experts, RING * P]) if gate is not None else None
        gs = [s.sb(f"gs{u}", [P, experts]) for u in range(RING)] if gate is not None else None
        h = [s.sb(f"h{q}", [128, jh * GROUP]) for q in range(2)]
        ps_h = [s.ps(f"ps_h{r}", [128, 1024]) for r in range(2)]
        ps_y = s.ps("ps_y", [P, 3 * 512])
        w_in = [s.sem(f"w_in{e}") for e in range(twin)]
        small = s.sem("small")
        hidden_ready = s.sem("hidden_ready")
        activated = s.sem("activated")
        multiplied = s.sem("multiplied")
        summed = s.sem("summed")
        go, g_copied, g_turned, g_kept, biased, bias_kept = (s.sem(n) for n in (
            "go", "g_copied", "g_turned", "g_kept", "biased", "bias_kept"))

        def ycols(k):
            return ps_y[:, (k // 2) * 512 + (k % 2) * D:(k // 2) * 512 + (k % 2) * D + D]

        program = scatters(nc, s, side)
        with s.block() as block:
            if side:
                @block.gpsimd
                def _(pool):
                    program(pool)

            @block.sync
            def _(sp):
                def weights_of(ex):
                    if picked is None:
                        return ex
                    return sp.value_load(picked[0:1, bass.ds(ex, 1)], min_val=0, max_val=w1_d.shape[0] - 1)

                for k in range(experts):
                    ex = weights_of(k)
                    sp.dma_start(b1[:, k * fc:(k + 1) * fc], b1_d[bass.ds(ex, 1), :, :].rearrange("e p f -> (e p) f")).then_inc(small, 16)
                    sp.dma_start(b2[k:k + 1, :], b2_d[bass.ds(ex, 1), :]).then_inc(small, 16)
                with sp.Fori(0, experts // twin) as eo:
                    for e in range(twin):
                        ex = eo * twin + e
                        into = weights_of(ex)
                        sp.wait_ge(multiplied, 2 * steps_per * (ex + 1))
                        sp.dma_start(w1[e][:], w1_d[bass.ds(into, 1), :, :].rearrange("e p f -> (e p) f")).then_inc(w_in[e], 16)
                        sp.dma_start(w2[e][:], w2_d[bass.ds(into, 1), :, :].rearrange("e p f -> (e p) f")).then_inc(w_in[e], 16)

            @block.scalar
            def _(act):
                act.sem_inc(activated, 2)
                act.wait_ge(small, 32 * experts)
                if gate is not None:
                    def copy_gate(t, u):
                        act.wait_ge(g_turned, t + 1)
                        nc.scalar.copy(gs[u][:], gate[0:P, bass.ds(t * experts, experts)]).then_inc(g_copied, 1)
                    tiles_loop(act, copy_gate)
                with act.Fori(0, experts // twin) as eo:
                    for e in range(twin):
                        ex = eo * twin + e
                        with act.Fori(0, steps_per) as g:
                            st = ex * steps_per + g
                            for q in range(2):
                                act.wait_ge(multiplied, PRIME + 2 * st + q - 1)
                                for j in range(jh):
                                    act.wait_ge(hidden_ready, 2 * jh * st + q * jh + j + 1)
                                    for m, (m0, mn) in enumerate(PIECES):
                                        ins = nc.scalar.activation(
                                            h[q][:, j * GROUP + m0:j * GROUP + m0 + mn],
                                            ps_h[j % 2][:, 512 * m:512 * m + mn], act_fn,
                                            bias=b1[:, bass.ds(ex * fc + q * jh + j, 1)])
                                    ins.then_inc(activated, 1)

            @block.tensor
            def _(pe):
                pe.sem_inc(multiplied, PRIME)
                pe.wait_ge(small, 32 * experts)
                if gate is not None:
                    pe.sem_inc(g_turned, RING)

                    def bias_part(t, u):
                        pe.wait_ge(g_copied, t + 1)
                        pe.wait_ge(bias_kept, t + 1)
                        nc.tensor.transpose(ps_h[0][0:experts, 0:P], gs[u][:], c["ident"][0:P, 0:P]).then_inc(g_turned, 1)
                        pe.wait_ge(g_kept, t + 1)
                        nc.tensor.matmul(ps_h[1][0:P, 0:D], gt[:, u * P:(u + 1) * P], b2[:], start=True, stop=True).then_inc(biased, 1)
                    tiles_loop(pe, bias_part)
                    pe.wait_ge(bias_kept, T + 1)
                with pe.Fori(0, experts // twin) as eo:
                    for e in range(twin):
                        ex = eo * twin + e
                        pe.wait_ge(w_in[e], 32 * (eo + 1))
                        pe.sem_inc(go, 1)
                        with pe.Fori(0, steps_per) as g:
                            st = ex * steps_per + g
                            for q in range(2):
                                for j in range(jh):
                                    pe.wait_ge(activated, 2 * jh * st + q * jh + j + 1)
                                    f0 = (q * jh + j) * 128
                                    for m, (m0, mn) in enumerate(PIECES):
                                        for k in range(DC):
                                            ins = nc.tensor.matmul(
                                                ps_h[j % 2][:, 512 * m:512 * m + mn],
                                                w1[e][:, k * hidden + f0:k * hidden + f0 + 128],
                                                xt[:, bass.ds(g * GROUP + (k * N + m0), mn)],
                                                start=(k == 0), stop=(k == DC - 1))
                                    ins.then_inc(hidden_ready, 1)
                            for q in range(2):
                                pe.wait_ge(activated, 2 + 2 * jh * st + (q + 1) * jh)
                                if q == 0:
                                    pe.wait_ge(summed, st + 1)
                                for k in range(RING):
                                    for j in range(jh):
                                        ins = nc.tensor.matmul(
                                            ycols(k), h[q][:, j * GROUP + k * P:j * GROUP + (k + 1) * P],
                                            w2[e][:, (q * jh + j) * D:(q * jh + j + 1) * D],
                                            start=(q == 0 and j == 0 and k % 2 == 0), stop=(q == 1 and j == jh - 1),
                                            skip_group_check=True)
                                ins.then_inc(multiplied, 1)

            @block.vector
            def _(dve):
                dve.sem_inc(summed, 1)
                dve.wait_ge(small, 32 * experts)
                if gate is not None:
                    dve.sem_inc(bias_kept, 1)

                    def keep_bias(t, u):
                        dve.wait_ge(g_turned, RING + t + 1)
                        nc.vector.tensor_copy(gt[:, u * P:(u + 1) * P], ps_h[0][0:experts, 0:P]).then_inc(g_kept, 1)
                        dve.wait_ge(biased, t + 1)
                        nc.vector.tensor_copy(acc[:, tile_of(t, D)], ps_h[1][0:P, 0:D]).then_inc(bias_kept, 1)
                    tiles_loop(dve, keep_bias)
                    dve.wait_ge(bias_kept, T + 1)
                with dve.Fori(0, experts) as ex:
                    with dve.Fori(0, steps_per) as g:
                        st = ex * steps_per + g
                        dve.wait_ge(multiplied, PRIME + 2 * st + 2)
                        dve.wait_ge(summed, st + 1)
                        for k in range(RING):
                            to = acc[:, bass.ds(g * (RING * D) + k * D, D)]
                            if gate is None:
                                ins = nc.vector.tensor_copy(to, ycols(k))
                            else:
                                ins = nc.vector.scalar_tensor_tensor(
                                    to, ycols(k), gate[0:P, bass.ds(g * (RING * experts) + k * experts + ex, 1)], to,
                                    ALU.mult, ALU.add)
                        ins.then_inc(summed, 1)



ST = 128


def pair_loop(eng, groups, body):
    body(0, True, False)
    with eng.Fori(1, groups // 2 - 1) as i:
        body(i, False, False)
    body(groups // 2 - 1, False, True)


def dispatch(nc, c, name, picks, experts, tiles, groups, capacity, slot_d, slots, which, pos, kept):
    g = tiles * ST
    q = groups * tiles
    wide = T * experts
    with Stage(nc, name) as s:
        sel, inside, totals, before, rank, tmp = (s.sb(k, [P, wide]) for k in ("sel", "inside", "totals", "before", "rank", "tmp"))
        zeros, past, lost = s.sb("zeros", [P, T]), s.sb("past", [P, T]), s.sb("lost", [P, T])
        ends, ng, start = s.sb("ends", [P, experts]), s.sb("ng", [P, experts]), s.sb("start", [P, experts])
        posf, row_f, lin = s.sb("posf", [P, T]), s.sb("row_f", [P, T]), s.sb("lin", [P, T])
        row_i, slot_i, node_i = s.sb("row_i", [P, T], I32), s.sb("slot_i", [P, T], I32), s.sb("node_i", [P, T], I32)
        to_i = [s.sb(f"to_i{k}", [P, T], I32) for k in range(len(picks))]
        blank = s.sb("blank", [ST, q], I32)
        giter, which_f = s.sb("giter", [1, groups]), s.sb("which_f", [1, groups])
        upto = s.sb("upto", [P, P])
        ps = [s.ps(f"ps{k}", [P, 512]) for k in range(2)]
        steps, made, hot, counted, ready, blanked, sent, back = (s.sem(k) for k in (
            "steps", "made", "hot", "counted", "ready", "blanked", "sent", "back"))

        def view(x):
            return x[:].rearrange("p (t e) -> p t e", e=experts)

        def per_expert(x):
            return x[:].unsqueeze(1).broadcast_to([P, T, experts])

        with s.block() as block:
            @block.sync
            def _(sp):
                sp.wait_ge(made, 6)
                sp.dma_start(slot_d[0:ST * q, :].rearrange("(p c) f -> p (c f)", p=ST), blank[:]).then_inc(blanked, 16)
                sp.wait_ge(sent, 16 * T * len(picks))
                sp.dma_start(slots[:], slot_d[0:ST * q, :].rearrange("(p c) f -> p (c f)", p=ST)).then_inc(back, 16)
                sp.wait_ge(back, 16)

            @block.gpsimd
            def _(pool):
                nc.gpsimd.memset(upto[:], 1.0).then_inc(made, 1)
                nc.gpsimd.memset(blank[:], 0).then_inc(made, 1)
                nc.gpsimd.iota(node_i[:], pattern=[[P, T]], base=0, channel_multiplier=1).then_inc(made, 1)
                nc.gpsimd.iota(past[:], pattern=[[P, T]], base=ST * q, channel_multiplier=1,
                               allow_small_or_imprecise_dtypes=True).then_inc(made, 1)
                nc.gpsimd.iota(giter[:], pattern=[[1, groups]], base=0, channel_multiplier=0,
                               allow_small_or_imprecise_dtypes=True).then_inc(made, 1)
                pool.wait_ge(made, 5)
                nc.gpsimd.affine_select(out=upto[:], in_=upto[:], compare_op=ALU.is_ge, fill=0.0, base=0,
                                        pattern=[[1, P]], channel_multiplier=-1).then_inc(made, 1)
                pool.wait_ge(blanked, 16)
                pool.wait_ge(ready, 1)
                for k in range(len(picks)):
                    for t in range(T):
                        pool.indirect_dma_start(slot_d, bass.IndirectOffsetOnAxis(ap=to_i[k][:, t:t + 1], axis=0),
                                                node_i[:, t:t + 1], None).then_inc(sent, 16)

            @block.tensor
            def _(pe):
                pe.wait_ge(made, 6)
                pe.wait_ge(hot, 1)
                nc.tensor.matmul(ps[0][:, 0:wide], upto[:], sel[:], start=True, stop=True).then_inc(counted, 1)
                nc.tensor.matmul(ps[1][:, 0:wide], c["ones"][0:P, 0:P], sel[:], start=True, stop=True).then_inc(counted, 1)

            @block.vector
            def _(dve):
                step = Steps(dve, steps)
                V = nc.vector
                step(V.memset(zeros[:], 0.0))
                step(V.tensor_copy(sel[:], picks[0][:]))
                for k in picks[1:]:
                    step(V.tensor_tensor(sel[:], sel[:], k[:], ALU.add))
                dve.sem_inc(hot, 1)
                dve.wait_ge(counted, 2)
                step(V.tensor_copy(inside[:], ps[0][:, 0:wide]))
                step(V.tensor_copy(totals[:], ps[1][:, 0:wide]))
                for e in range(experts):
                    step(V.tensor_tensor_scan(view(before)[:, :, e], zeros[:], view(totals)[:, :, e], 0.0, ALU.add, ALU.add))
                step(V.tensor_tensor(rank[:], before[:], totals[:], ALU.subtract))
                step(V.tensor_tensor(rank[:], rank[:], inside[:], ALU.add))
                step(V.tensor_scalar(rank[:], rank[:], -1.0, None, ALU.add))
                if capacity is None:
                    step(V.tensor_copy(ends[:], view(before)[:, T - 1, :]))
                    step(V.memset(ng[:], 0.0))
                    for k in range(-(-N // g)):
                        step(V.scalar_tensor_tensor(ng[:], ends[:], float(k * g), ng[:], ALU.is_gt, ALU.add))
                    step(V.tensor_tensor_scan(ends[:], zeros[:, 0:experts], ng[:], 0.0, ALU.add, ALU.add))
                    step(V.tensor_tensor(start[:], ends[:], ng[:], ALU.subtract))
                    step(V.memset(which_f[:], -1.0))
                    for e in range(experts):
                        step(V.scalar_tensor_tensor(which_f[:], giter[:], start[0:1, e:e + 1], which_f[:], ALU.is_ge, ALU.add))
                    step(V.tensor_copy(which[:], which_f[:]))
                else:
                    for e in range(experts):
                        step(V.memset(start[:, e:e + 1], float(e)))
                step(V.tensor_scalar(start[:], start[:], float(g), None, ALU.mult))
                step(V.tensor_tensor(view(sel), view(rank), per_expert(start), ALU.add))
                dve.wait_ge(made, 6)
                for k, pick in enumerate(picks):
                    step(V.tensor_tensor(tmp[:], sel[:], pick[:], ALU.mult))
                    step(V.tensor_reduce(posf[:], view(tmp), AX.X, ALU.add))
                    if capacity is not None:
                        step(V.scalar_tensor_tensor(tmp[:], rank[:], float(capacity), pick[:], ALU.is_lt, ALU.mult))
                        step(V.tensor_reduce(kept[:], view(tmp), AX.X, ALU.add))
                        step(V.tensor_tensor(posf[:], posf[:], kept[:], ALU.mult))
                    step(V.tensor_copy(pos[k][:], posf[:]))
                    step(V.tensor_scalar(row_i[:], pos[k][:], ST - 1, None, ALU.bitwise_and))
                    step(V.tensor_scalar(slot_i[:], pos[k][:], 7, None, ALU.arith_shift_right))
                    step(V.tensor_copy(row_f[:], row_i[:]))
                    step(V.tensor_copy(posf[:], slot_i[:]))
                    step(V.scalar_tensor_tensor(lin[:], row_f[:], float(q), posf[:], ALU.mult, ALU.add))
                    if capacity is not None:
                        step(V.scalar_tensor_tensor(lost[:], kept[:], 0.0, past[:], ALU.is_equal, ALU.mult))
                        step(V.tensor_tensor(lin[:], lin[:], kept[:], ALU.mult))
                        step(V.tensor_tensor(lin[:], lin[:], lost[:], ALU.add))
                    step(V.tensor_copy(to_i[k][:], lin[:]))
                dve.sem_inc(ready, 1)


def routed(nc, c, name, y_d, slots, which, hidden, act_fn, w1_d, b1_d, w2_d, b2_d, tiles, groups, out_d):
    fc = hidden // 128
    jh = fc // 2
    g = tiles * ST
    with Stage(nc, name) as s:
        w1 = [s.sb(f"w1_{e}", [128, DC * hidden]) for e in range(2)]
        w2 = [s.sb(f"w2_{e}", [128, fc * D]) for e in range(2)]
        b1 = [s.sb(f"b1_{e}", [128, fc]) for e in range(2)]
        b2 = [s.sb(f"b2_{e}", [ST, D]) for e in range(2)]
        idx = [s.sb(f"idx{e}", [ST, tiles], I32) for e in range(2)]
        rows = [s.sb(f"rows{k}", [ST, D]) for k in range(2 * tiles)]
        xt = [s.sb(f"xt{e}", [128, DC * g]) for e in range(2)]
        h = [s.sb(f"h{q}", [128, jh * g]) for q in range(2)]
        y = [s.sb(f"y{e}", [ST, tiles * D]) for e in range(2)]
        ps_t = [s.ps(f"ps_t{k}", [128, 512]) for k in range(2)]
        ps_h = [s.ps(f"ps_h{k}", [128, 512]) for k in range(2)]
        ps_y = s.ps("ps_y", [ST, tiles // 2 * 512])
        w_in = [s.sem(f"w_in{e}") for e in range(2)]
        landed = [s.sem(f"landed{k}") for k in range(2 * tiles)]
        out_done = [s.sem(f"out_done{e}") for e in range(2)]
        idx_ready, hidden_ready, go = s.sem("idx_ready"), s.sem("hidden_ready"), s.sem("go")
        turned = s.sem("turned")
        kept = s.sem("kept")
        activated = s.sem("activated")
        multiplied = s.sem("multiplied")
        summed = s.sem("summed")

        with s.block() as block:
            @block.sync
            def _(sp):
                def store(i, e):
                    n = 2 * i + e
                    sp.wait_ge(summed, n + 3)
                    sp.sem_inc(go, 1)
                    sp.dma_start(out_d[bass.ds(n * g, g), :].rearrange("(k p) f -> p k f", p=ST),
                                 y[e][:].rearrange("p (k f) -> p k f", f=D)).then_inc(out_done[e], 16)

                def body(i, first, last):
                    for e in range(2):
                        n = 2 * i + e
                        sp.wait_ge(multiplied, 2 * n + 2)
                        sp.sem_inc(go, 1)
                        sp.wait_ge(summed, n + 1)
                        sp.sem_inc(go, 1)
                        if which is None:
                            ex = n
                        else:
                            ex = sp.value_load(which[0:1, bass.ds(n, 1)], min_val=0, max_val=w1_d.shape[0] - 1)
                        for dst, src in ((w1[e], w1_d), (w2[e], w2_d), (b1[e], b1_d)):
                            sp.dma_start(dst[:], src[bass.ds(ex, 1), :, :].rearrange("e p f -> (e p) f")).then_inc(w_in[e], 16)
                        sp.dma_start(b2[e][:], b2_d[bass.ds(ex, 1), :].rearrange("e f -> (e f)").partition_broadcast(ST)).then_inc(w_in[e], 16)
                        if not first:
                            store(i - 1, e)
                pair_loop(sp, groups, body)
                for e in range(2):
                    store(groups // 2 - 1, e)
                for e in range(2):
                    sp.wait_ge(out_done[e], 16 * (groups // 2))

            @block.gpsimd
            def _(pool):
                def body(i, first, last):
                    for e in range(2):
                        n = 2 * i + e
                        pool.wait_ge(turned, tiles * (n + 1))
                        nc.gpsimd.tensor_copy(idx[e][:], slots[:, bass.ds(n * tiles, tiles)]).then_inc(idx_ready, 1)
                        pool.wait_ge(idx_ready, n + 1)
                        pool.sem_inc(go, 1)
                        for k in range(tiles):
                            pool.indirect_dma_start(rows[e * tiles + k][:], None, y_d,
                                                    bass.IndirectOffsetOnAxis(ap=idx[e][:, k:k + 1], axis=0)
                                                    ).then_inc(landed[e * tiles + k], 16)
                pair_loop(pool, groups, body)

            @block.scalar
            def _(act):
                act.sem_inc(activated, 2)

                def body(i, first, last):
                    for e in range(2):
                        n = 2 * i + e
                        act.wait_ge(w_in[e], 64 * (i + 1))
                        for q in range(2):
                            act.wait_ge(multiplied, 2 * n + q + 3)
                            for j in range(jh):
                                act.wait_ge(hidden_ready, fc * n + q * jh + j + 1)
                                nc.scalar.activation(h[q][:, j * g:(j + 1) * g], ps_h[j % 2][:, 0:g], act_fn,
                                                     bias=b1[e][:, q * jh + j:q * jh + j + 1]).then_inc(activated, 1)
                pair_loop(act, groups, body)

            @block.tensor
            def _(pe):
                pe.sem_inc(turned, 2 * tiles)
                pe.sem_inc(multiplied, 4)

                def turn(i, e):
                    n = 2 * i + e
                    for k in range(tiles):
                        pe.wait_ge(landed[e * tiles + k], 16 * (i + 1))
                        pe.wait_ge(kept, tiles * n + k + 1)
                        for d in range(DC):
                            ins = nc.tensor.transpose(ps_t[k % 2][:, d * ST:(d + 1) * ST], rows[e * tiles + k][:, d * 128:(d + 1) * 128],
                                                      c["ident"][:])
                        ins.then_inc(turned, 1)

                def body(i, first, last):
                    for e in range(2):
                        n = 2 * i + e
                        pe.wait_ge(kept, 2 + tiles * (n + 1))
                        pe.wait_ge(w_in[e], 64 * (i + 1))
                        for q in range(2):
                            for j in range(jh):
                                pe.wait_ge(activated, fc * n + q * jh + j + 1)
                                f0 = (q * jh + j) * 128
                                for d in range(DC):
                                    ins = nc.tensor.matmul(ps_h[j % 2][:, 0:g], w1[e][:, d * hidden + f0:d * hidden + f0 + 128],
                                                           xt[e][:, d * g:(d + 1) * g], start=(d == 0), stop=(d == DC - 1))
                                ins.then_inc(hidden_ready, 1)
                        if not (last and e == 1):
                            turn(i + e, 1 - e)
                        for q in range(2):
                            pe.wait_ge(activated, 2 + fc * n + (q + 1) * jh)
                            if q == 0:
                                pe.wait_ge(summed, n + 2)
                            for k in range(tiles):
                                for j in range(jh):
                                    ins = nc.tensor.matmul(
                                        ps_y[:, k * D:(k + 1) * D], h[q][:, j * g + k * ST:j * g + (k + 1) * ST],
                                        w2[e][:, (q * jh + j) * D:(q * jh + j + 1) * D],
                                        start=(q == 0 and j == 0 and k % 2 == 0), stop=(q == 1 and j == jh - 1),
                                        skip_group_check=True)
                            ins.then_inc(multiplied, 1)
                turn(0, 0)
                pair_loop(pe, groups, body)

            @block.vector
            def _(dve):
                dve.sem_inc(kept, 2)
                dve.sem_inc(summed, 2)

                def keep(i, e):
                    n = 2 * i + e
                    for k in range(tiles):
                        dve.wait_ge(turned, 2 * tiles + tiles * n + k + 1)
                        nc.vector.tensor_copy(xt[e][:].rearrange("p (d m) -> p d m", d=DC)[:, :, k * ST:(k + 1) * ST],
                                              ps_t[k % 2][:, 0:DC * ST].rearrange("p (d m) -> p d m", d=DC)).then_inc(kept, 1)

                def body(i, first, last):
                    for e in range(2):
                        n = 2 * i + e
                        if not (last and e == 1):
                            keep(i + e, 1 - e)
                        dve.wait_ge(multiplied, 6 + 2 * n)
                        dve.wait_ge(w_in[e], 64 * (i + 1))
                        if not first:
                            dve.wait_ge(out_done[e], 16 * i)
                        nc.vector.tensor_tensor(y[e][:].rearrange("p (k f) -> p k f", f=D),
                                                ps_y[:].rearrange("p (k f) -> p k f", f=D),
                                                b2[e][:].unsqueeze(1).broadcast_to([ST, tiles, D]), ALU.add).then_inc(summed, 1)
                keep(0, 0)
                pair_loop(dve, groups, body)


def combine(nc, name, out_d, pos, weights, acc):
    ring = 8
    items = [(t, k) for t in range(T) for k in range(len(pos))]
    with Stage(nc, name) as s:
        rows = [s.sb(f"rows{u}", [P, D]) for u in range(ring)]
        landed = [s.sem(f"landed{u}") for u in range(ring)]
        used = s.sem("used")
        with s.block() as block:
            @block.gpsimd
            def _(pool):
                for n, (t, k) in enumerate(items):
                    if n >= ring:
                        pool.wait_ge(used, n - ring + 1)
                    pool.indirect_dma_start(rows[n % ring][:], None, out_d,
                                            bass.IndirectOffsetOnAxis(ap=pos[k][:, t:t + 1], axis=0)).then_inc(landed[n % ring], 16)

            @block.vector
            def _(dve):
                for n, (t, k) in enumerate(items):
                    dve.wait_ge(landed[n % ring], 16 * (n // ring + 1))
                    to = acc[:, t * D:(t + 1) * D]
                    if len(pos) == 1:
                        nc.vector.tensor_scalar(to, rows[n % ring][:], weights[k][:, t:t + 1], None, ALU.mult).then_inc(used, 1)
                    else:
                        if k > 0:
                            dve.wait_ge(used, n)
                        nc.vector.scalar_tensor_tensor(to, rows[n % ring][:], weights[k][:, t:t + 1], to,
                                                       ALU.mult, ALU.add).then_inc(used, 1)



def first_of(nc, step, eq, out, seen, experts):
    step(nc.vector.memset(seen[:], 0.0))
    for e in range(experts):
        step(nc.vector.tensor_tensor(out[:, :, e], eq[:, :, e], seen[:], ALU.is_gt))
        step(nc.vector.tensor_tensor(seen[:], seen[:], eq[:, :, e], ALU.max))


def top_two(nc, c, name, scores, n, experts, one, two, w1, w2):
    with Stage(nc, name) as s:
        eq = s.sb("eq", [P, n * experts])
        rest = s.sb("rest", [P, n * experts])
        seen, m1, m2, gap, ex, den = (s.sb(k, [P, n]) for k in ("seen", "m1", "m2", "gap", "ex", "den"))
        steps, exps = s.sem("steps"), s.sem("exps")
        gap_ready = s.sem("gap_ready")

        def view(x):
            return x[:, 0:n * experts].rearrange("p (t e) -> p t e", e=experts)

        def wide(x):
            return x[:].unsqueeze(2).broadcast_to([P, n, experts])

        with s.block() as block:
            @block.scalar
            def _(act):
                act.wait_ge(gap_ready, 1)
                nc.scalar.activation(ex[:], gap[:], ACT.Exp).then_inc(exps, 1)

            @block.vector
            def _(dve):
                step = Steps(dve, steps)
                V = nc.vector
                sc = view(scores)
                step(V.tensor_reduce(m1[:], sc, AX.X, ALU.max))
                step(V.tensor_tensor(view(eq), sc, wide(m1), ALU.is_equal))
                first_of(nc, step, view(eq), view(one), seen, experts)
                step(V.scalar_tensor_tensor(rest[:], one[:], -3e38, scores[:, 0:n * experts], ALU.mult, ALU.add))
                step(V.tensor_reduce(m2[:], view(rest), AX.X, ALU.max))
                step(V.tensor_tensor(view(eq), view(rest), wide(m2), ALU.is_equal))
                first_of(nc, step, view(eq), view(two), seen, experts)
                V.tensor_tensor(gap[:], m2[:], m1[:], ALU.subtract).then_inc(gap_ready, 1)
                dve.wait_ge(exps, 1)
                step(V.tensor_scalar(den[:], ex[:], 1.0, None, ALU.add))
                step(V.reciprocal(w1[:], den[:]))
                step(V.tensor_tensor(w2[:], ex[:], w1[:], ALU.mult))


def top_one(nc, c, name, logits, experts, one, pm):
    with Stage(nc, name) as s:
        shift, ex, probs, eq = (s.sb(k, [P, T * experts]) for k in ("shift", "ex", "probs", "eq"))
        mx, tot, inv, seen = (s.sb(k, [P, T]) for k in ("mx", "tot", "inv", "seen"))
        steps, exps, shifted = (s.sem(k) for k in ("steps", "exps", "shifted"))

        def view(x):
            return x[:].rearrange("p (t e) -> p t e", e=experts)

        def wide(x):
            return x[:].unsqueeze(2).broadcast_to([P, T, experts])

        with s.block() as block:
            @block.scalar
            def _(act):
                act.wait_ge(shifted, 1)
                nc.scalar.activation(ex[:], shift[:], ACT.Exp).then_inc(exps, 1)

            @block.vector
            def _(dve):
                step = Steps(dve, steps)
                V = nc.vector
                step(V.tensor_reduce(mx[:], view(logits), AX.X, ALU.max))
                V.tensor_tensor(view(shift), view(logits), wide(mx), ALU.subtract).then_inc(shifted, 1)
                dve.wait_ge(exps, 1)
                step(V.tensor_reduce(tot[:], view(ex), AX.X, ALU.add))
                step(V.reciprocal(inv[:], tot[:]))
                step(V.tensor_tensor(view(probs), view(ex), wide(inv), ALU.mult))
                step(V.tensor_reduce(pm[:], view(probs), AX.X, ALU.max))
                step(V.tensor_tensor(view(eq), view(probs), wide(pm), ALU.is_equal))
                first_of(nc, step, view(eq), view(one), seen, experts)


def finite(nc, name, y):
    top = 3.4028234663852886e38
    w = RING * D
    with Stage(nc, name) as s:
        mask, low, nan = (s.sb(k, [P, w], I32) for k in ("mask", "low", "nan"))
        fill = s.sb("fill", [P, 3])
        steps = s.sem("steps")

        def filled(k):
            return fill[:, k:k + 1].broadcast_to([P, w])

        with s.block() as block:
            @block.vector
            def _(dve):
                step = Steps(dve, steps)
                V = nc.vector
                for k, v in enumerate((1e4, -1e4, 0.0)):
                    step(V.memset(fill[:, k:k + 1], v))
                for g in range(T // RING):
                    yt = y[:, g * w:(g + 1) * w]
                    step(V.tensor_scalar(mask[:], yt, top, None, ALU.is_gt))
                    step(V.tensor_scalar(low[:], yt, -top, None, ALU.is_lt))
                    step(V.tensor_tensor(nan[:], yt, yt, ALU.not_equal))
                    step(V.copy_predicated(yt, mask[:], filled(0)))
                    step(V.copy_predicated(yt, low[:], filled(1)))
                    step(V.copy_predicated(yt, nan[:], filled(2)))


def global_scores(nc, c, name, yt_feat, wr_d, br_d, experts, capacity, scores):
    with Stage(nc, name) as s:
        wr = s.sb("wr", [128, DC * experts])
        br = s.sb("br", [P, experts])
        tot = s.sb("tot", [128, DC])
        mean = s.sb("mean", [128, DC * P])
        lg, ex, rw, load, scale, low, a2, ex2 = (s.sb(k, [P, experts]) for k in ("lg", "ex", "rw", "load", "scale", "low", "a2", "ex2"))
        mx, sm, inv = (s.sb(k, [P, 1]) for k in ("mx", "sm", "inv"))
        ps = s.ps("ps", [P, 512])
        loaded, steps, averaged, routed, asked, exps = (s.sem(k) for k in ("loaded", "steps", "averaged", "routed", "asked", "exps"))
        with s.block() as block:
            @block.sync
            def _(sp):
                sp.dma_start(wr[:], wr_d).then_inc(loaded, 16)
                sp.dma_start(br[:], br_d.partition_broadcast(P)).then_inc(loaded, 16)

            @block.scalar
            def _(act):
                act.wait_ge(asked, 1)
                nc.scalar.activation(ex[:], lg[:], ACT.Exp).then_inc(exps, 1)
                act.wait_ge(asked, 2)
                nc.scalar.activation(ex2[:], a2[:], ACT.Exp).then_inc(exps, 1)

            @block.tensor
            def _(pe):
                pe.wait_ge(loaded, 32)
                pe.wait_ge(averaged, 1)
                for k in range(DC):
                    ins = nc.tensor.matmul(ps[:, 0:experts], mean[:, k * P:(k + 1) * P], wr[:, k * experts:(k + 1) * experts],
                                           start=(k == 0), stop=(k == DC - 1))
                ins.then_inc(routed, 1)

            @block.vector
            def _(dve):
                step = Steps(dve, steps)
                V = nc.vector
                step(V.tensor_reduce(tot[:], yt_feat[:].rearrange("p (k n) -> p k n", k=DC), AX.X, ALU.add))
                V.tensor_scalar(mean[:].rearrange("p (k m) -> p k m", k=DC),
                                tot[:].unsqueeze(2).broadcast_to([128, DC, P]), 1.0 / N, None, ALU.mult).then_inc(averaged, 1)
                dve.wait_ge(loaded, 32)
                dve.wait_ge(routed, 1)
                step(V.tensor_tensor(lg[:], ps[:, 0:experts], br[:], ALU.add))
                step(V.tensor_reduce(mx[:], lg[:], AX.X, ALU.max))
                step(V.tensor_scalar(lg[:], lg[:], mx[:, 0:1], None, ALU.subtract))
                dve.sem_inc(asked, 1)
                dve.wait_ge(exps, 1)
                step(V.tensor_reduce(sm[:], ex[:], AX.X, ALU.add))
                step(V.reciprocal(inv[:], sm[:]))
                step(V.tensor_scalar(rw[:], ex[:], inv[:, 0:1], None, ALU.mult))
                step(V.tensor_scalar(load[:], rw[:], float(N), float(capacity), ALU.mult, ALU.max))
                step(V.reciprocal(scale[:], load[:]))
                step(V.tensor_scalar(scale[:], scale[:], float(capacity), None, ALU.mult))
                step(V.tensor_scalar(low[:], load[:], float(capacity), None, ALU.is_le))
                step(V.tensor_tensor(scale[:], scale[:], low[:], ALU.max))
                step(V.tensor_tensor(a2[:], rw[:], scale[:], ALU.mult))
                step(V.tensor_reduce(mx[:], a2[:], AX.X, ALU.max))
                step(V.tensor_scalar(a2[:], a2[:], mx[:, 0:1], None, ALU.subtract))
                dve.sem_inc(asked, 1)
                dve.wait_ge(exps, 2)
                step(V.tensor_reduce(sm[:], ex2[:], AX.X, ALU.add))
                step(V.reciprocal(inv[:], sm[:]))
                step(V.tensor_scalar(scores[:], ex2[:], inv[:, 0:1], None, ALU.mult))



def vector_steps(nc, name, fn):
    with Stage(nc, name) as s:
        steps = s.sem("steps")
        with s.block() as block:
            @block.vector
            def _(dve):
                fn(Steps(dve, steps), nc.vector)


def root(nc, name, x, out):
    with Stage(nc, name) as s:
        r = s.sb("r", list(x.shape))
        rooted, inverted = s.sem("rooted"), s.sem("inverted")
        with s.block() as block:
            @block.scalar
            def _(act):
                nc.scalar.activation(r[:], x[:], ACT.Sqrt).then_inc(rooted, 1)

            @block.vector
            def _(dve):
                dve.wait_ge(rooted, 1)
                nc.vector.reciprocal(out[:], r[:]).then_inc(inverted, 1)


def batch_norm_relu(nc, name, xt, ch, bias_d, gamma_d, beta_d):
    with Stage(nc, name) as s:
        col = s.sb("col", [ch, 3])
        stats = s.sb("stats", [ch, T * 6])
        mv = s.sb("mv", [ch, 2])
        var, std, rstd = (s.sb(k, [ch, 1]) for k in ("var", "std", "rstd"))
        loaded, steps, ready, rooted, normed, done = (s.sem(k) for k in ("loaded", "steps", "ready", "rooted", "normed", "done"))
        with s.block() as block:
            @block.sync
            def _(sp):
                for k, v in enumerate((bias_d, gamma_d, beta_d)):
                    sp.dma_start(col[:, k:k + 1], v).then_inc(loaded, 16)

            @block.scalar
            def _(act):
                act.wait_ge(ready, 1)
                nc.scalar.activation(std[:], var[:], ACT.Sqrt).then_inc(rooted, 1)
                act.wait_ge(normed, 1)
                nc.scalar.activation(xt[:], xt[:], ACT.Relu, bias=col[:, 2:3], scale=col[:, 1:2]).then_inc(done, 1)

            @block.vector
            def _(dve):
                step = Steps(dve, steps)
                dve.wait_ge(loaded, 48)
                step(nc.vector.tensor_scalar(xt[:], xt[:], col[:, 0:1], None, ALU.add))
                tiles_loop(dve, lambda t, u: nc.vector.bn_stats(stats[:, tile_of(t, 6)], xt[:, tile_of(t, P)]).then_inc(steps, 1))
                step.n += T
                dve.wait_ge(steps, step.n)
                step(nc.vector.bn_aggr(mv[:], stats[:]))
                nc.vector.tensor_scalar(var[:], mv[:, 1:2], EPS, None, ALU.add).then_inc(ready, 1)
                dve.wait_ge(rooted, 1)
                step(nc.vector.reciprocal(rstd[:], std[:]))
                nc.vector.tensor_scalar(xt[:], xt[:], mv[:, 0:1], rstd[:, 0:1], ALU.subtract, ALU.mult).then_inc(normed, 1)
                dve.wait_ge(normed, 1)



def model(nc, I, out, probes=None):
    E0 = 53125
    E3 = 32768
    CH0, CH3 = chunk_bound(E0), chunk_bound(E3)
    heads, hd = 8, 32
    gh, ge = 4, 4
    capacity = -(-N * 5 // (4 * 8))

    def dram(name, shape):
        return nc.dram_tensor(name, shape, F32, kind="Internal").ap()

    def slot_table(name, tiles):
        return nc.dram_tensor(name, [ST * tiles + N, 1], I32, kind="Internal").ap()

    with Stage(nc, "model") as m:
        x = m.sb("x", [P, T * D])
        c = {"ident": m.sb("ident", [128, 128]), "iota": m.sb("iota", [128, 128]), "ones": m.sb("ones", [128, 128])}
        count = m.sb("count", [P, T])
        inv2 = m.sb("inv2", [P, T])
        inv3 = m.sb("inv3", [P, T])

        def chunks_of(w):
            wide = w.shape[1] // DC
            return [w[:, k * wide:(k + 1) * wide] for k in range(DC)]

        def from_features(t, w):
            return [(t, 128, k, wk) for k, wk in enumerate(chunks_of(w))]

        def probe(k):
            if probes is not None and k in probes:
                transfer(nc, "probe", [(by_tile(probes[k], D), as_tiles(x, D))])

        y_d = dram("y", [N, D])
        constants(nc, c, I)

        by_dst3 = Table(nc, m, "by_dst3", 128, 256, (4, 4, 16), CH3)
        with Stage(nc, "graph") as g:
            by_dst = Table(nc, g, "by_dst", 125, 425, (5, 5, 17), CH0)
            by_src = Table(nc, g, "by_src", 125, 425, (5, 5, 17), CH0)
            bucket(nc, c, "by_dst", I["dst"], I["src"], None, by_dst, moves=[(as_tiles(x, D), by_tile(I["x"], D))])
            bucket(nc, c, "by_src", I["src"], I["dst"], I["edge_weight"], by_src, [(by_dst, 0, 3)])
            bucket(nc, c, "by_dst3", I["edge3_dst"], I["edge3_src"], None, by_dst3, [(by_dst, 3, 2)])
            collect(nc, "collect", [by_dst])
            rec_d, blk_d, rec_s, blk_s = by_dst.rec, by_dst.blk, by_src.rec, by_src.blk

            with Stage(nc, "l0g") as s:
                yf = s.sb("yf", [128, DC * N])
                mf = s.sb("mf", [128, DC * N])
                with Stage(nc, "l0y") as s2:
                    y = s2.sb("y", [P, T * D])
                    layernorm(nc, "ln0", x, y)
                    turn_tiles(nc, c, "turn0", y, D, yf, table=y_d)
                with Stage(nc, "l0a") as s2:
                    acc = s2.sb("acc", [P, T * (D + 1)])
                    inv = s2.sb("inv", [P, T])
                    segment_sum(nc, c, "sum0", y_d, D, rec_d, blk_d, CH0, acc, True)
                    a3 = as_tiles(acc, D + 1)

                    def mean(step, V):
                        step(V.tensor_copy(count[:], a3[:, :, D]))
                        step(V.tensor_scalar(inv[:], count[:], 1.0, None, ALU.max))
                        step(V.reciprocal(inv[:], inv[:]))
                        step(V.tensor_tensor(a3[:, :, 0:D], a3[:, :, 0:D], inv[:].unsqueeze(2).broadcast_to([P, T, D]), ALU.mult))
                        step(V.tensor_scalar(inv3[:], count[:], 1.0, 1.0, ALU.add, ALU.max))
                    vector_steps(nc, "mean0", mean)
                    root(nc, "root3", inv3, inv3)
                    turn_tiles(nc, c, "turn0b", acc, D, mf, stride=D + 1)
                project(nc, c, "out0", from_features(mf, I["L0_gnn_W_neigh"]) + from_features(yf, I["L0_gnn_W_self"]),
                        D, "add", x, bias=I["L0_gnn_b_self"])
            probe(1)

            with Stage(nc, "l0f") as s:
                one, pm, kept = s.sb("one", [P, T * 8]), s.sb("pm", [P, T]), s.sb("kept", [P, T])
                slots, pos = s.sb("slots", [ST, 8 * 4], I32), s.sb("pos", [P, T], I32)
                router(nc, c, "l0r", x, y_d, I["L0_ffn_gate_w"], I["L0_ffn_gate_b"], 8,
                       lambda lg: top_one(nc, c, "gate0", lg, 8, one, pm))
                assert capacity <= 4 * ST
                dispatch(nc, c, "disp0", [one], 8, 4, 8, capacity, slot_table("slots0", 8 * 4), slots, None, [pos], kept)
                out_d = dram("out0", [8 * 4 * ST, D])
                routed(nc, c, "net0", y_d, slots, None, 1024, ACT.Relu, I["L0_ffn_w1"], I["L0_ffn_b1"], I["L0_ffn_w2"],
                       I["L0_ffn_b2"], 4, 8, out_d)
                acc = s.sb("acc", [P, T * D])
                vector_steps(nc, "keep0", lambda step, V: step(V.tensor_tensor(pm[:], pm[:], kept[:], ALU.mult)))
                combine(nc, "comb0", out_d, [pos], [pm], acc)
                finite(nc, "finite0", acc)
                vector_steps(nc, "res0", lambda step, V: step(V.tensor_tensor(x[:], x[:], acc[:], ALU.add)))
            probe(2)

            k_d, v_d = dram("k", [N, D]), dram("v", [N, D])
            with Stage(nc, "l1g") as s:
                y = s.sb("y", [P, T * D])
                attended = s.sb("attended", [P, T * (D + heads)])
                layernorm(nc, "ln1", x, y)
                with Stage(nc, "l1e") as s1:
                    scores = s1.sb("scores", [EC, CH0 * heads])
                    best = s1.sb("best", [P, T * heads])
                    with Stage(nc, "l1q") as s2:
                        q = s2.sb("q", [P, T * D])
                        with Stage(nc, "l1kv") as s3:
                            yf = s3.sb("yf", [128, DC * N])
                            turn_tiles(nc, c, "turn1", y, D, yf)
                            for wname, table in (("L1_gnn_Wk", k_d), ("L1_gnn_Wv", v_d)):
                                project(nc, c, "kv", from_features(yf, I[wname]), D, "copy", q, table=table)
                            project(nc, c, "q", from_features(yf, I["L1_gnn_Wq"]), D, "copy", q)
                        edge_scores(nc, c, "scores", k_d, q, rec_d, blk_d, CH0, heads, hd ** -0.5, scores)
                    vector_steps(nc, "max0", lambda step, V: step(V.memset(best[:], 0.0)))
                    segment_max(nc, c, "max1", scores, heads, heads, rec_d, blk_d, CH0, best, None, None,
                                [(by_src, 0, 5), (by_dst3, 0, 2)])
                    collect(nc, "collect", [by_src])
                    softmax_sum(nc, c, "att1", heads, hd, rec_d, blk_d, CH0, attended, best, heads, v_d, scores, None, False)
                af = s.sb("af", [128, DC * N])
                inv = s.sb("inv", [P, T * heads])

                def normalise(step, V):
                    a = as_tiles(attended, D + heads)
                    i3 = inv[:].rearrange("p (t h) -> p t h", h=heads)
                    step(V.tensor_scalar(i3, a[:, :, D:D + heads], 1e-8, None, ALU.add))
                    step(V.reciprocal(inv[:], inv[:]))
                    for h in range(heads):
                        v = a[:, :, h * hd:(h + 1) * hd]
                        step(V.tensor_tensor(v, v, i3[:, :, h:h + 1].broadcast_to([P, T, hd]), ALU.mult))
                vector_steps(nc, "norm1", normalise)
                turn_tiles(nc, c, "turn1a", attended, D, af, stride=D + heads)
                project(nc, c, "out1", from_features(af, I["L1_gnn_Wo_w"]), D, "add", y, bias=I["L1_gnn_Wo_b"])
                layernorm(nc, "ln1a", y, y, I["L1_gnn_ln1_g"], I["L1_gnn_ln1_b"])
                turn_tiles(nc, c, "turn1h", y, D, af)
                acc = attended[:, 0:T * D]
                network(nc, c, "net1", af, 1, 512, ACT.Gelu, I["L1_gnn_ffn_w1"], I["L1_gnn_ffn_b1"], I["L1_gnn_ffn_w2"],
                        I["L1_gnn_ffn_b2"], c["ones"], acc, side=[(by_dst3, 2, 2)])
                collect(nc, "collect", [by_dst3])
                vector_steps(nc, "res1", lambda step, V: step(V.tensor_tensor(y[:], y[:], acc, ALU.add)))
                layernorm(nc, "ln1b", y, y, I["L1_gnn_ln2_g"], I["L1_gnn_ln2_b"])
                vector_steps(nc, "res1b", lambda step, V: step(V.tensor_tensor(x[:], x[:], y[:], ALU.add)))
            probe(3)

            with Stage(nc, "l1f") as s:
                one, two = s.sb("one", [P, T * 8]), s.sb("two", [P, T * 8])
                pw1, pw2 = s.sb("pw1", [P, T]), s.sb("pw2", [P, T])
                router(nc, c, "l1r", x, y_d, I["L1_ffn_Wg"], I["L1_ffn_bg"], 8,
                       lambda lg: top_two(nc, c, "gate1", lg, T, 8, one, two, pw1, pw2))
                two_of(nc, c, "l1n", s, dram, slot_table, y_d, one, two, pw1, pw2, 8, 1024, ACT.Relu,
                       I["L1_ffn_W1"], I["L1_ffn_b1"], I["L1_ffn_W2"], I["L1_ffn_b2"], x)
            probe(4)

            z_d = dram("z", [N, D])
            with Stage(nc, "l2g") as s:
                yf = s.sb("yf", [128, DC * N])
                acc = s.sb("acc", [P, T * D])
                with Stage(nc, "l2d") as s2:
                    deg = s2.sb("deg", [P, T])
                    guard = s2.sb("guard", [P, T])
                    degree(nc, c, "deg2", rec_s, CH0, deg)

                    def guarded(step, V):
                        step(V.tensor_scalar(deg[:], deg[:], 1.0, None, ALU.add))
                        step(V.tensor_scalar(guard[:], deg[:], 0.0, None, ALU.is_gt))
                        step(V.tensor_scalar(deg[:], deg[:], 1e-38, None, ALU.max))
                    vector_steps(nc, "guard2", guarded)
                    root(nc, "root2", deg, inv2)
                    vector_steps(nc, "guard2b", lambda step, V: step(V.tensor_tensor(inv2[:], inv2[:], guard[:], ALU.mult)))
                with Stage(nc, "l2y") as s2:
                    y = s2.sb("y", [P, T * D])
                    layernorm(nc, "ln2", x, y)
                    turn_tiles(nc, c, "turn2", y, D, yf)
                with Stage(nc, "l2z") as s2:
                    z = s2.sb("z", [P, T * D])
                    project(nc, c, "z2", from_features(yf, I["L2_gnn_W"]), D, "scale", z, scale=inv2, table=z_d)
                    segment_sum(nc, c, "sum2", z_d, D, rec_s, blk_s, CH0, acc, False)

                    def finish(step, V):
                        step(V.tensor_tensor(acc[:], acc[:], z[:], ALU.add))
                        step(V.tensor_tensor(as_tiles(acc, D), as_tiles(acc, D), inv2[:].unsqueeze(2).broadcast_to([P, T, D]), ALU.mult))
                    vector_steps(nc, "self2", finish)
                turn_tiles(nc, c, "turn2b", acc, D, yf)
                column_add(nc, "b2", yf, I["L2_gnn_b"])
                vector_steps(nc, "zero2", lambda step, V: step(V.memset(acc[:], 0.0)))
                project(nc, c, "head2", from_features(yf, I["L2_gnn_W1"]), D, "relu_add", acc, bias=I["L2_gnn_b1"])
                turn_tiles(nc, c, "turn2c", acc, D, yf)
                project(nc, c, "head2b", from_features(yf, I["L2_gnn_W2"]), D, "add", x, bias=I["L2_gnn_b2"])
            probe(5)

            with Stage(nc, "l2f") as s:
                yf = s.sb("yf", [128, DC * N])
                y = s.sb("y", [P, T * D])
                acc = s.sb("acc", [P, T * D])
                scores, picked, gate = s.sb("scores", [P, 8]), s.sb("picked", [1, 2], I32), s.sb("gate", [P, T * 2])
                layernorm(nc, "ln2f", x, y)
                turn_tiles(nc, c, "turn2f", y, D, yf)
                global_scores(nc, c, "route2", yf, I["L2_ffn_Wr"], I["L2_ffn_br"], 8, capacity, scores)
                with Stage(nc, "l2p") as s2:
                    one, two, pw1, pw2 = s2.sb("one", [P, 8]), s2.sb("two", [P, 8]), s2.sb("pw1", [P, 1]), s2.sb("pw2", [P, 1])
                    tmp, num = s2.sb("tmp", [P, 8]), s2.sb("num", [P, 2])
                    top_two(nc, c, "gate2", scores, 1, 8, one, two, pw1, pw2)

                    def picks(step, V):
                        g3 = gate[:].rearrange("p (t e) -> p t e", e=2)
                        for k, (pick, w) in enumerate(((one, pw1), (two, pw2))):
                            step(V.tensor_tensor(tmp[:], pick[:], c["iota"][0:P, 0:8], ALU.mult))
                            step(V.tensor_reduce(num[:, k:k + 1], tmp[:], AX.X, ALU.add))
                            step(V.tensor_copy(g3[:, :, k], w[:].broadcast_to([P, T])))
                        step(V.tensor_copy(picked[:], num[0:1, :]))
                    vector_steps(nc, "picks2", picks)
                network(nc, c, "net2", yf, 2, 512, ACT.Gelu, I["L2_ffn_W1"], I["L2_ffn_b1"], I["L2_ffn_W2"], I["L2_ffn_b2"], gate, acc,
                        picked)
                vector_steps(nc, "res2", lambda step, V: step(V.tensor_tensor(y[:], y[:], acc[:], ALU.add)))
                layernorm(nc, "ln2b", y, y, I["L2_ffn_gamma"], I["L2_ffn_beta"])
                vector_steps(nc, "res2b", lambda step, V: step(V.tensor_tensor(x[:], x[:], y[:], ALU.add)))
            probe(6)

            z1_d, z2_d = dram("z1", [N, 128]), dram("z2t", [N, 64])
            with Stage(nc, "l3g") as s:
                yf = s.sb("yf", [128, DC * N])
                x1f, x2f = s.sb("x1f", [128, N]), s.sb("x2f", [64, N])
                with Stage(nc, "l3y") as s2:
                    y = s2.sb("y", [P, T * D])
                    layernorm(nc, "ln3", x, y)
                    turn_tiles(nc, c, "turn3", y, D, yf)
                for k, (wide, srcs, table, xf) in enumerate((
                        (128, from_features(yf, I["L3_gnn_W1"]), z1_d, x1f),
                        (64, [(x1f, 128, 0, I["L3_gnn_W2"])], z2_d, x2f))):
                    with Stage(nc, "l3z") as s2:
                        z, acc = s2.sb("z", [P, T * wide]), s2.sb("acc", [P, T * wide])
                        project(nc, c, "z3", srcs, wide, "scale", z, scale=inv3, table=table)
                        segment_sum(nc, c, "sum3", table, wide, rec_d, blk_d, CH0, acc, False)

                        def finish(step, V):
                            step(V.tensor_tensor(acc[:], acc[:], z[:], ALU.add))
                            step(V.tensor_tensor(as_tiles(acc, wide), as_tiles(acc, wide),
                                                 inv3[:].unsqueeze(2).broadcast_to([P, T, wide]), ALU.mult))
                        vector_steps(nc, "self3", finish)
                        turn_tiles(nc, c, "turn3b", acc, wide, xf)
                    batch_norm_relu(nc, "bn3", xf, wide, I[f"L3_gnn_b{k + 1}"], I[f"L3_gnn_g{k + 1}"], I[f"L3_gnn_be{k + 1}"])
                wfc = I["L3_gnn_Wfc"]
                project(nc, c, "out3", [(yf, 128, 0, wfc[0:128, :]), (yf, 128, 1, wfc[128:256, :]),
                                        (x1f, 128, 0, wfc[256:384, :]), (x2f, 64, 0, wfc[384:448, :])],
                        D, "relu_add", x, bias=I["L3_gnn_bfc"])
            probe(7)

        with Stage(nc, "l3f") as s:
            one, two = s.sb("one", [P, T * ge]), s.sb("two", [P, T * ge])
            pw1, pw2 = s.sb("pw1", [P, T]), s.sb("pw2", [P, T])
            with Stage(nc, "gat") as s2:
                yf = s2.sb("yf", [128, DC * N])
                with Stage(nc, "l3fy") as s3:
                    y = s3.sb("y", [P, T * D])
                    layernorm(nc, "ln3f", x, y)
                    turn_tiles(nc, c, "turn3f", y, D, yf, table=y_d)
                attention_gate(nc, c, I, s2, dram, yf, by_dst3, gh, ge, one, two, pw1, pw2)
            two_of(nc, c, "l3n", s, dram, slot_table, y_d, one, two, pw1, pw2, ge, 512, ACT.Gelu,
                   I["L3_ffn_W1"], I["L3_ffn_b1"], I["L3_ffn_W2"], I["L3_ffn_b2"], x)
        transfer(nc, "store_out", [(by_tile(out, D), as_tiles(x, D))])


def router(nc, c, name, x, y_d, w_d, b_d, experts, choose):
    with Stage(nc, name) as s:
        y, yf, logits = s.sb("y", [P, T * D]), s.sb("yf", [128, DC * N]), s.sb("logits", [P, T * experts])
        layernorm(nc, "ln", x, y)
        turn_tiles(nc, c, "turn", y, D, yf, table=y_d)
        project(nc, c, "route", from_chunks(yf, w_d), experts, "copy", logits, bias=b_d)
        choose(logits)


def two_of(nc, c, name, s, dram, slot_table, y_d, one, two, pw1, pw2, experts, hidden, act_fn, w1_d, b1_d, w2_d, b2_d, x):
    tiles = 2
    groups = (2 * N + experts * (tiles * ST - 1)) // (tiles * ST)
    groups += groups % 2
    slots, which = s.sb("slots", [ST, groups * tiles], I32), s.sb("which", [1, groups], I32)
    pos = [s.sb(f"pos{k}", [P, T], I32) for k in range(2)]
    dispatch(nc, c, name + "d", [one, two], experts, tiles, groups, None, slot_table(name + "slots", groups * tiles), slots,
             which, pos, None)
    out_d = dram(name + "out", [groups * tiles * ST, D])
    routed(nc, c, name, y_d, slots, which, hidden, act_fn, w1_d, b1_d, w2_d, b2_d, tiles, groups, out_d)
    combine(nc, name + "c", out_d, pos, [pw1, pw2], x)


def column_add(nc, name, xf, bias_d):
    with Stage(nc, name) as s:
        col = s.sb("col", [128, DC])
        loaded, steps = s.sem("loaded"), s.sem("steps")
        with s.block() as block:
            @block.sync
            def _(sp):
                sp.dma_start(col[:], bias_d).then_inc(loaded, 16)

            @block.vector
            def _(dve):
                step = Steps(dve, steps)
                dve.wait_ge(loaded, 16)
                for k in range(DC):
                    v = xf[:, k * N:(k + 1) * N]
                    step(nc.vector.tensor_scalar(v, v, col[:, k:k + 1], None, ALU.add))


def attention_gate(nc, c, I, s, dram, yf, edges, gh, ge, one, two, pw1, pw2):
    w = gh * ge
    rec, blk, chunks = edges.rec, edges.blk, edges.chunks
    row = w + gh
    hs = s.sb("hs", [P, T * row])
    best = s.sb("best", [P, T * gh])
    node = s.sb("node", [P, T * 2 * gh])
    att = s.sb("att", [P, 3 * w])
    tmp = s.sb("tmp", [P, T * w])
    e_self, p_self = s.sb("e_self", [P, T * gh]), s.sb("p_self", [P, T * gh])
    acc = s.sb("acc", [P, T * row])
    stored = s.sb("stored", [EC, chunks * row])
    table = dram("gat", [N, row])
    h3, n3, a3 = as_tiles(hs, row), as_tiles(node, 2 * gh), as_tiles(acc, row)

    def heads_of(v):
        return v.rearrange("p t (h e) -> p t h e", h=gh)

    project(nc, c, "h_gat", from_chunks(yf, I["L3_ffn_W_gat"]), w, "copy", hs, stride=row)
    transfer(nc, "att", [(att[:, 0:w], I["L3_ffn_att_src"].partition_broadcast(P)),
                         (att[:, w:2 * w], I["L3_ffn_att_dst"].partition_broadcast(P)),
                         (att[:, 2 * w:3 * w], I["L3_ffn_b_gat"].partition_broadcast(P))])

    def parts(step, V):
        t3 = as_tiles(tmp, w)
        for k, dst in ((0, h3[:, :, w:row]), (1, n3[:, :, 0:gh])):
            step(V.tensor_tensor(t3, h3[:, :, 0:w], att[:, k * w:(k + 1) * w].unsqueeze(1).broadcast_to([P, T, w]), ALU.mult))
            step(V.tensor_reduce(dst, heads_of(t3), AX.X, ALU.add))
        step(V.tensor_copy(as_tiles(best, gh), h3[:, :, w:row]))
    vector_steps(nc, "parts", parts)
    transfer(nc, "store_gat", [(by_tile(table, row), h3)])
    segment_max(nc, c, "max3", None, row, gh, rec, blk, chunks, best, table, stored)

    def maxima(step, V):
        b3, e3 = as_tiles(best, gh), as_tiles(e_self, gh)
        step(V.tensor_tensor(b3, b3, n3[:, :, 0:gh], ALU.add))
        step(V.scalar_tensor_tensor(n3[:, :, gh:2 * gh], b3, 0.2, b3, ALU.mult, ALU.max))
        step(V.tensor_tensor(e3, h3[:, :, w:row], n3[:, :, 0:gh], ALU.add))
        step(V.scalar_tensor_tensor(as_tiles(p_self, gh), e3, 0.2, e3, ALU.mult, ALU.max))
        step(V.tensor_tensor(e3, as_tiles(p_self, gh), n3[:, :, gh:2 * gh], ALU.subtract))
    vector_steps(nc, "maxima", maxima)
    exponential(nc, "exp_self", e_self, p_self)
    softmax_sum(nc, c, "att3", gh, ge, rec, blk, chunks, acc, node, 2 * gh, None, None, stored, True)

    def scores(step, V):
        p3, t3 = as_tiles(p_self, gh), as_tiles(tmp, w)
        step(V.tensor_tensor(a3[:, :, w:row], a3[:, :, w:row], p3, ALU.add))
        step(V.tensor_scalar(as_tiles(e_self, gh), a3[:, :, w:row], 1e-16, None, ALU.add))
        step(V.reciprocal(e_self[:], e_self[:]))
        for h in range(gh):
            k = slice(h * ge, (h + 1) * ge)
            step(V.tensor_tensor(t3[:, :, k], h3[:, :, k], p3[:, :, h:h + 1].broadcast_to([P, T, ge]), ALU.mult))
            step(V.tensor_tensor(t3[:, :, k], t3[:, :, k], a3[:, :, k], ALU.add))
            step(V.tensor_tensor(t3[:, :, k], t3[:, :, k], as_tiles(e_self, gh)[:, :, h:h + 1].broadcast_to([P, T, ge]), ALU.mult))
        step(V.tensor_tensor(t3, t3, att[:, 2 * w:3 * w].unsqueeze(1).broadcast_to([P, T, w]), ALU.add))
    vector_steps(nc, "scores3", scores)
    with Stage(nc, "ln_gat") as s2:
        mean, var, inv = s2.sb("mean", [P, T]), s2.sb("var", [P, T]), s2.sb("inv", [P, T])
        sq = s2.sb("sq", [P, T * w])
        gb = s2.sb("gb", [P, 2 * w])
        sc = s2.sb("sc", [P, T * ge])
        t3 = as_tiles(tmp, w)
        transfer(nc, "gb", [(gb[:, 0:w], I["L3_ffn_ln_gamma"].partition_broadcast(P)),
                            (gb[:, w:2 * w], I["L3_ffn_ln_beta"].partition_broadcast(P))])

        def variance(step, V):
            step(V.tensor_reduce(mean[:], t3, AX.X, ALU.add))
            step(V.tensor_scalar(mean[:], mean[:], 1.0 / w, None, ALU.mult))
            step(V.tensor_tensor(t3, t3, mean[:].unsqueeze(2).broadcast_to([P, T, w]), ALU.subtract))
            step(V.tensor_tensor(sq[:], tmp[:], tmp[:], ALU.mult))
            step(V.tensor_reduce(var[:], as_tiles(sq, w), AX.X, ALU.add))
            step(V.tensor_scalar(var[:], var[:], 1.0 / w, EPS, ALU.mult, ALU.add))
        vector_steps(nc, "variance", variance)
        root(nc, "root_gat", var, inv)

        def average(step, V):
            step(V.tensor_tensor(t3, t3, inv[:].unsqueeze(2).broadcast_to([P, T, w]), ALU.mult))
            step(V.tensor_tensor(t3, t3, gb[:, 0:w].unsqueeze(1).broadcast_to([P, T, w]), ALU.mult))
            step(V.tensor_tensor(t3, t3, gb[:, w:2 * w].unsqueeze(1).broadcast_to([P, T, w]), ALU.add))
            s3 = as_tiles(sc, ge)
            step(V.tensor_tensor(s3, t3[:, :, 0:ge], t3[:, :, ge:2 * ge], ALU.add))
            for h in range(2, gh):
                step(V.tensor_tensor(s3, s3, t3[:, :, h * ge:(h + 1) * ge], ALU.add))
            step(V.tensor_scalar(sc[:], sc[:], 1.0 / gh, None, ALU.mult))
        vector_steps(nc, "average", average)
        top_two(nc, c, "gate3", sc, T, ge, one, two, pw1, pw2)


def from_chunks(t, w):
    wide = w.shape[1] // DC
    return [(t, 128, k, w[:, k * wide:(k + 1) * wide]) for k in range(DC)]


def exponential(nc, name, src, dst):
    with Stage(nc, name) as s:
        done = s.sem("done")
        with s.block() as block:
            @block.scalar
            def _(act):
                nc.scalar.activation(dst[:], src[:], ACT.Exp).then_inc(done, 1)



def lay_out(inputs):
    import numpy as np
    a = {k: np.ascontiguousarray(v) for k, v in inputs.items()}
    o = {"x": a["x"]}

    def rows(w):
        w = w.reshape(-1, 128, w.shape[-1])
        return w.transpose(1, 0, 2).reshape(128, -1)

    def experts(w):
        return np.stack([rows(e) for e in w])

    def columns(b):
        return b.reshape(b.shape[0], -1, 128).transpose(0, 2, 1)

    o["src"], o["dst"] = a["src"].reshape(125, -1), a["dst"].reshape(125, -1)
    o["edge_weight"] = a["edge_weight"].reshape(125, -1)
    o["edge3_src"], o["edge3_dst"] = a["L3_ffn_edge_index"][0].reshape(128, -1), a["L3_ffn_edge_index"][1].reshape(128, -1)
    for k in ("L0_gnn_W_neigh", "L0_gnn_W_self"):
        o[k] = rows(a[k].T)
    o["L1_ffn_Wg"] = rows(a["L1_ffn_Wg"].T)
    for k in ("L0_ffn_gate_w", "L1_gnn_Wq", "L1_gnn_Wk", "L1_gnn_Wv", "L1_gnn_Wo_w", "L2_gnn_W", "L2_gnn_W1",
              "L2_gnn_W2", "L2_ffn_Wr", "L3_gnn_W1", "L3_ffn_W_gat"):
        o[k] = rows(a[k])
    for k in ("L3_gnn_W2", "L3_gnn_Wfc"):
        o[k] = a[k]
    for k in ("L0_gnn_b_self", "L0_ffn_gate_b", "L1_gnn_Wo_b", "L1_ffn_bg", "L2_gnn_b1", "L2_gnn_b2", "L3_gnn_bfc"):
        o[k] = a[k].reshape(1, -1)
    for k in ("L1_gnn_ln1_g", "L1_gnn_ln1_b", "L1_gnn_ln2_g", "L1_gnn_ln2_b", "L2_ffn_br", "L2_ffn_gamma", "L2_ffn_beta",
              "L3_ffn_att_src", "L3_ffn_att_dst", "L3_ffn_b_gat", "L3_ffn_ln_gamma", "L3_ffn_ln_beta"):
        o[k] = a[k].reshape(-1)
    o["L2_gnn_b"] = a["L2_gnn_b"].reshape(-1, 128).T
    for k in ("b1", "g1", "be1", "b2", "g2", "be2"):
        o[f"L3_gnn_{k}"] = a[f"L3_gnn_{k}"].reshape(-1, 1)
    for pre, w1, w2 in (("L0_ffn", "w1", "w2"), ("L2_ffn", "W1", "W2"), ("L3_ffn", "W1", "W2")):
        o[f"{pre}_{w1}"], o[f"{pre}_{w2}"] = experts(a[f"{pre}_{w1}"]), experts(a[f"{pre}_{w2}"])
    o["L1_ffn_W1"], o["L1_ffn_W2"] = experts(a["L1_ffn_W1"].transpose(0, 2, 1)), experts(a["L1_ffn_W2"].transpose(0, 2, 1))
    o["L1_gnn_ffn_w1"], o["L1_gnn_ffn_w2"] = experts(a["L1_gnn_ffn_w1"][None]), experts(a["L1_gnn_ffn_w2"][None])
    for pre in ("L0_ffn", "L1_ffn", "L2_ffn", "L3_ffn"):
        o[f"{pre}_b1"], o[f"{pre}_b2"] = columns(a[f"{pre}_b1"]), a[f"{pre}_b2"]
    o["L1_gnn_ffn_b1"], o["L1_gnn_ffn_b2"] = columns(a["L1_gnn_ffn_b1"][None]), a["L1_gnn_ffn_b2"][None]
    return {k: np.ascontiguousarray(v) for k, v in o.items()}


def kernel(**inputs):
    import concourse.bacc as _bacc
    from concourse.bass_utils import run_bass_kernel_spmd as _run

    nc = _bacc.Bacc("TRN2", target_bir_lowering=False, num_devices=1)
    arrays = {f"in_{k}": v for k, v in lay_out(inputs).items()}
    aps = {k[3:]: nc.dram_tensor(k, v.shape, mybir.dt.from_np(v.dtype), kind="ExternalInput").ap()
           for k, v in arrays.items()}
    out = nc.dram_tensor("out", (N, D), F32, kind="ExternalOutput").ap()
    model(nc, aps, out)
    r = _run(nc, [arrays], core_ids=[0])
    return r.results[0]["out"]
```
